# Optimizing a Trainium2 kernel written in Bass

```python
import numpy as np
import jax
import jax.numpy as jnp

def _softmax(x, axis=-1):
    return jax.nn.softmax(x, axis=axis)

def _gelu(x):
    return jax.nn.gelu(x, approximate=True)

def _silu(x):
    return jax.nn.silu(x)

def _sigmoid(x):
    return jax.nn.sigmoid(x)

def _layernorm(x, axis=-1, eps=1e-05):
    m = jnp.mean(x, axis=axis, keepdims=True)
    v = jnp.var(x, axis=axis, keepdims=True)
    return (x - m) / jnp.sqrt(v + eps)

def _scatter_add(tgt, idx, src, axis=0):
    return tgt.at[idx].add(src)

def _segment_sum(src, seg, n):
    return jax.ops.segment_sum(src, seg, n)
kernel_name = 'mk_early_fusion_embed_d1_tok_img1024_r4_f5883f'

def setup_inputs(seed: int=0):
    np.random.seed(seed)
    _w = jnp.asarray

    def _rec_inputs():
        import jax
        import jax.numpy as jnp
        _rk = jax.random.key(seed)
        x = 7.22013e-05 + 1.00017 * jax.random.normal(jax.random.fold_in(_rk, 1), (8, 64, 256, 4), jnp.float32)
        x_txt = jax.random.randint(jax.random.fold_in(_rk, 51), (8, 77), 0, 4097, jnp.int32)
        itok_BS_0_4096 = jax.random.randint(jax.random.fold_in(_rk, 71), (8, 77), 0, 4097, jnp.int32)
        fside_BS_delta_x1 = jax.random.uniform(jax.random.fold_in(_rk, 72), (8, 77), jnp.float32, 0.0, 0.999957)
        fside_BS_delta_x2 = jax.random.uniform(jax.random.fold_in(_rk, 73), (8, 77), jnp.float32, 0.0, 0.999931)
        fside_BS_delta_y1 = jax.random.uniform(jax.random.fold_in(_rk, 74), (8, 77), jnp.float32, 0.0, 0.999963)
        fside_BS_delta_y2 = jax.random.uniform(jax.random.fold_in(_rk, 75), (8, 77), jnp.float32, 0.0, 0.999984)
        return (x, x_txt, itok_BS_0_4096, fside_BS_delta_x1, fside_BS_delta_x2, fside_BS_delta_y1, fside_BS_delta_y2)
    x, x_txt, itok_BS_0_4096, fside_BS_delta_x1, fside_BS_delta_x2, fside_BS_delta_y1, fside_BS_delta_y2 = _rec_inputs()

    def _L0_tok_setup():
        import jax, jax.numpy as jnp
        import numpy as np
        B, F, L, H, D = (8, 64, 256, 4, 64)
        MODEL = H * F
        WIN = 128

        def _local_mask():
            m = np.ones((L, L), dtype=bool)
            m = np.tril(m, WIN - 1)
            m = np.triu(m, -(WIN - 1))
            return jnp.asarray(m)

        def _flatten(y):
            n = y.shape[0]
            return y.transpose(0, 2, 3, 1).reshape(n, L, -1)
        key = jax.random.key(seed)
        ks = jax.random.split(key, 12)
        s = lambda n: 1.0 / np.sqrt(n)
        xav = np.sqrt(6.0 / (L + L))
        return {'x': jax.random.normal(ks[0], (B, F, L, H), jnp.float32), 'Wq_w': jax.random.normal(ks[1], (D, F), jnp.float32) * s(F), 'Wq_b': jnp.zeros((D,), jnp.float32), 'Wk_w': jax.random.normal(ks[2], (D, F), jnp.float32) * s(F), 'Wk_b': jnp.zeros((D,), jnp.float32), 'Wv_w': jax.random.normal(ks[3], (D, F), jnp.float32) * s(F), 'Wv_b': jnp.zeros((D,), jnp.float32), 'w_bias': jax.random.uniform(ks[4], (L, L), jnp.float32, -xav, xav), 'out_w': jax.random.normal(ks[5], (H * D, MODEL), jnp.float32) * s(H * D), 'out_b': jnp.zeros((MODEL,), jnp.float32), 'ln_g': jnp.ones((MODEL,), jnp.float32), 'ln_b': jnp.zeros((MODEL,), jnp.float32), 'local_mask': _local_mask()}
    _L0_tok_all = _L0_tok_setup()
    _L0_tok_in = {k: v for k, v in _L0_tok_all.items() if k in ('Wq_w', 'Wq_b', 'Wk_w', 'Wk_b', 'Wv_w', 'Wv_b', 'w_bias', 'out_w', 'out_b', 'ln_g', 'ln_b', 'local_mask')}
    del _L0_tok_all

    def _L0_txt_setup():
        import jax, jax.numpy as jnp
        import numpy as np
        NUM_BINS = 64
        PAD_ID = NUM_BINS ** 2
        VOCAB = NUM_BINS ** 2 + 1
        D_MODEL = 256
        B, S = (32, 128)
        key = jax.random.key(seed)
        k = jax.random.split(key, 8)
        ri = lambda kk: jax.random.randint(kk, (B, S), 0, VOCAB)
        dx1 = jax.random.uniform(k[4], (B, S), dtype=jnp.float32)
        dy1 = jax.random.uniform(k[5], (B, S), dtype=jnp.float32)
        return {'quant_poly11': ri(k[0]), 'quant_poly21': ri(k[1]), 'quant_poly12': ri(k[2]), 'quant_poly22': ri(k[3]), 'delta_x1': dx1, 'delta_x2': 1.0 - dx1, 'delta_y1': dy1, 'delta_y2': 1.0 - dy1, 'loc_embeds': jax.random.normal(k[6], (VOCAB, D_MODEL), dtype=jnp.float32) * 0.02}
    _L0_txt_all = _L0_txt_setup()
    _L0_txt_in = {k: v for k, v in _L0_txt_all.items() if k in ('loc_embeds',)}
    del _L0_txt_all

    def _L0_attn_setup():
        import jax, jax.numpy as jnp
        import numpy as np
        DEPTH, DIM, H, DH, MKV, TOPK = (2, 256, 16, 64, 32, 64)
        INNER = H * DH
        FFD = 4 * DIM
        SCALE = DH ** (-0.5)
        EPS = 1e-05

        def layer_norm(x, g, b):
            mu = x.mean(-1, keepdims=True)
            var = ((x - mu) ** 2).mean(-1, keepdims=True)
            return (x - mu) * jax.lax.rsqrt(var + EPS) * g + b

        def attn_block(x, wq, wk, wv, mk, mv, pre, post, wo, bo):
            b, n, _ = x.shape
            q = (x @ wq).reshape(b, n, H, DH).transpose(0, 2, 1, 3)
            k = (x @ wk).reshape(b, n, H, DH).transpose(0, 2, 1, 3)
            v = (x @ wv).reshape(b, n, H, DH).transpose(0, 2, 1, 3)
            mk_b = jnp.broadcast_to(mk[None], (b, H, MKV, DH))
            mv_b = jnp.broadcast_to(mv[None], (b, H, MKV, DH))
            k = jnp.concatenate([mk_b, k], axis=2)
            v = jnp.concatenate([mv_b, v], axis=2)
            dots = jnp.einsum('bhid,bhjd->bhij', q, k) * SCALE
            dots = jnp.einsum('bhij,hk->bkij', dots, pre)
            neg = -jnp.finfo(dots.dtype).max
            j = n + MKV
            causal = jnp.arange(n)[:, None] + MKV < jnp.arange(j)[None, :]
            dots = jnp.where(causal[None, None], neg, dots)
            vk = jax.lax.top_k(dots, TOPK)[0][..., -1:]
            dots = jnp.where(dots < vk, neg, dots)
            attn = jax.nn.softmax(dots, axis=-1)
            attn = jnp.einsum('bhij,hk->bkij', attn, post)
            out = jnp.einsum('bhij,bhjd->bhid', attn, v)
            out = out.transpose(0, 2, 1, 3).reshape(b, n, INNER)
            return out @ wo + bo

        def ff_block(x, w1, b1, w2, b2):
            return jax.nn.gelu(x @ w1 + b1, approximate=False) @ w2 + b2
        key = jax.random.key(seed)
        ks = jax.random.split(key, 16)
        s = 0.02
        inp = {'x': jax.random.normal(ks[0], (4, 256, DIM), jnp.float32), 'ln1_g': jnp.ones((DEPTH, DIM), jnp.float32), 'ln1_b': jnp.zeros((DEPTH, DIM), jnp.float32), 'wq': jax.random.normal(ks[1], (DEPTH, DIM, INNER), jnp.float32) * s, 'wk': jax.random.normal(ks[2], (DEPTH, DIM, INNER), jnp.float32) * s, 'wv': jax.random.normal(ks[3], (DEPTH, DIM, INNER), jnp.float32) * s, 'mem_k': jax.random.normal(ks[4], (DEPTH, H, MKV, DH), jnp.float32), 'mem_v': jax.random.normal(ks[5], (DEPTH, H, MKV, DH), jnp.float32), 'pre_proj': jax.random.normal(ks[6], (DEPTH, H, H), jnp.float32), 'post_proj': jax.random.normal(ks[7], (DEPTH, H, H), jnp.float32), 'wo': jax.random.normal(ks[8], (DEPTH, INNER, DIM), jnp.float32) * s, 'bo': jnp.zeros((DEPTH, DIM), jnp.float32), 'ln2_g': jnp.ones((DEPTH, DIM), jnp.float32), 'ln2_b': jnp.zeros((DEPTH, DIM), jnp.float32), 'w1': jax.random.normal(ks[9], (DEPTH, DIM, FFD), jnp.float32) * s, 'b1': jnp.zeros((DEPTH, FFD), jnp.float32), 'w2': jax.random.normal(ks[10], (DEPTH, FFD, DIM), jnp.float32) * s, 'b2': jnp.zeros((DEPTH, DIM), jnp.float32)}
        return inp
    _L0_attn_all = _L0_attn_setup()
    _L0_attn_in = {k: v for k, v in _L0_attn_all.items() if k in ('ln1_g', 'ln1_b', 'wq', 'wk', 'wv', 'mem_k', 'mem_v', 'pre_proj', 'post_proj', 'wo', 'bo', 'ln2_g', 'ln2_b', 'w1', 'b1', 'w2', 'b2')}
    del _L0_attn_all

    def _L0_ffn_setup():
        import jax, jax.numpy as jnp
        import numpy as np
        H = 256
        I = 512
        E = 32
        B, S = (4, 512)

        def _grouped_mm(a, w, group_sizes):
            return jax.lax.ragged_dot(a, w, group_sizes)

        def _swiglu(x, gw, uw, dw):
            return jax.nn.silu(x @ gw) * (x @ uw) @ dw
        key = jax.random.key(seed)
        ks = jax.random.split(key, 8)
        scale = 0.02
        inp = {'hidden_states': jax.random.normal(ks[0], (B, S, H), dtype=jnp.float32), 'gate_w': jax.random.normal(ks[1], (H, E), dtype=jnp.float32) * scale, 'shared_gate_w': jax.random.normal(ks[2], (H, I), dtype=jnp.float32) * scale, 'shared_up_w': jax.random.normal(ks[3], (H, I), dtype=jnp.float32) * scale, 'shared_down_w': jax.random.normal(ks[4], (I, H), dtype=jnp.float32) * scale, 'routed_gate_w': jax.random.normal(ks[5], (E, H, I), dtype=jnp.float32) * scale, 'routed_up_w': jax.random.normal(ks[6], (E, H, I), dtype=jnp.float32) * scale, 'routed_down_w': jax.random.normal(ks[7], (E, I, H), dtype=jnp.float32) * scale}
        return inp
    _L0_ffn_all = _L0_ffn_setup()
    _L0_ffn_in = {k: v for k, v in _L0_ffn_all.items() if k in ('gate_w', 'shared_gate_w', 'shared_up_w', 'shared_down_w', 'routed_gate_w', 'routed_up_w', 'routed_down_w')}
    del _L0_ffn_all
    return {'x': x, 'x_txt': x_txt, 'itok_BS_0_4096': itok_BS_0_4096, 'fside_BS_delta_x1': fside_BS_delta_x1, 'fside_BS_delta_x2': fside_BS_delta_x2, 'fside_BS_delta_y1': fside_BS_delta_y1, 'fside_BS_delta_y2': fside_BS_delta_y2, 'L0_tok_Wq_w': _L0_tok_in['Wq_w'], 'L0_tok_Wq_b': _L0_tok_in['Wq_b'], 'L0_tok_Wk_w': _L0_tok_in['Wk_w'], 'L0_tok_Wk_b': _L0_tok_in['Wk_b'], 'L0_tok_Wv_w': _L0_tok_in['Wv_w'], 'L0_tok_Wv_b': _L0_tok_in['Wv_b'], 'L0_tok_w_bias': _L0_tok_in['w_bias'], 'L0_tok_out_w': _L0_tok_in['out_w'], 'L0_tok_out_b': _L0_tok_in['out_b'], 'L0_tok_ln_g': _L0_tok_in['ln_g'], 'L0_tok_ln_b': _L0_tok_in['ln_b'], 'L0_tok_local_mask': _L0_tok_in['local_mask'], 'L0_txt_loc_embeds': _L0_txt_in['loc_embeds'], 'L0_attn_ln1_g': _L0_attn_in['ln1_g'], 'L0_attn_ln1_b': _L0_attn_in['ln1_b'], 'L0_attn_wq': _L0_attn_in['wq'], 'L0_attn_wk': _L0_attn_in['wk'], 'L0_attn_wv': _L0_attn_in['wv'], 'L0_attn_mem_k': _L0_attn_in['mem_k'], 'L0_attn_mem_v': _L0_attn_in['mem_v'], 'L0_attn_pre_proj': _L0_attn_in['pre_proj'], 'L0_attn_post_proj': _L0_attn_in['post_proj'], 'L0_attn_wo': _L0_attn_in['wo'], 'L0_attn_bo': _L0_attn_in['bo'], 'L0_attn_ln2_g': _L0_attn_in['ln2_g'], 'L0_attn_ln2_b': _L0_attn_in['ln2_b'], 'L0_attn_w1': _L0_attn_in['w1'], 'L0_attn_b1': _L0_attn_in['b1'], 'L0_attn_w2': _L0_attn_in['w2'], 'L0_attn_b2': _L0_attn_in['b2'], 'L0_ffn_gate_w': _L0_ffn_in['gate_w'], 'L0_ffn_shared_gate_w': _L0_ffn_in['shared_gate_w'], 'L0_ffn_shared_up_w': _L0_ffn_in['shared_up_w'], 'L0_ffn_shared_down_w': _L0_ffn_in['shared_down_w'], 'L0_ffn_routed_gate_w': _L0_ffn_in['routed_gate_w'], 'L0_ffn_routed_up_w': _L0_ffn_in['routed_up_w'], 'L0_ffn_routed_down_w': _L0_ffn_in['routed_down_w']}

def reference(x, x_txt, itok_BS_0_4096, fside_BS_delta_x1, fside_BS_delta_x2, fside_BS_delta_y1, fside_BS_delta_y2, L0_tok_Wq_w, L0_tok_Wq_b, L0_tok_Wk_w, L0_tok_Wk_b, L0_tok_Wv_w, L0_tok_Wv_b, L0_tok_w_bias, L0_tok_out_w, L0_tok_out_b, L0_tok_ln_g, L0_tok_ln_b, L0_tok_local_mask, L0_txt_loc_embeds, L0_attn_ln1_g, L0_attn_ln1_b, L0_attn_wq, L0_attn_wk, L0_attn_wv, L0_attn_mem_k, L0_attn_mem_v, L0_attn_pre_proj, L0_attn_post_proj, L0_attn_wo, L0_attn_bo, L0_attn_ln2_g, L0_attn_ln2_b, L0_attn_w1, L0_attn_b1, L0_attn_w2, L0_attn_b2, L0_ffn_gate_w, L0_ffn_shared_gate_w, L0_ffn_shared_up_w, L0_ffn_shared_down_w, L0_ffn_routed_gate_w, L0_ffn_routed_up_w, L0_ffn_routed_down_w):
    import jax
    import jax.numpy as jnp

    def _L0_tok_ref(x, Wq_w, Wq_b, Wk_w, Wk_b, Wv_w, Wv_b, w_bias, out_w, out_b, ln_g, ln_b, local_mask):
        import jax, jax.numpy as jnp
        import numpy as np
        B, F, L, H, D = (8, 64, 256, 4, 64)
        MODEL = H * F
        WIN = 128

        def _local_mask():
            m = np.ones((L, L), dtype=bool)
            m = np.tril(m, WIN - 1)
            m = np.triu(m, -(WIN - 1))
            return jnp.asarray(m)

        def _flatten(y):
            n = y.shape[0]
            return y.transpose(0, 2, 3, 1).reshape(n, L, -1)

        def proj(w, b):
            y = jnp.einsum('nclh,dc->ndlh', x, w) + b[None, :, None, None]
            return _flatten(y)
        q = proj(Wq_w, Wq_b)
        k = proj(Wk_w, Wk_b)
        v = proj(Wv_w, Wv_b)
        wb = w_bias * local_mask.astype(w_bias.dtype)
        ew = jnp.exp(wb)
        ek = jnp.exp(k)
        num = jnp.einsum('ts,nsd->ntd', ew, ek * v)
        den = jnp.einsum('ts,nsd->ntd', ew, ek)
        y = jax.nn.sigmoid(q) * num / den
        h = y @ out_w + out_b + _flatten(x)
        mu = jnp.mean(h, axis=-1, keepdims=True)
        var = jnp.mean(jnp.square(h - mu), axis=-1, keepdims=True)
        return (h - mu) * jax.lax.rsqrt(var + 1e-05) * ln_g + ln_b

    def _L0_txt_ref(quant_poly11, quant_poly21, quant_poly12, quant_poly22, delta_x1, delta_x2, delta_y1, delta_y2, loc_embeds):
        import jax, jax.numpy as jnp
        import numpy as np
        NUM_BINS = 64
        PAD_ID = NUM_BINS ** 2
        VOCAB = NUM_BINS ** 2 + 1
        D_MODEL = 256
        B, S = (32, 128)
        fix = lambda q: jnp.where(q == -1, PAD_ID, q)
        e11 = loc_embeds[fix(quant_poly11)]
        e21 = loc_embeds[fix(quant_poly21)]
        e12 = loc_embeds[fix(quant_poly12)]
        e22 = loc_embeds[fix(quant_poly22)]
        w11 = (delta_x2 * delta_y2)[..., None]
        w12 = (delta_x2 * delta_y1)[..., None]
        w21 = (delta_x1 * delta_y2)[..., None]
        w22 = (delta_x1 * delta_y1)[..., None]
        return e11 * w11 + e12 * w12 + e21 * w21 + e22 * w22

    def _L0_attn_ref(x, ln1_g, ln1_b, wq, wk, wv, mem_k, mem_v, pre_proj, post_proj, wo, bo, ln2_g, ln2_b, w1, b1, w2, b2):
        import jax, jax.numpy as jnp
        import numpy as np
        DEPTH, DIM, H, DH, MKV, TOPK = (2, 256, 16, 64, 32, 64)
        INNER = H * DH
        FFD = 4 * DIM
        SCALE = DH ** (-0.5)
        EPS = 1e-05

        def layer_norm(x, g, b):
            mu = x.mean(-1, keepdims=True)
            var = ((x - mu) ** 2).mean(-1, keepdims=True)
            return (x - mu) * jax.lax.rsqrt(var + EPS) * g + b

        def attn_block(x, wq, wk, wv, mk, mv, pre, post, wo, bo):
            b, n, _ = x.shape
            q = (x @ wq).reshape(b, n, H, DH).transpose(0, 2, 1, 3)
            k = (x @ wk).reshape(b, n, H, DH).transpose(0, 2, 1, 3)
            v = (x @ wv).reshape(b, n, H, DH).transpose(0, 2, 1, 3)
            mk_b = jnp.broadcast_to(mk[None], (b, H, MKV, DH))
            mv_b = jnp.broadcast_to(mv[None], (b, H, MKV, DH))
            k = jnp.concatenate([mk_b, k], axis=2)
            v = jnp.concatenate([mv_b, v], axis=2)
            dots = jnp.einsum('bhid,bhjd->bhij', q, k) * SCALE
            dots = jnp.einsum('bhij,hk->bkij', dots, pre)
            neg = -jnp.finfo(dots.dtype).max
            j = n + MKV
            causal = jnp.arange(n)[:, None] + MKV < jnp.arange(j)[None, :]
            dots = jnp.where(causal[None, None], neg, dots)
            vk = jax.lax.top_k(dots, TOPK)[0][..., -1:]
            dots = jnp.where(dots < vk, neg, dots)
            attn = jax.nn.softmax(dots, axis=-1)
            attn = jnp.einsum('bhij,hk->bkij', attn, post)
            out = jnp.einsum('bhij,bhjd->bhid', attn, v)
            out = out.transpose(0, 2, 1, 3).reshape(b, n, INNER)
            return out @ wo + bo

        def ff_block(x, w1, b1, w2, b2):
            return jax.nn.gelu(x @ w1 + b1, approximate=False) @ w2 + b2
        for l in range(DEPTH):
            a = attn_block(layer_norm(x, ln1_g[l], ln1_b[l]), wq[l], wk[l], wv[l], mem_k[l], mem_v[l], pre_proj[l], post_proj[l], wo[l], bo[l])
            x = a + x
            f = ff_block(layer_norm(x, ln2_g[l], ln2_b[l]), w1[l], b1[l], w2[l], b2[l])
            x = f + x
        return x

    def _L0_ffn_ref(hidden_states, gate_w, shared_gate_w, shared_up_w, shared_down_w, routed_gate_w, routed_up_w, routed_down_w):
        import jax, jax.numpy as jnp
        import numpy as np
        H = 256
        I = 512
        E = 32
        B, S = (4, 512)

        def _grouped_mm(a, w, group_sizes):
            return jax.lax.ragged_dot(a, w, group_sizes)

        def _swiglu(x, gw, uw, dw):
            return jax.nn.silu(x @ gw) * (x @ uw) @ dw
        b, s, h = hidden_states.shape
        x = hidden_states.reshape(-1, h)
        shared_out = _swiglu(x, shared_gate_w, shared_up_w, shared_down_w)
        logits = x @ gate_w
        topk_ids = jnp.argmax(logits, axis=-1)
        topk_val = jnp.max(logits, axis=-1)
        scores = jax.nn.sigmoid(topk_val)[:, None]
        xs = x * scores
        tokens_per_expert = jnp.zeros((E,), jnp.int32).at[topk_ids].add(1)
        order = jnp.argsort(topk_ids)
        sorted_x = xs[order]
        g = _grouped_mm(sorted_x, routed_gate_w, tokens_per_expert)
        u = _grouped_mm(sorted_x, routed_up_w, tokens_per_expert)
        d = _grouped_mm(jax.nn.silu(g) * u, routed_down_w, tokens_per_expert)
        inv = jnp.argsort(order)
        routed_out = d[inv]
        return (shared_out + routed_out).reshape(b, s, h)
    h = _L0_tok_ref(x, L0_tok_Wq_w, L0_tok_Wq_b, L0_tok_Wk_w, L0_tok_Wk_b, L0_tok_Wv_w, L0_tok_Wv_b, L0_tok_w_bias, L0_tok_out_w, L0_tok_out_b, L0_tok_ln_g, L0_tok_ln_b, L0_tok_local_mask)
    h = jnp.concatenate([h, _L0_txt_ref(x_txt, itok_BS_0_4096, itok_BS_0_4096, itok_BS_0_4096, fside_BS_delta_x1, fside_BS_delta_x2, fside_BS_delta_y1, fside_BS_delta_y2, L0_txt_loc_embeds)], axis=1)
    h = h + _L0_attn_ref(_layernorm(h, axis=-1), L0_attn_ln1_g, L0_attn_ln1_b, L0_attn_wq, L0_attn_wk, L0_attn_wv, L0_attn_mem_k, L0_attn_mem_v, L0_attn_pre_proj, L0_attn_post_proj, L0_attn_wo, L0_attn_bo, L0_attn_ln2_g, L0_attn_ln2_b, L0_attn_w1, L0_attn_b1, L0_attn_w2, L0_attn_b2)
    h = h + _L0_ffn_ref(_layernorm(h, axis=-1), L0_ffn_gate_w, L0_ffn_shared_gate_w, L0_ffn_shared_up_w, L0_ffn_shared_down_w, L0_ffn_routed_gate_w, L0_ffn_routed_up_w, L0_ffn_routed_down_w)
    return h

_drawn_inputs = setup_inputs


def setup_inputs(seed=0):
    import zlib

    import numpy as np

    out = dict(_drawn_inputs(seed))
    spreads = {'L0_tok_Wq_b': (0.0, 0.8),
     'L0_tok_Wk_b': (0.0, 0.8),
     'L0_tok_Wv_b': (0.0, 0.1),
     'L0_tok_out_b': (0.0, 0.1),
     'L0_tok_ln_g': (1.0, 0.2),
     'L0_tok_ln_b': (0.0, 0.1),
     'L0_attn_ln1_g': (1.0, 0.2),
     'L0_attn_ln1_b': (0.0, 0.1),
     'L0_attn_bo': (0.0, 0.1),
     'L0_attn_ln2_g': (1.0, 0.6),
     'L0_attn_ln2_b': (0.0, 0.797),
     'L0_attn_b1': (0.0, 0.281),
     'L0_attn_b2': (0.0, 0.1)}
    factors = {'L0_tok_w_bias': 8.0,
     'L0_ffn_gate_w': 8.0,
     'L0_ffn_shared_gate_w': 4.898,
     'L0_ffn_shared_up_w': 4.84,
     'L0_ffn_shared_down_w': 4.815,
     'L0_ffn_routed_gate_w': 8.0,
     'L0_ffn_routed_up_w': 8.0,
     'L0_ffn_routed_down_w': 8.0}
    for name, (base, spread) in spreads.items():
        noise = np.random.default_rng([zlib.crc32(name.encode()), seed]).standard_normal(out[name].shape)
        drawn = base * np.exp(spread * noise) if base else spread * noise
        out[name] = jnp.asarray(drawn.astype(out[name].dtype))
    for name, factor in factors.items():
        out[name] = (out[name] * factor).astype(out[name].dtype)
    return out
```

```python
from contextlib import ExitStack

import numpy as np
import concourse.bass as bass
from concourse import mybir

F32 = mybir.dt.float32
I32 = mybir.dt.int32
U32 = mybir.dt.uint32
U8 = mybir.dt.uint8
ALU = mybir.AluOpType
ACT = mybir.ActivationFunctionType
AX = mybir.AxisListType

B, F, L, HD, D = 8, 64, 256, 4, 256
S_TXT = 77
SEQ = L + S_TXT
H, DH, MEM = 16, 64, 32
KEYS = SEQ + MEM
TILE0 = (0, 96, 224)
TILE_N = (96, 128, 109)
ROWS = 8
BLOCKS = -(-SEQ // ROWS)
GROUP0 = (0, 12, 28, BLOCKS)
FULL_ROWS = MEM // ROWS
EXPERTS, HID = 32, 512
SLOT_TILES = EXPERTS + (B * SEQ - EXPERTS) // 128
BIG = 3.4028234663852886e38
EPS = 1e-5


def all_rows(vector, rows):
    return bass.AP(vector.tensor, vector.offset, [[0, rows], [1, vector.shape[-1]]])


def block_width(n):
    return min(MEM + ROWS * (n + 1), KEYS)


def tile_of(n):
    return sum(n >= g for g in GROUP0[1:3])


def layer_norm_stats(dve, stats, moments, source):
    dve.bn_stats(stats, source)
    dve.drain()
    return dve.bn_aggr(moments, stats)


def tokens_stage(nc, a, c, state_h, state_x):
    with ExitStack() as ctx:
        sb = lambda n, s, d=F32: ctx.enter_context(nc.sbuf_tensor(n, s, d))
        ps = lambda n, s, d=F32: ctx.enter_context(nc.psum_tensor(n, s, d))
        sem = lambda n: ctx.enter_context(nc.semaphore(n))
        xa = sb("xa", [65, L * HD])
        w_q = sb("w_q", [65, 64])
        w_kv = sb("w_kv", [65, 128])
        id_b = sb("id_b", [65, HD, 64])
        ew = sb("ew", [128, 2, L])
        mask8 = sb("mask8", [128, 2, L // 4], I32)
        maskf = sb("maskf", [128, 2, L])
        w_out = sb("w_out", [128, 2, D])
        gain = sb("gain", [128, D])
        shift = sb("shift", [128, D])
        ekv = sb("ekv", [128, 2, 2, D])
        e_q = sb("e_q", [128, 2, L])
        dq = sb("dq", [128, 2, L])
        rq = sb("rq", [128, 2, L])
        y_t = sb("y_t", [128, 2, L])
        stats = sb("stats", [128, 6])
        mom = sb("mom", [128, 2])
        rstd = sb("rstd", [128, 1])
        half = sb("half", [128, 1])
        xn = sb("xn", [128, D])
        xg = sb("xg", [128, D])
        ids = sb("ids", [S_TXT, B, 2], I32)
        idf = sb("idf", [S_TXT, B, 2])
        pad = sb("pad", [S_TXT, B, 2])
        idx = sb("idx", [S_TXT, B, 2], U32)
        fr = sb("fr", [S_TXT, 4, B])
        w4 = sb("w4", [S_TXT, 4, B])
        emb = sb("emb", [S_TXT, 2, D])
        mixed = sb("mixed", [S_TXT, D])
        p_kv = ps("p_kv", [128, 2, HD, 2, 64])
        p_q = ps("p_q", [128, 2, L])
        p_num = ps("p_num", [128, 2, L])
        p_den = ps("p_den", [128, 2, L])
        p_h = ps("p_h", [128, 3, 512])
        loaded = sem("t_loaded")
        x_in = sem("t_x_in")
        ready = sem("t_ready")
        kv_full = sem("t_kv_full")
        q_full = sem("t_q_full")
        ek_done = sem("t_ek_done")
        eq_done = sem("t_eq_done")
        ekv_done = sem("t_ekv_done")
        nd_full = sem("t_nd_full")
        y_done = sem("t_y_done")
        h_full = sem("t_h_full")
        mom_done = sem("t_mom_done")
        rstd_done = sem("t_rstd_done")
        gathered = sem("t_gathered")
        text_done = sem("t_text_done")
        text_moved = sem("t_text_moved")
        b_done = sem("t_b_done")
        idx_done = sem("t_idx_done")
        chain = sem("t_chain")
        NLOAD = 12
        xv = xa[:, :].rearrange("c (l h) -> c h l", h=HD)
        with nc.Block() as block:
            @block.sync
            def _(sp):
                loads = [(w_q[:, :], a["Wq"]), (w_kv[:, :], a["Wkv"]), (id_b[:, :, :], a["id_b"]),
                         (ew[:, :, :], a["w_bias_t"].rearrange("(s p) t -> p s t", p=128)),
                         (mask8[:, :, :], a["mask_t"].rearrange("(s p) t -> p s t", p=128)),
                         (w_out[:, :, :], a["out_w"].rearrange("(c p) n -> p c n", p=128)),
                         (gain[:, :], all_rows(a["ln_g"], 128)),
                         (shift[:, :], all_rows(a["ln_b"], 128)),
                         (ids[:, :, :], a["ids"]), (fr[:, :, :], a["fractions"]),
                         (c["ident"][:, :], a["ident"]), (xa[64:65, :], a["ones"])]
                assert len(loads) == NLOAD
                for dst, src in loads:
                    sp.dma_start(dst, src).then_inc(loaded, 16)
                with sp.Fori(0, B) as b:
                    sp.wait_ge(b_done, b + 1)
                    sp.dma_start(xa[0:64, :], a["x"][b].rearrange("c l h -> c (l h)")).then_inc(x_in, 16)
                    sp.wait_ge(text_done, b + 1)
                    sp.dma_start(state_h[32:32 + S_TXT, b, 2, :], mixed[:, :]).then_inc(text_moved, 16)
                sp.wait_ge(text_moved, 16 * B)

            @block.gpsimd
            def _(pool):
                pool.memset(half[:, :], -0.5)
                pool.drain()
                pool.wait_ge(idx_done, 1)
                for b in range(B):
                    if b:
                        pool.wait_ge(text_done, b)
                    for j in range(2):
                        pool.indirect_dma_start(emb[:, j, :], None, a["embeds"],
                                                bass.IndirectOffsetOnAxis(ap=idx[:, b, j:j + 1], axis=0)).then_inc(gathered, 16)
                    for k, n in enumerate((96, 96, 128, 128, 32)):
                        pool.wait_ge(mom_done, 5 * b + k + 1)
                        pool.tensor_scalar(rstd[0:n, :], mom[0:n, 1:2], EPS, None, ALU.add)
                        pool.drain()
                        pool.tensor_tensor(rstd[0:n, :], rstd[0:n, :], half[0:n, :], ALU.pow).then_inc(rstd_done, 1)

            @block.tensor
            def _(pe):
                pe.wait_ge(loaded, 16 * NLOAD)
                pe.wait_ge(ready, 1)
                with pe.Fori(0, B) as b:
                    pe.wait_ge(x_in, 16 * b + 16)
                    for s in range(2):
                        for h in range(HD):
                            last = pe.matmul(p_kv[:, s, h, :, :], xv[:, h, s * 128:s * 128 + 128], w_kv[:, :], start=(h == 0), stop=True,
                                             skip_group_check=True)
                    last.then_inc(kv_full, 1)
                    for h in range(HD):
                        last = pe.matmul(p_q[64 * (h % 2):64 * (h % 2) + 64, h // 2, :], w_q[:, :], xv[:, h, :],
                                         start=(h // 2 == 0), stop=True, skip_group_check=True)
                    last.then_inc(q_full, 1)
                    pe.wait_ge(ekv_done, b + 1)
                    for out, j in ((p_num, 0), (p_den, 1)):
                        for m in range(2):
                            for s in range(2):
                                last = pe.matmul(out[:, m, :], ekv[:, s, j, m * 128:m * 128 + 128], ew[:, s, :],
                                                 start=(m == 0 and s == 0), stop=(s == 1), skip_group_check=True)
                    last.then_inc(nd_full, 1)
                    pe.wait_ge(y_done, b + 1)
                    for g, (t0, n) in enumerate(((0, 96), (96, 128), (224, 32))):
                        for m in range(2):
                            pe.matmul(p_h[0:n, g, 0:D], y_t[:, m, t0:t0 + n], w_out[:, m, :], start=(m == 0), stop=False,
                                      skip_group_check=True)
                        for h in range(HD):
                            last = pe.matmul(p_h[0:n, g, 64 * h:64 * h + 64], xv[:, h, t0:t0 + n], id_b[:, h, :],
                                             start=False, stop=True, skip_group_check=True)
                        last.then_inc(h_full, 1)

            @block.scalar
            def _(act):
                act.wait_ge(chain, 3)
                act.activation(ew[:, :, :], ew[:, :, :], ACT.Exp).then_inc(ready, 1)
                with act.Fori(0, B) as b:
                    act.wait_ge(kv_full, b + 1)
                    act.activation(ekv[:, :, 1, :].rearrange("p s (h d) -> p s h d", h=HD), p_kv[:, :, :, 0, :], ACT.Exp).then_inc(ek_done, 1)
                    act.wait_ge(q_full, b + 1)
                    act.activation(e_q[:, :, :], p_q[:, :, :], ACT.Exp, scale=-1.0).then_inc(eq_done, 1)

            @block.vector
            def _(dve):
                dve.wait_ge(loaded, 16 * NLOAD)
                dve.tensor_copy(maskf[:, :, :], mask8[:, :, :].bitcast(U8))
                dve.tensor_copy(idf[:, :, :], ids[:, :, :]).then_inc(chain, 2)
                dve.drain()
                dve.tensor_tensor(ew[:, :, :], ew[:, :, :], maskf[:, :, :], ALU.mult).then_inc(chain, 1)
                dve.tensor_scalar(pad[:, :, :], idf[:, :, :], -1.0, 4097.0, ALU.is_equal, ALU.mult)
                dve.drain()
                dve.tensor_tensor(idx[:, :, :], idf[:, :, :], pad[:, :, :], ALU.add).then_inc(idx_done, 1)
                for k, (u, v) in enumerate(((1, 3), (1, 2), (0, 3), (0, 2))):
                    dve.tensor_tensor(w4[:, k, :], fr[:, u, :], fr[:, v, :], ALU.mult)
                dve.wait_ge(ready, 1)
                dve.drain().then_inc(b_done, 1)
                with dve.Fori(0, B) as b:
                    dve.wait_ge(ek_done, b + 1)
                    for s in range(2):
                        last = dve.tensor_tensor(ekv[:, s, 0, :].rearrange("p (h d) -> p h d", h=HD), p_kv[:, s, :, 1, :],
                                                 ekv[:, s, 1, :].rearrange("p (h d) -> p h d", h=HD), ALU.mult)
                    last.then_inc(ekv_done, 1)
                    dve.wait_ge(nd_full, b + 1)
                    dve.wait_ge(eq_done, b + 1)
                    dve.scalar_tensor_tensor(dq[:, :, :], e_q[:, :, :], 1.0, p_den[:, :, :], ALU.add, ALU.mult)
                    dve.drain()
                    dve.reciprocal(rq[:, :, :], dq[:, :, :])
                    dve.drain()
                    dve.tensor_tensor(y_t[:, :, :], p_num[:, :, :], rq[:, :, :], ALU.mult).then_inc(y_done, 1)
                    dve.wait_ge(gathered, 32 * b + 32)
                    dve.tensor_scalar(mixed[:, :], emb[:, 0, :], w4[:, 0, bass.ds(b, 1)], None, ALU.mult)
                    for k in range(1, 4):
                        dve.drain()
                        last = dve.scalar_tensor_tensor(mixed[:, :], emb[:, 1, :], w4[:, k, bass.ds(b, 1)], mixed[:, :], ALU.mult, ALU.add)
                    last.then_inc(text_done, 1)
                    k = 0
                    for g, n in enumerate((96, 128, 32)):
                        dve.drain()
                        dve.wait_ge(h_full, 3 * b + g + 1)
                        layer_norm_stats(dve, stats[0:n, :], mom[0:n, :], p_h[0:n, g, 0:D]).then_inc(mom_done, 1)
                        k += 1
                        dve.wait_ge(rstd_done, 5 * b + k)
                        dve.tensor_scalar(xn[0:n, :], p_h[0:n, g, 0:D], mom[0:n, 0:1], rstd[0:n, :], ALU.subtract, ALU.mult)
                        dve.drain()
                        dve.tensor_tensor(xg[0:n, :], xn[0:n, :], gain[0:n, :], ALU.mult)
                        dve.drain()
                        if g == 2:
                            dve.tensor_tensor(state_h[0:n, b, g, :], xg[0:n, :], shift[0:n, :], ALU.add)
                            dve.drain()
                            dve.wait_ge(text_moved, 16 * b + 16)
                            break
                        dve.tensor_tensor(state_h[0:n, b, g, :], xg[0:n, :], shift[0:n, :], ALU.add)
                        dve.drain()
                        layer_norm_stats(dve, stats[0:n, :], mom[0:n, :], state_h[0:n, b, g, :]).then_inc(mom_done, 1)
                        k += 1
                        dve.wait_ge(rstd_done, 5 * b + k)
                        dve.tensor_scalar(state_x[0:n, b, g, :], state_h[0:n, b, g, :], mom[0:n, 0:1], rstd[0:n, :],
                                          ALU.subtract, ALU.mult)
                        dve.drain()
                    n = TILE_N[2]
                    dve.tensor_scalar(xn[0:n, :], state_h[0:n, b, 2, :], 1.0, None, ALU.mult)
                    dve.drain()
                    layer_norm_stats(dve, stats[0:n, :], mom[0:n, :], xn[0:n, :])
                    dve.drain()
                    dve.tensor_copy(c["mom_last"][0:n, b, :], mom[0:n, :])
                    dve.drain().then_inc(b_done, 1)
        last_done = sem("t_last_done")
        with nc.Block() as block:
            rs = sb("rs_last", [128, B])
            mh = sb("mh_last", [128, B])
            n = TILE_N[2]

            @block.gpsimd
            def _(pool):
                pool.memset(mh[:, :], -0.5)
                pool.tensor_scalar(rs[0:n, :], c["mom_last"][0:n, :, 1], EPS, None, ALU.add)
                pool.drain()
                pool.tensor_tensor(rs[0:n, :], rs[0:n, :], mh[0:n, :], ALU.pow).then_inc(last_done, 1)

            @block.vector
            def _(dve):
                dve.wait_ge(last_done, 1)
                for b in range(B):
                    dve.tensor_scalar(state_x[0:n, b, 2, :], state_h[0:n, b, 2, :], c["mom_last"][0:n, b, 0:1], rs[0:n, b:b + 1],
                                      ALU.subtract, ALU.mult)


PIECE_BY = {"T": "act", "K": "act", "V": "act", "Q": "act", "PV": "act", "WO": "dve", "T2": "act", "F1": "act", "F2": "dve"}
PARTS = {"T": 2, "K": 8, "V": 2, "Q": 8, "PV": 8, "WO": 1, "T2": 2, "F1": 8, "F2": 1}


def steps_plan():
    before = [[] for _ in range(BLOCKS + 4)]
    after = [[] for _ in range(BLOCKS + 4)]
    pieces = lambda kind, g: [(kind, g, p) for p in range(PARTS[kind])]
    first = [("LN", 0, 0), ("N", 0, 0)] + [x for k in "TKVQ" for x in pieces(k, 0)]
    for g in (1, 2):
        s0 = GROUP0[g - 1] + (6 if g == 2 else 1)
        after[s0] += [("LN", g, 0)]
        after[s0 + 1] += [("N", g, 0)] + pieces("T", g)
        for i, x in enumerate(pieces("K", g) + pieces("V", g)):
            after[s0 + 2 + i // 2].append(x)
        after[GROUP0[g] - 1] += pieces("Q", g)
    for g in range(3):
        s = GROUP0[g + 1] + 3
        if g < 2:
            before[s] += pieces("PV", g)
            after[s] += pieces("WO", g)
            after[s + 1] += [("LN", g, 1)]
            after[s + 2] += [("N", g, 1)] + pieces("T2", g)
            for i, x in enumerate(pieces("F1", g)):
                after[s + 3 + i // 2].append(x)
            after[s + 7] += pieces("F2", g)
    last = pieces("PV", 2) + pieces("WO", 2) + [("LN", 2, 1), ("N", 2, 1)] + pieces("T2", 2) + pieces("F1", 2) + pieces("F2", 2)
    return first, before, after, last


def piece_places():
    first, before, after, last = steps_plan()
    order = first + [x for b, f in zip(before, after) for x in b + f] + last
    place, count, two_back = {}, {"act": 0, "dve": 0}, []
    k = 0
    for x in order:
        if x[0] in PIECE_BY:
            by = PIECE_BY[x[0]]
            count[by] += 1
            place[x] = (k, by, count[by])
            two_back.append((by, count[by]))
            k += 1
    return place, two_back, count


def attention_stage(nc, a, c, state_x):
    first, before, after, final = steps_plan()
    place, two_back, count = piece_places()
    n_pieces = len(place)
    with ExitStack() as ctx:
        sb = lambda n, s, d=F32: ctx.enter_context(nc.sbuf_tensor(n, s, d))
        ps = lambda n, s, d=F32: ctx.enter_context(nc.psum_tensor(n, s, d))
        sem = lambda n: ctx.enter_context(nc.semaphore(n))
        ident = c["ident"]
        wqkv = sb("wqkv", [128, 2, 3, 1024])
        wo = sb("wo", [128, 8, D])
        w1 = sb("w1", [128, 2, 1024])
        w2 = sb("w2", [128, 8, D])
        mem_v = sb("mem_v", [MEM, 1024])
        rows1 = sb("rows1", [1, 2, D])
        ones1 = sb("ones1", [1, 128])
        gb = sb("gb", [128, 2, 4])
        b1 = sb("b1", [128, 8])
        mixb = sb("mixb", [128, 2, H])
        eye8 = sb("eye8", [128, ROWS])
        diag = sb("diag", [128, ROWS])
        mix = sb("mix", [128, 2, H, ROWS])
        k_t = sb("k_t", [128, 8, KEYS])
        v = sb("v", [128, 3, 1024])
        q_bd = sb("q_bd", [128, 16, 8, 32])
        xn = sb("xn_a", [128, D])
        xn_t = sb("xn_t", [128, 2, MEM + 336])
        xn2_t = sb("xn2_t", [128, 2, 128])
        dots = sb("dots", [128, 2, KEYS])
        mixed = sb("mixed_a", [128, 2, KEYS])
        work = sb("work", [128, KEYS])
        vals = sb("vals", [128, 8, 8])
        nmax = sb("nmax", [128, 2])
        rsum = sb("rsum", [128, 2])
        rinv = sb("rinv", [128, 2])
        expd = sb("expd", [128, 2, KEYS])
        prob = sb("prob", [128, 2, 384])
        post = sb("post", [128, 2, 128])
        attn_t = sb("attn_t", [128, 3, H, 128])
        out_t = sb("out_t", [128, 8, 128])
        hid_t = sb("hid_t", [128, 8, 128])
        stats = sb("stats_a", [128, 6])
        mom = sb("mom_a", [128, 2])
        rstd = sb("rstd_a", [128, 1])
        half = sb("half_a", [128, 1])
        eps = sb("eps_a", [128, 1])
        minus = sb("minus_a", [128, 1])
        zeros = sb("zeros_a", [128, 384])
        p_dots = ps("p_dots", [128, 2, 512])
        p_mix = ps("p_mix", [128, 2, 512])
        p_post = ps("p_post", [128, 2, 512])
        p_any = ps("p_any", [128, 2, 512])
        s_w = sem("a_weights")
        s_c = sem("a_consts")
        s_kv_mem = sem("a_mem")
        s_set = sem("a_set")
        s_mixw = sem("a_mix_built")
        s_iter = sem("a_iter_done")
        dots_full = sem("a_dots_full")
        dots_out = sem("a_dots_out")
        mix_full = sem("a_mix_full")
        mix_out = sem("a_mix_out")
        max_ready = sem("a_max_ready")
        nmax_ready = sem("a_nmax_ready")
        exp_ready = sem("a_exp_ready")
        tail_zero = sem("a_tail_zero")
        prob_ready = sem("a_prob_ready")
        post_scaled = sem("a_post_scaled")
        post_full = sem("a_post_full")
        attn_out = sem("a_attn_out")
        piece_full = sem("a_piece_full")
        piece_out = {"act": sem("a_piece_out_act"), "dve": sem("a_piece_out_dve")}
        mom_ready = sem("a_mom_ready")
        rstd_ready = sem("a_rstd_ready")
        xn_ready = sem("a_xn_ready")
        ln_order = [x for x in first + [y for b_, f_ in zip(before, after) for y in b_ + f_] + final if x[0] == "LN"]
        ln_no = {x[1:]: i + 1 for i, x in enumerate(ln_order)}
        n_ln = len(ln_order)
        read_xn = {i + 1: place[("T2" if x[2] else "T", x[1], 1)][0] for i, x in enumerate(ln_order)}
        N_W = 13
        tail_no = {n: i + 1 for i, n in enumerate(n for n in range(BLOCKS) if block_width(n) < 128 * (tile_of(n) + 1))}

        def piece_bank(x):
            return p_any[:, place[x][0] % 2, :]

        def pipeline(step_first, step_block, step_piece):
            for x in first:
                step_piece(x)
            for s in range(BLOCKS + 4):
                step_first(s)
                for x in before[s]:
                    step_piece(x)
                step_block(s)
                for x in after[s]:
                    step_piece(x)
            for x in final:
                step_piece(x)

        with nc.Block() as block:
            @block.sync
            def _(sp):
                for dst, src in ((eye8[:, :], a["eye8"]), (diag[:, :], a["diag"]), (ones1[:, :], a["ones"][:, 0:128])):
                    sp.dma_start(dst, src).then_inc(s_c, 16)
                with sp.Fori(0, 2) as l:
                    sp.wait_ge(s_iter, l * B + 1)
                    loads = [(wqkv[:, :, 0, :], a["wq"][l].rearrange("(c p) n -> p c n", p=128)),
                             (wqkv[:, :, 1, :], a["wk"][l].rearrange("(c p) n -> p c n", p=128)),
                             (wqkv[:, :, 2, :], a["wv"][l].rearrange("(c p) n -> p c n", p=128)),
                             (wo[:, :, :], a["wo"][l].rearrange("(c p) n -> p c n", p=128)),
                             (w1[:, :, :], a["w1"][l].rearrange("(c p) n -> p c n", p=128)),
                             (w2[:, :, :], a["w2"][l].rearrange("(c p) n -> p c n", p=128)),
                             (mem_v[:, :], a["mem_v"][l]),
                             (rows1[:, :, :], a["bo_b2"][l]),
                             (gb[:, :, :], a["gb"][l]),
                             (b1[:, :], a["b1"][l]),
                             (k_t[:, :, 0:MEM], a["mem_k"][l])]
                    for dst, src in loads:
                        sp.dma_start(dst, src).then_inc(s_w, 16)
                    for j, name in enumerate(("pre", "post")):
                        m = a[name][l]
                        src = bass.AP(m.tensor, m.offset, [[H, H], [0, ROWS], [1, H]])
                        sp.dma_start(mixb[:, j, :], src).then_inc(s_w, 16)

            @block.gpsimd
            def _(pool):
                pool.memset(q_bd[:, :, :, :], 0.0)
                pool.memset(xn_t[:, :, :], 0.0)
                pool.memset(prob[:, :, :], 0.0)
                pool.memset(half[:, :], -0.5)
                pool.memset(eps[:, :], EPS)
                pool.memset(minus[:, :], -1.0)
                pool.memset(zeros[:, :], 0.0)
                pool.drain().then_inc(s_set, 1)
                with pool.Fori(0, 2 * B) as it:
                    nb, nl = pool.snap(it * BLOCKS), pool.snap(it * n_ln)

                    def start(s):
                        pass

                    def block_part(s):
                        n = s - 2
                        if 0 <= n < BLOCKS:
                            if n in tail_no:
                                w, end = block_width(n), 128 * (tile_of(n) + 1)
                                if n >= 2:
                                    pool.wait_ge(post_full, nb + n - 1)
                                pool.tensor_tensor(prob[:, n % 2, w:end], zeros[:, w:end], zeros[:, w:end], ALU.mult).then_inc(tail_zero, 1)
                            pool.wait_ge(max_ready, nb + n + 1)
                            pool.tensor_tensor(nmax[:, n % 2:n % 2 + 1], vals[:, 0, 0:1], minus[:, :], ALU.mult).then_inc(nmax_ready, 1)

                    def piece(x):
                        if x[0] == "LN":
                            k = ln_no[x[1:]]
                            n = TILE_N[x[1]]
                            pool.wait_ge(mom_ready, nl + k)
                            pool.tensor_tensor(rstd[0:n, :], mom[0:n, 1:2], eps[0:n, :], ALU.add)
                            pool.drain()
                            pool.tensor_tensor(rstd[0:n, :], rstd[0:n, :], half[0:n, :], ALU.pow).then_inc(rstd_ready, 1)

                    pipeline(start, block_part, piece)

            @block.tensor
            def _(pe):
                pe.wait_ge(s_set, 1)
                with pe.Fori(0, 2 * B) as it:
                    nb = pe.snap(it * BLOCKS)
                    free = {k: pe.snap(it * count[k]) for k in count}
                    if True:
                        pe.wait_ge(s_w, (it // B + 1) * (16 * N_W))
                        pe.wait_ge(s_mixw, it + 1)
                        pe.wait_ge(s_iter, it + 1)

                    def start(s):
                        n = s
                        if n < BLOCKS:
                            g, w = tile_of(n), block_width(n)
                            if n >= 2:
                                pe.wait_ge(dots_out, nb + n - 1)
                            if n in GROUP0[0:3]:
                                pe.wait_ge(piece_out["act"], free["act"] + place[("Q", g, 7)][2])
                            for j in range(2):
                                for q in range(4):
                                    last = pe.matmul(p_dots[32 * q:32 * q + 32, n % 2, 0:w], q_bd[:, n - GROUP0[g], 2 * q + j, :],
                                                     k_t[:, 2 * q + j, 0:w], start=(j == 0), stop=(j == 1))
                            last.then_inc(dots_full, 1)
                        n = s - 1
                        if 0 <= n < BLOCKS:
                            w = block_width(n)
                            pe.wait_ge(dots_out, nb + n + 1)
                            if n >= 2:
                                pe.wait_ge(mix_out, nb + n - 1)
                            pe.matmul(p_mix[:, n % 2, 0:w], mix[:, 0, :, :].rearrange("p k i -> p (k i)"), dots[:, n % 2, 0:w],
                                      start=True, stop=True).then_inc(mix_full, 1)

                    def block_part(s):
                        n = s - 3
                        if 0 <= n < BLOCKS:
                            pe.wait_ge(prob_ready, nb + n + 1)
                            pe.wait_ge(post_scaled, nb + n + 1)
                            if n >= 2:
                                pe.wait_ge(attn_out, nb + n - 1)
                            for j in range(tile_of(n) + 1):
                                last = pe.matmul(p_post[:, n % 2, 128 * j:128 * j + 128], prob[:, n % 2, 128 * j:128 * j + 128],
                                                 post[:, n % 2, :], start=(j == 0), stop=True, skip_group_check=True)
                            last.then_inc(post_full, 1)

                    def piece(x):
                        kind, g, p = x
                        if kind not in PIECE_BY:
                            return
                        k = place[x][0]
                        n, t0 = TILE_N[g], TILE0[g]
                        bank = piece_bank(x)
                        if k >= 2:
                            by, c2 = two_back[k - 2]
                            pe.wait_ge(piece_out[by], free[by] + c2)
                        if kind in ("T", "T2"):
                            if p == 0:
                                pe.wait_ge(xn_ready, it * n_ln + ln_no[(g, 0 if kind == "T" else 1)])
                            last = pe.transpose(bank[:, 0:n], xn[0:n, 128 * p:128 * p + 128], ident[0:n, 0:n])
                        elif kind == "K":
                            if p == 0:
                                pe.wait_ge(piece_out["act"], free["act"] + place[("T", g, 1)][2])
                            for j in range(2):
                                last = pe.matmul(bank[:, 0:n], wqkv[:, j, 1, 128 * p:128 * p + 128], xn_t[:, j, MEM + t0:MEM + t0 + n],
                                                 start=(j == 0), stop=(j == 1))
                        elif kind == "V":
                            m = 128 if g < 2 else n
                            for j in range(2):
                                last = pe.matmul(bank[0:m, :], xn_t[:, j, 128 * g:128 * g + m], wqkv[:, j, 2, 512 * p:512 * p + 512],
                                                 start=(j == 0), stop=(j == 1 and g > 0))
                            if g == 0:
                                last = pe.matmul(bank[0:m, :], ident[0:MEM, 0:128], mem_v[:, 512 * p:512 * p + 512], start=False, stop=True)
                        elif kind == "Q":
                            m = 8 * (-(-n // 8))
                            for j in range(2):
                                last = pe.matmul(bank[:, 0:m], wqkv[:, j, 0, 128 * p:128 * p + 128], xn_t[:, j, MEM + t0:MEM + t0 + m],
                                                 start=(j == 0), stop=(j == 1))
                        elif kind == "PV":
                            if p == 0:
                                pe.wait_ge(attn_out, nb + GROUP0[g + 1])
                                pe.wait_ge(piece_out["act"], free["act"] + place[("V", g, 1)][2])
                            for hh in range(2):
                                h = 2 * p + hh
                                for j in range(g + 1):
                                    r = 128 if j < 2 else TILE_N[2]
                                    last = pe.matmul(bank[64 * hh:64 * hh + 64, 0:n], v[0:r, j, 64 * h:64 * h + 64], attn_t[0:r, j, h, 0:n],
                                                     start=(j == 0), stop=(j == g))
                        elif kind in ("WO", "F2"):
                            src, w, r = (out_t, wo, 0) if kind == "WO" else (hid_t, w2, 1)
                            before_ = ("PV", g, 7) if kind == "WO" else ("F1", g, 7)
                            pe.wait_ge(piece_out["act"], free["act"] + place[before_][2])
                            for j in range(8):
                                pe.matmul(bank[0:n, 0:D], src[:, j, 0:n], w[:, j, :], start=(j == 0), stop=False)
                            last = pe.matmul(bank[0:n, 0:D], ones1[0:1, 0:n], rows1[0:1, r, :], start=False, stop=True)
                        elif kind == "F1":
                            if p == 0:
                                pe.wait_ge(piece_out["act"], free["act"] + place[("T2", g, 1)][2])
                            for j in range(2):
                                last = pe.matmul(bank[:, 0:n], w1[:, j, 128 * p:128 * p + 128], xn2_t[:, j, 0:n], start=(j == 0), stop=(j == 1))
                        last.then_inc(piece_full, 1)

                    pipeline(start, block_part, piece)

            @block.scalar
            def _(act):
                act.wait_ge(s_set, 1)
                with act.Fori(0, 2 * B) as it:
                    nb, np_ = act.snap(it * BLOCKS), act.snap(it * n_pieces)
                    act.wait_ge(s_w, (it // B + 1) * (16 * N_W))
                    act.wait_ge(s_mixw, it + 1)

                    def start(s):
                        n = s
                        if n < BLOCKS:
                            w = block_width(n)
                            act.wait_ge(dots_full, nb + n + 1)
                            act.activation(dots[:, n % 2, 0:w], p_dots[:, n % 2, 0:w], ACT.Copy, scale=DH ** -0.5).then_inc(dots_out, 1)
                        n = s - 1
                        if 0 <= n < BLOCKS:
                            w = block_width(n)
                            act.wait_ge(mix_full, nb + n + 1)
                            if n >= 2:
                                act.wait_ge(prob_ready, nb + n - 1)
                            act.activation(mixed[:, n % 2, 0:w], p_mix[:, n % 2, 0:w], ACT.Copy).then_inc(mix_out, 1)
                        n = s - 2
                        if 0 <= n < BLOCKS:
                            w = block_width(n)
                            act.wait_ge(nmax_ready, nb + n + 1)
                            act.activation(expd[:, n % 2, 0:w], mixed[:, n % 2, 0:w], ACT.Exp, bias=nmax[:, n % 2:n % 2 + 1]).then_inc(exp_ready, 1)

                    def block_part(s):
                        n = s - 3
                        if 0 <= n < BLOCKS:
                            g = tile_of(n)
                            act.wait_ge(prob_ready, nb + n + 1)
                            act.activation(post[:, n % 2, :], mix[:, 1, :, :].rearrange("p k i -> p (k i)"), ACT.Copy,
                                           scale=rinv[:, n % 2:n % 2 + 1]).then_inc(post_scaled, 1)
                            act.wait_ge(post_full, nb + n + 1)
                            i0 = ROWS * (n - GROUP0[g])
                            act.activation(attn_t[:, 0:g + 1, :, i0:i0 + ROWS],
                                           p_post[:, n % 2, 0:128 * (g + 1)].rearrange("p (j k i) -> p j k i", j=g + 1, k=H),
                                           ACT.Copy).then_inc(attn_out, 1)

                    def piece(x):
                        kind, g, p = x
                        if PIECE_BY.get(kind) != "act":
                            return
                        n, t0 = TILE_N[g], TILE0[g]
                        bank = piece_bank(x)
                        act.wait_ge(piece_full, np_ + place[x][0] + 1)
                        if kind == "T":
                            last = act.activation(xn_t[:, p, MEM + t0:MEM + t0 + n], bank[:, 0:n], ACT.Identity,
                                                  scale=gb[:, p, 0:1], bias=gb[:, p, 1:2])
                        elif kind == "T2":
                            last = act.activation(xn2_t[:, p, 0:n], bank[:, 0:n], ACT.Identity, scale=gb[:, p, 2:3], bias=gb[:, p, 3:4])
                        elif kind == "K":
                            last = act.activation(k_t[:, p, MEM + t0:MEM + t0 + n], bank[:, 0:n], ACT.Copy)
                        elif kind == "V":
                            m = 128 if g < 2 else n
                            last = act.activation(v[0:m, g, 512 * p:512 * p + 512], bank[0:m, :], ACT.Copy)
                        elif kind == "Q":
                            nbk = -(-n // 8)
                            for hh in range(2):
                                h4 = 2 * (p % 2) + hh
                                last = act.activation(q_bd[64 * hh:64 * hh + 64, 0:nbk, p, 8 * h4:8 * h4 + 8],
                                                      bank[64 * hh:64 * hh + 64, 0:8 * nbk].rearrange("p (b i) -> p b i", i=8), ACT.Copy)
                        elif kind == "PV":
                            last = act.activation(out_t[:, p, 0:n], bank[:, 0:n], ACT.Copy)
                        elif kind == "F1":
                            last = act.activation(hid_t[:, p, 0:n], bank[:, 0:n], ACT.Gelu, bias=b1[:, p:p + 1])
                        last.then_inc(piece_out["act"], 1)

                    pipeline(start, block_part, piece)

            @block.vector
            def _(dve):
                dve.wait_ge(s_c, 48)
                dve.sem_inc(s_iter, 1)
                with dve.Fori(0, 2 * B) as it:
                    b = dve.snap(it % B)
                    nt = dve.snap(it * len(tail_no))
                    nb, np_, nl = dve.snap(it * BLOCKS), dve.snap(it * n_pieces), dve.snap(it * n_ln)
                    dve.wait_ge(s_w, (it // B + 1) * (16 * N_W))
                    for j in range(2):
                        dve.tensor_tensor(mix[:, j, :, :], mixb[:, j, :].unsqueeze(2).broadcast_to([128, H, ROWS]),
                                          eye8[:, :].unsqueeze(1).broadcast_to([128, H, ROWS]), ALU.mult)
                    dve.drain().then_inc(s_mixw, 1)

                    def start(s):
                        n = s - 2
                        if not 0 <= n < BLOCKS:
                            return
                        w = block_width(n)
                        m = mixed[:, n % 2, :]
                        d0 = MEM + ROWS * n
                        dve.wait_ge(mix_out, nb + n + 1)
                        dve.tensor_tensor(m[:, d0:w], m[:, d0:w], diag[:, 0:w - d0], ALU.min)
                        dve.drain()
                        threshold = -BIG
                        dve.max(vals[:, 0, :], m[:, 0:w])
                        dve.drain().then_inc(max_ready, 1)
                        if n >= FULL_ROWS:
                            for r in range(1, 8):
                                src = m[:, 0:w] if r == 1 else work[:, 0:w]
                                dve.match_replace(work[:, 0:w], vals[:, r - 1, :], src, -BIG)
                                dve.drain()
                                dve.max(vals[:, r, :], work[:, 0:w])
                                dve.drain()
                            threshold = vals[:, 7, 7:8]
                        dve.wait_ge(exp_ready, nb + n + 1)
                        if n in tail_no:
                            dve.wait_ge(tail_zero, nt + tail_no[n])
                        if n >= 2:
                            dve.wait_ge(post_full, nb + n - 1)
                        dve.scalar_tensor_tensor(prob[:, n % 2, 0:w], m[:, 0:w], threshold, expd[:, n % 2, 0:w], ALU.is_ge, ALU.mult,
                                                 accum_out=rsum[:, n % 2:n % 2 + 1])
                        dve.drain()
                        dve.reciprocal(rinv[:, n % 2:n % 2 + 1], rsum[:, n % 2:n % 2 + 1]).then_inc(prob_ready, 1)

                    def block_part(s):
                        pass

                    def piece(x):
                        kind, g, p = x
                        n = TILE_N[g]
                        if kind == "LN":
                            dve.drain()
                            layer_norm_stats(dve, stats[0:n, :], mom[0:n, :], state_x[0:n, b, g, :]).then_inc(mom_ready, 1)
                        elif kind == "N":
                            k = ln_no[(g, p)]
                            if k > 1:
                                dve.wait_ge(piece_full, np_ + read_xn[k - 1] + 1)
                            dve.wait_ge(rstd_ready, nl + k)
                            dve.tensor_scalar(xn[0:n, :], state_x[0:n, b, g, :], mom[0:n, 0:1], rstd[0:n, :],
                                              ALU.subtract, ALU.mult).then_inc(xn_ready, 1)
                            dve.drain()
                        elif PIECE_BY[kind] == "dve":
                            dve.wait_ge(piece_full, np_ + place[x][0] + 1)
                            dve.tensor_tensor(state_x[0:n, b, g, :], state_x[0:n, b, g, :], piece_bank(x)[0:n, 0:D],
                                              ALU.add).then_inc(piece_out["dve"], 1)
                            dve.drain()

                    pipeline(start, block_part, piece)
                    dve.drain().then_inc(s_iter, 1)


def router_stage(nc, a, c, state_h, state_x, m):
    with ExitStack() as ctx:
        sb = lambda n, s, d=F32: ctx.enter_context(nc.sbuf_tensor(n, s, d))
        ps = lambda n, s, d=F32: ctx.enter_context(nc.psum_tensor(n, s, d))
        sem = lambda n: ctx.enter_context(nc.semaphore(n))
        ident = c["ident"]
        gate = sb("gate", [128, 2, EXPERTS])
        sg = sb("sg", [128, 2, HID])
        su = sb("su", [128, 2, HID])
        sd = sb("sd", [128, 4, D])
        tri = sb("tri", [128, 128])
        ones_c = sb("ones_c", [128, 1])
        ones_r = sb("ones_r", [1, 128])
        iota_e = sb("iota_e", [128, EXPERTS])
        iota_p = sb("iota_p", [128, 1])
        zero = sb("zero", [128, D])
        run = sb("run", [1, EXPERTS])
        xn = sb("xn_m", [128, D])
        x_t = sb("x_t", [128, 2, 128])
        sl = sb("sl", [128, 4, 128])
        hid = sb("hid", [128, 4, 128])
        top = sb("top", [128, 8])
        top_i = sb("top_i", [128, 8], U32)
        top_f = sb("top_f", [128, 1])
        e_s = sb("e_s", [128, 1])
        d_s = sb("d_s", [128, 1])
        score = sb("score", [128, 1])
        junk = sb("junk", [128, EXPERTS])
        stats = sb("stats_m", [128, 6])
        mom = sb("mom_m", [128, 2])
        rstd = sb("rstd_m", [128, 1])
        half = sb("half_m", [128, 1])
        eps = sb("eps_m", [128, 1])
        onehot = sb("onehot", [128, B * 3, EXPERTS])
        spread = sb("spread", [128, B * 3, EXPERTS])
        rank = sb("rank", [128, B * 3])
        slot_f = sb("slot_f", [128, B * 3])
        tiles_i = sb("tiles_i", [1, EXPERTS], I32)
        tiles_s = sb("tiles_s", [1, EXPERTS], I32)
        tiles_f = sb("tiles_f", [1, EXPERTS])
        ones_e = sb("ones_e", [1, EXPERTS])
        bounds = sb("bounds", [1, 2, EXPERTS])
        before = sb("before", [128, EXPERTS])
        e_col = sb("e_col", [128, 1])
        p_t = ps("pm_t", [128, 4, 128])[:, 0:2, :]
        p_g = ps("pm_g", [128, 4, 128])
        p_u = ps("pm_u", [128, 4, 128])
        p_y = ps("pm_y", [128, 512])[:, 0:D]
        p_l = ps("pm_l", [128, 512])[:, 0:EXPERTS]
        p_r = ps("pm_r", [128, 512])[:, 0:EXPERTS]
        p_l2 = p_t[:, 0, :]
        hot_now = sb("hot_now", [128, EXPERTS])
        logits = sb("logits", [128, EXPERTS])
        p_c = ps("pm_c", [128, 512])[:, 0:EXPERTS]
        p_b = ps("pm_b", [128, 8, 64])[:, 0, :].rearrange("p (j e) -> p j e", j=2)
        loaded, zeroed, ready = sem("m_loaded"), sem("m_zeroed"), sem("m_ready")
        mom_ready, rstd_ready, xn_ready = sem("m_mom"), sem("m_rstd"), sem("m_xn")
        t_full, t_out, l_full, g_full, s_out = sem("m_t_full"), sem("m_t_out"), sem("m_l_full"), sem("m_g_full"), sem("m_silu")
        hid_ready, y_full, top_ready, exp_ready = sem("m_hid"), sem("m_y_full"), sem("m_top"), sem("m_exp")
        hot_ready, r_full, tile_done = sem("m_hot"), sem("m_r_full"), sem("m_tile_done")
        bound_ready, bound_full, col_ready, row_full, slots_ready = (sem("m_bound"), sem("m_bound_full"), sem("m_col"),
                                                                     sem("m_row_full"), sem("m_slots"))
        scattered = sem("m_scattered")
        NL = 9
        ZC = 4
        with nc.Block() as block:
            @block.sync
            def _(sp):
                for dst, src in ((gate[:, :, :], a["gate_w"].rearrange("(c p) n -> p c n", p=128)),
                                 (sg[:, :, :], a["sg"].rearrange("(c p) n -> p c n", p=128)),
                                 (su[:, :, :], a["su"].rearrange("(c p) n -> p c n", p=128)),
                                 (sd[:, :, :], a["sd"].rearrange("(c p) n -> p c n", p=128)),
                                 (tri[:, :], a["tri"]), (iota_e[:, :], a["iota_e"]), (iota_p[:, :], a["iota_p"]),
                                 (ones_r[:, :], a["ones"][:, 0:128]), (ones_c[:, :], a["ones_c"])):
                    sp.dma_start(dst, src).then_inc(loaded, 16)
                sp.wait_ge(ready, 1)
                for k in range(ZC):
                    n = SLOT_TILES // ZC
                    sp.dma_start(m["xs"][128 * n * k:128 * n * (k + 1), :].rearrange("(t p) n -> p t n", p=128),
                                 zero[:, :].unsqueeze(1).broadcast_to([128, n, D])).then_inc(zeroed, 16)
                sp.wait_ge(zeroed, 16 * ZC)

            @block.gpsimd
            def _(pool):
                pool.memset(half[:, :], -0.5)
                pool.memset(eps[:, :], EPS)
                pool.memset(zero[:, :], 0.0)
                pool.memset(run[:, :], 0.0)
                pool.memset(ones_e[:, :], 1.0)
                pool.memset(onehot[:, :, :], 0.0)
                pool.memset(rank[:, :], 0.0)
                pool.drain().then_inc(ready, 1)
                with pool.Fori(0, B) as b:
                    t0 = pool.snap(b * 3)
                    for g in range(3):
                        n = TILE_N[g]
                        pool.wait_ge(mom_ready, t0 + g + 1)
                        pool.tensor_tensor(rstd[0:n, :], mom[0:n, 1:2], eps[0:n, :], ALU.add)
                        pool.drain()
                        pool.tensor_tensor(rstd[0:n, :], rstd[0:n, :], half[0:n, :], ALU.pow).then_inc(rstd_ready, 1)
                pool.wait_ge(slots_ready, 1)
                pool.wait_ge(zeroed, 16 * ZC)
                for b in range(B):
                    for g in range(3):
                        n, t = TILE_N[g], 3 * b + g
                        pool.indirect_dma_start(m["xs"], bass.IndirectOffsetOnAxis(ap=m["slot"][0:n, t:t + 1], axis=0),
                                                state_x[0:n, b, g, :], None).then_inc(scattered, 16)
                pool.wait_ge(scattered, 16 * 3 * B)

            @block.tensor
            def _(pe):
                pe.wait_ge(loaded, 16 * NL)
                pe.wait_ge(ready, 1)
                with pe.Fori(0, B) as b:
                    t0 = pe.snap(b * 3)
                    for g in range(3):
                        n, t = TILE_N[g], t0 + g
                        pe.wait_ge(xn_ready, t + 1)
                        for j in range(2):
                            last = pe.transpose(p_t[:, j, 0:n], xn[0:n, 128 * j:128 * j + 128], ident[0:n, 0:n])
                        last.then_inc(t_full, 1)
                        pe.wait_ge(t_out, t + 1)
                        for j in range(2):
                            last = pe.matmul(p_l[0:n, :], x_t[:, j, 0:n], gate[:, j, :], start=(j == 0), stop=(j == 1))
                        last.then_inc(l_full, 1)
                        for p, w in ((p_g, sg), (p_u, su)):
                            for q in range(4):
                                for j in range(2):
                                    last = pe.matmul(p[:, q, 0:n], w[:, j, 128 * q:128 * q + 128], x_t[:, j, 0:n],
                                                     start=(j == 0 and q == 0), stop=(j == 1), skip_group_check=True)
                        last.then_inc(g_full, 1)
                        pe.wait_ge(hot_ready, t + 1)
                        hot = hot_now[0:n, :]
                        pe.matmul(p_r[0:n, :], tri[0:n, 0:n], hot, start=True, stop=False)
                        pe.matmul(p_r[0:n, :], ones_r[0:1, 0:n], run[0:1, :], start=False, stop=True)
                        pe.matmul(p_c[0:1, :], ones_c[0:n, 0:1], hot, start=True, stop=True).then_inc(r_full, 1)
                        pe.wait_ge(hid_ready, t + 1)
                        for q in range(4):
                            last = pe.matmul(p_y[0:n, :], hid[:, q, 0:n], sd[:, q, :], start=(q == 0), stop=(q == 3))
                        last.then_inc(y_full, 1)
                pe.wait_ge(bound_ready, 1)
                pe.matmul(p_b[:, :, :], ones_r[0:1, :], bounds[0:1, :, :], start=True, stop=True).then_inc(bound_full, 1)
                pe.wait_ge(col_ready, 1)
                pe.matmul(p_l2[0:1, 0:SLOT_TILES], e_col[0:SLOT_TILES, :],
                          ident[0:SLOT_TILES, 0:SLOT_TILES], start=True, stop=True).then_inc(row_full, 1)

            @block.scalar
            def _(act):
                with act.Fori(0, B) as b:
                    t0 = act.snap(b * 3)
                    for g in range(3):
                        n, t = TILE_N[g], t0 + g
                        act.wait_ge(t_full, t + 1)
                        act.activation(x_t[:, :, 0:n], p_t[:, :, 0:n], ACT.Copy).then_inc(t_out, 1)
                        act.wait_ge(top_ready, t + 1)
                        act.activation(e_s[0:n, :], top[0:n, 0:1], ACT.Exp, scale=-1.0).then_inc(exp_ready, 1)
                        act.wait_ge(g_full, t + 1)
                        act.activation(sl[:, :, 0:n], p_g[:, :, 0:n], ACT.Silu).then_inc(s_out, 1)

            @block.vector
            def _(dve):
                dve.wait_ge(loaded, 16 * NL)
                dve.wait_ge(ready, 1)
                with dve.Fori(0, B) as b:
                    t0 = dve.snap(b * 3)
                    for g in range(3):
                        n, t = TILE_N[g], t0 + g
                        h, x = state_h[0:n, b, g, :], state_x[0:n, b, g, :]
                        dve.tensor_tensor(h, h, x, ALU.add)
                        dve.drain()
                        layer_norm_stats(dve, stats[0:n, :], mom[0:n, :], h).then_inc(mom_ready, 1)
                        dve.wait_ge(rstd_ready, t + 1)
                        dve.tensor_scalar(xn[0:n, :], h, mom[0:n, 0:1], rstd[0:n, :], ALU.subtract, ALU.mult).then_inc(xn_ready, 1)
                        dve.wait_ge(l_full, t + 1)
                        dve.tensor_copy(logits[0:n, :], p_l[0:n, :])
                        dve.drain()
                        dve.max(top[0:n, :], logits[0:n, :])
                        dve.drain()
                        dve.max_index(top_i[0:n, :], top[0:n, :], logits[0:n, :]).then_inc(top_ready, 1)
                        dve.drain()
                        dve.tensor_copy(top_f[0:n, :], top_i[0:n, 0:1])
                        dve.drain()
                        dve.tensor_scalar(hot_now[0:n, :], iota_e[0:n, :], top_f[0:n, :], None, ALU.is_equal).then_inc(hot_ready, 1)
                        dve.drain()
                        dve.tensor_copy(onehot[0:n, t, :], hot_now[0:n, :])
                        dve.wait_ge(exp_ready, t + 1)
                        dve.tensor_scalar(d_s[0:n, :], e_s[0:n, :], 1.0, None, ALU.add)
                        dve.drain()
                        dve.reciprocal(score[0:n, :], d_s[0:n, :])
                        dve.drain()
                        dve.tensor_scalar(x, xn[0:n, :], score[0:n, :], None, ALU.mult)
                        dve.wait_ge(s_out, t + 1)
                        dve.tensor_tensor(hid[:, :, 0:n], sl[:, :, 0:n], p_u[:, :, 0:n], ALU.mult).then_inc(hid_ready, 1)
                        dve.wait_ge(r_full, t + 1)
                        dve.tensor_tensor(junk[0:n, :], hot_now[0:n, :], p_r[0:n, :], ALU.mult)
                        dve.tensor_tensor(run[:, :], run[:, :], p_c[0:1, :], ALU.add)
                        dve.drain()
                        dve.tensor_reduce(rank[0:n, bass.ds(t, 1)], junk[0:n, :], AX.X, ALU.add)
                        dve.wait_ge(y_full, t + 1)
                        dve.tensor_tensor(h, h, p_y[0:n, :], ALU.add)
                        dve.drain()
                dve.tensor_scalar(tiles_i[:, :], run[:, :], 127.0, None, ALU.add)
                dve.drain()
                dve.tensor_scalar(tiles_s[:, :], tiles_i[:, :], 7, None, ALU.arith_shift_right)
                dve.drain()
                dve.tensor_copy(tiles_f[:, :], tiles_s[:, :])
                dve.drain()
                dve.tensor_tensor_scan(bounds[:, 0, :], ones_e[:, :], tiles_f[:, :], 0.0, ALU.mult, ALU.add)
                dve.drain()
                dve.tensor_tensor(junk[0:1, :], bounds[:, 0, :], tiles_f[:, :], ALU.subtract)
                dve.drain()
                dve.tensor_scalar(bounds[:, 1, :], junk[0:1, :], 128.0, None, ALU.mult).then_inc(bound_ready, 1)
                dve.wait_ge(bound_full, 1)
                dve.tensor_tensor(spread[:, :, :], onehot[:, :, :], p_b[:, 1, :].unsqueeze(1).broadcast_to([128, 3 * B, EXPERTS]), ALU.mult)
                dve.tensor_scalar(before[:, :], p_b[:, 0, :], iota_p[:, 0:1], None, ALU.is_le)
                dve.drain()
                dve.tensor_reduce(slot_f[:, :], spread[:, :, :], AX.X, ALU.add)
                dve.tensor_reduce(e_col[:, :], before[:, :], AX.X, ALU.add)
                dve.drain()
                dve.tensor_scalar(e_col[:, :], e_col[:, :], EXPERTS - 1.0, None, ALU.min).then_inc(col_ready, 1)
                dve.tensor_tensor(m["slot"][:, :], slot_f[:, :], rank[:, :], ALU.add).then_inc(slots_ready, 1)
                dve.wait_ge(row_full, 1)
                dve.tensor_copy(m["experts"][:, :], p_l2[0:1, 0:SLOT_TILES])


def experts_stage(nc, a, c, m):
    with ExitStack() as ctx:
        sb = lambda n, s, d=F32: ctx.enter_context(nc.sbuf_tensor(n, s, d))
        ps = lambda n, s, d=F32: ctx.enter_context(nc.psum_tensor(n, s, d))
        sem = lambda n: ctx.enter_context(nc.semaphore(n))
        ident = c["ident"]
        wg = sb("wg", [128, 2, 2, HID])
        wu = sb("wu", [128, 2, 2, HID])
        wd = sb("wd", [128, 2, 4, D])
        xs = sb("xs_sb", [128, 2, D])
        x_t = sb("xs_t", [128, 2, 2, 128])
        sl = sb("sl_e", [128, 2, 4, 128])
        hid = sb("hid_e", [128, 2, 4, 128])
        y = sb("y_e", [128, 2, D])
        p_t = ps("pe_t", [128, 1, 4, 128])
        p_g = ps("pe_g", [128, 2, 4, 128])
        p_u = ps("pe_u", [128, 2, 4, 128])
        p_y = ps("pe_y", [128, 2, 512])
        in_x, in_w = [sem("e_in_x0"), sem("e_in_x1")], [sem("e_in_w0"), sem("e_in_w1")]
        t_full, t_out, g_full, s_out, hid_ready, y_full, y_out = [sem("e_" + k) for k in (
            "t_full", "t_out", "g_full", "silu", "hid", "y_full", "y_out")]
        stored = [sem("e_stored0"), sem("e_stored1")]
        with nc.Block() as block:
            @block.sync
            def _(sp):
                with sp.Fori(0, SLOT_TILES // 2) as i:
                    for u in range(2):
                        t = i * 2 + u
                        e = sp.value_load(m["experts"][0:1, bass.ds(t, 1)], min_val=0, max_val=EXPERTS - 1)
                        sp.wait_ge(y_full, t + 1)
                        sp.dma_start(xs[:, u, :], m["xs"].rearrange("(t p) n -> t p n", p=128)[t]).then_inc(in_x[u], 16)
                        sp.dma_start(wg[:, u, :, :], a["rg"][e].rearrange("(c p) n -> p c n", p=128)).then_inc(in_w[u], 16)
                        sp.dma_start(wu[:, u, :, :], a["ru"][e].rearrange("(c p) n -> p c n", p=128)).then_inc(in_w[u], 16)
                        sp.dma_start(wd[:, u, :, :], a["rd"][e].rearrange("(c p) n -> p c n", p=128)).then_inc(in_w[u], 16)

            @block.tensor
            def _(pe):
                pe.sem_inc(y_full, 2)
                with pe.Fori(0, SLOT_TILES // 2) as i:
                    for u in range(2):
                        t = i * 2 + u
                        pe.wait_ge(in_x[u], i * 16 + 16)
                        for j in range(2):
                            last = pe.transpose(p_t[:, 0, j, :], xs[:, u, 128 * j:128 * j + 128], ident[:, :])
                        last.then_inc(t_full, 1)
                        pe.wait_ge(in_w[u], i * 48 + 48)
                        pe.wait_ge(t_out, t + 1)
                        for p, w in ((p_g, wg), (p_u, wu)):
                            for q in range(4):
                                for j in range(2):
                                    last = pe.matmul(p[:, u, q, :], w[:, u, j, 128 * q:128 * q + 128], x_t[:, u, j, :],
                                                     start=(j == 0 and q == 0), stop=(j == 1), skip_group_check=True)
                        last.then_inc(g_full, 1)
                        pe.wait_ge(hid_ready, t + 1)
                        pe.wait_ge(y_out, t + 1)
                        for q in range(4):
                            last = pe.matmul(p_y[:, u, 0:D], hid[:, u, q, :], wd[:, u, q, :], start=(q == 0), stop=(q == 3))
                        last.then_inc(y_full, 1)

            @block.scalar
            def _(act):
                with act.Fori(0, SLOT_TILES // 2) as i:
                    for u in range(2):
                        t = i * 2 + u
                        act.wait_ge(t_full, t + 1)
                        act.activation(x_t[:, u, :, :], p_t[:, 0, 0:2, :], ACT.Copy).then_inc(t_out, 1)
                        act.wait_ge(g_full, t + 1)
                        act.activation(sl[:, u, :, :], p_g[:, u, :, :], ACT.Silu).then_inc(s_out, 1)
                        act.wait_ge(y_out, t + 2)
                        act.dma_start(m["ys"].rearrange("(t p) n -> t p n", p=128)[t], y[:, u, :]).then_inc(stored[u], 16)
                for u in range(2):
                    act.wait_ge(stored[u], 16 * (SLOT_TILES // 2) + 16)

            @block.vector
            def _(dve):
                dve.sem_inc(y_out, 1)
                for u in range(2):
                    dve.sem_inc(stored[u], 16)
                with dve.Fori(0, SLOT_TILES // 2) as i:
                    for u in range(2):
                        t = i * 2 + u
                        dve.wait_ge(s_out, t + 1)
                        dve.tensor_tensor(hid[:, u, :, :], sl[:, u, :, :], p_u[:, u, :, :], ALU.mult).then_inc(hid_ready, 1)
                        dve.wait_ge(y_full, t + 3)
                        dve.wait_ge(stored[u], i * 16 + 16)
                        dve.tensor_copy(y[:, u, :], p_y[:, u, 0:D]).then_inc(y_out, 1)


def combine_stage(nc, out, state_h, m):
    RING = 6
    with ExitStack() as ctx:
        sem = lambda n: ctx.enter_context(nc.semaphore(n))
        got = ctx.enter_context(nc.sbuf_tensor("got", [128, RING, D], F32))
        fetched, added, stored = [sem(f"c_fetched{i}") for i in range(RING)], sem("c_added"), sem("c_stored")
        tiles = [(b, g) for b in range(B) for g in range(3)]
        with nc.Block() as block:
            @block.gpsimd
            def _(pool):
                for t, (b, g) in enumerate(tiles):
                    n = TILE_N[g]
                    if t >= RING:
                        pool.wait_ge(added, t - RING + 1)
                    pool.indirect_dma_start(got[0:n, t % RING, :], None, m["ys"],
                                            bass.IndirectOffsetOnAxis(ap=m["slot"][0:n, t:t + 1], axis=0)).then_inc(fetched[t % RING], 16)

            @block.vector
            def _(dve):
                for t, (b, g) in enumerate(tiles):
                    n = TILE_N[g]
                    dve.wait_ge(fetched[t % RING], 16 * (t // RING + 1))
                    dve.tensor_tensor(state_h[0:n, b, g, :], state_h[0:n, b, g, :], got[0:n, t % RING, :], ALU.add).then_inc(added, 1)

            @block.sync
            def _(sp):
                for t, (b, g) in enumerate(tiles):
                    sp.wait_ge(added, t + 1)
                    sp.dma_start(out[b, TILE0[g]:TILE0[g] + TILE_N[g], :], state_h[0:TILE_N[g], b, g, :]).then_inc(stored, 16)
                sp.wait_ge(stored, 16 * len(tiles))


def build(nc, a, out):
    with ExitStack() as ctx:
        sb = lambda n, s, d=F32: ctx.enter_context(nc.sbuf_tensor(n, s, d))
        state_h = sb("state_h", [128, B, 3, D])
        state_x = sb("state_x", [128, B, 3, D])
        c = {"ident": sb("ident", [128, 128]), "mom_last": sb("mom_last", [128, B, 2])}
        m = {"slot": sb("slot", [128, 3 * B], U32), "experts": sb("experts", [1, SLOT_TILES], I32),
             "xs": nc.dram_tensor("xs_slots", (SLOT_TILES * 128, D), F32, kind="Internal").ap(),
             "ys": nc.dram_tensor("ys_slots", (SLOT_TILES * 128, D), F32, kind="Internal").ap()}
        tokens_stage(nc, a, c, state_h, state_x)
        attention_stage(nc, a, c, state_x)
        router_stage(nc, a, c, state_h, state_x, m)
        experts_stage(nc, a, c, m)
        combine_stage(nc, out, state_h, m)


def kernel(**x):
    import concourse.bacc as _bacc
    from concourse.bass_utils import run_bass_kernel_spmd as _run

    t = {k: np.asarray(v) for k, v in x.items()}
    cat = np.concatenate
    tok = lambda k: t["L0_tok_" + k]
    att = lambda k: t["L0_attn_" + k]
    eye = np.eye(128, dtype=np.float32)
    row = lambda v: v.reshape(1, -1)
    feat = np.stack([att("ln1_g"), att("ln1_b"), att("ln2_g"), att("ln2_b")], 1).reshape(2, 4, 2, 128)
    i8 = np.arange(128) % ROWS
    arrays = {
        "x": t["x"], "ids": np.stack([t["x_txt"], t["itok_BS_0_4096"]], 0).transpose(2, 1, 0),
        "fractions": np.stack([t["fside_BS_delta_" + k] for k in ("x1", "x2", "y1", "y2")], 0).transpose(2, 0, 1),
        "Wq": cat([tok("Wq_w").T, row(tok("Wq_b"))]),
        "Wkv": cat([cat([tok("Wk_w").T, row(tok("Wk_b"))]), cat([tok("Wv_w").T, row(tok("Wv_b"))])], 1),
        "id_b": cat([np.broadcast_to(eye[:64, None, :64], (64, HD, 64)), tok("out_b").reshape(1, HD, 64)]),
        "w_bias_t": tok("w_bias").T, "mask_t": np.ascontiguousarray(tok("local_mask").T).view(np.int32),
        "out_w": tok("out_w"), "ln_g": tok("ln_g"), "ln_b": tok("ln_b"), "embeds": t["L0_txt_loc_embeds"],
        "wq": att("wq"), "wk": att("wk"), "wv": att("wv"), "wo": att("wo"), "w1": att("w1"), "w2": att("w2"),
        "mem_k": att("mem_k").reshape(2, 8, 2, MEM, DH).transpose(0, 2, 4, 1, 3).reshape(2, 128, 8, MEM),
        "mem_v": att("mem_v").transpose(0, 2, 1, 3).reshape(2, MEM, H * DH),
        "pre": att("pre_proj"), "post": att("post_proj"),
        "bo_b2": np.stack([att("bo"), att("b2")], 1).reshape(2, 1, 2, D), "b1": att("b1").reshape(2, 8, 128).transpose(0, 2, 1),
        "gb": feat.transpose(0, 3, 2, 1),
        "gate_w": t["L0_ffn_gate_w"], "sg": t["L0_ffn_shared_gate_w"], "su": t["L0_ffn_shared_up_w"], "sd": t["L0_ffn_shared_down_w"],
        "rg": t["L0_ffn_routed_gate_w"], "ru": t["L0_ffn_routed_up_w"], "rd": t["L0_ffn_routed_down_w"],
        "ident": eye, "ones": np.ones((1, L * HD), np.float32), "ones_c": np.ones((128, 1), np.float32),
        "eye8": eye[:ROWS, :ROWS][i8],
        "diag": np.where(np.arange(ROWS)[None, :] <= i8[:, None], np.float32(BIG), np.float32(-BIG)),
        "tri": np.triu(np.ones((128, 128), np.float32), 1),
        "iota_e": np.broadcast_to(np.arange(EXPERTS, dtype=np.float32), (128, EXPERTS)),
        "iota_p": np.arange(128, dtype=np.float32).reshape(128, 1),
    }
    nc = _bacc.Bacc("TRN2", target_bir_lowering=False, num_devices=1)
    arrays = {k: np.ascontiguousarray(v) for k, v in arrays.items()}
    a = {k: nc.dram_tensor("in_" + k, v.shape, mybir.dt.from_np(v.dtype), kind="ExternalInput").ap() for k, v in arrays.items()}
    out = nc.dram_tensor("out_0", (B, SEQ, D), F32, kind="ExternalOutput").ap()
    build(nc, a, out)
    r = _run(nc, [{"in_" + k: v for k, v in arrays.items()}], core_ids=[0])
    return r.results[0]["out_0"]
```

```python
from contextlib import ExitStack

import numpy as np
import concourse.bass as bass
from concourse import mybir

F32 = mybir.dt.float32
I32 = mybir.dt.int32
U32 = mybir.dt.uint32
U8 = mybir.dt.uint8
ALU = mybir.AluOpType
ACT = mybir.ActivationFunctionType
AX = mybir.AxisListType

B, F, L, HD, D = 8, 64, 256, 4, 256
S_TXT = 77
SEQ = L + S_TXT
H, DH, MEM = 16, 64, 32
KEYS = SEQ + MEM
TILE0 = (0, 96, 224)
TILE_N = (96, 128, 109)
ROWS = 8
BLOCKS = -(-SEQ // ROWS)
GROUP0 = (0, 12, 28, BLOCKS)
FULL_ROWS = MEM // ROWS
EXPERTS, HID = 32, 512
SLOT_TILES = EXPERTS + (B * SEQ - EXPERTS) // 128
BIG = 3.4028234663852886e38
EPS = 1e-5


def all_rows(vector, rows):
    return bass.AP(vector.tensor, vector.offset, [[0, rows], [1, vector.shape[-1]]])


def block_width(n):
    return min(MEM + ROWS * (n + 1), KEYS)


def tile_of(n):
    return sum(n >= g for g in GROUP0[1:3])


def layer_norm_stats(dve, stats, moments, source):
    dve.bn_stats(stats, source)
    dve.drain()
    return dve.bn_aggr(moments, stats)


def tokens_stage(nc, a, c, state_h, state_x):
    with ExitStack() as ctx:
        sb = lambda n, s, d=F32: ctx.enter_context(nc.sbuf_tensor(n, s, d))
        ps = lambda n, s, d=F32: ctx.enter_context(nc.psum_tensor(n, s, d))
        sem = lambda n: ctx.enter_context(nc.semaphore(n))
        xa = sb("xa", [65, L * HD])
        w_q = sb("w_q", [65, 64])
        w_kv = sb("w_kv", [65, 128])
        id_b = sb("id_b", [65, HD, 64])
        ew = sb("ew", [128, 2, L])
        mask8 = sb("mask8", [128, 2, L // 4], I32)
        maskf = sb("maskf", [128, 2, L])
        w_out = sb("w_out", [128, 2, D])
        gain = sb("gain", [128, D])
        shift = sb("shift", [128, D])
        ekv = sb("ekv", [128, 2, 2, D])
        e_q = sb("e_q", [128, 2, L])
        dq = sb("dq", [128, 2, L])
        rq = sb("rq", [128, 2, L])
        y_t = sb("y_t", [128, 2, L])
        stats = sb("stats", [128, 6])
        mom = sb("mom", [128, 2])
        rstd = sb("rstd", [128, 1])
        half = sb("half", [128, 1])
        xn = sb("xn", [128, D])
        xg = sb("xg", [128, D])
        ids = sb("ids", [S_TXT, B, 2], I32)
        idf = sb("idf", [S_TXT, B, 2])
        pad = sb("pad", [S_TXT, B, 2])
        idx = sb("idx", [S_TXT, B, 2], U32)
        fr = sb("fr", [S_TXT, 4, B])
        w4 = sb("w4", [S_TXT, 4, B])
        emb = sb("emb", [S_TXT, 2, D])
        mixed = sb("mixed", [S_TXT, D])
        p_kv = ps("p_kv", [128, 2, HD, 2, 64])
        p_q = ps("p_q", [128, 2, L])
        p_num = ps("p_num", [128, 2, L])
        p_den = ps("p_den", [128, 2, L])
        p_h = ps("p_h", [128, 3, 512])
        loaded = sem("t_loaded")
        x_in = sem("t_x_in")
        ready = sem("t_ready")
        kv_full = sem("t_kv_full")
        q_full = sem("t_q_full")
        ek_done = sem("t_ek_done")
        eq_done = sem("t_eq_done")
        ekv_done = sem("t_ekv_done")
        nd_full = sem("t_nd_full")
        y_done = sem("t_y_done")
        h_full = sem("t_h_full")
        mom_done = sem("t_mom_done")
        rstd_done = sem("t_rstd_done")
        gathered = sem("t_gathered")
        text_done = sem("t_text_done")
        text_moved = sem("t_text_moved")
        b_done = sem("t_b_done")
        idx_done = sem("t_idx_done")
        chain = sem("t_chain")
        NLOAD = 12
        xv = xa[:, :].rearrange("c (l h) -> c h l", h=HD)
        with nc.Block() as block:
            @block.sync
            def _(sp):
                loads = [(w_q[:, :], a["Wq"]), (w_kv[:, :], a["Wkv"]), (id_b[:, :, :], a["id_b"]),
                         (ew[:, :, :], a["w_bias_t"].rearrange("(s p) t -> p s t", p=128)),
                         (mask8[:, :, :], a["mask_t"].rearrange("(s p) t -> p s t", p=128)),
                         (w_out[:, :, :], a["out_w"].rearrange("(c p) n -> p c n", p=128)),
                         (gain[:, :], all_rows(a["ln_g"], 128)),
                         (shift[:, :], all_rows(a["ln_b"], 128)),
                         (ids[:, :, :], a["ids"]), (fr[:, :, :], a["fractions"]),
                         (c["ident"][:, :], a["ident"]), (xa[64:65, :], a["ones"])]
                assert len(loads) == NLOAD
                for dst, src in loads:
                    sp.dma_start(dst, src).then_inc(loaded, 16)
                with sp.Fori(0, B) as b:
                    sp.wait_ge(b_done, b + 1)
                    sp.dma_start(xa[0:64, :], a["x"][b].rearrange("c l h -> c (l h)")).then_inc(x_in, 16)
                    sp.wait_ge(text_done, b + 1)
                    sp.dma_start(state_h[32:32 + S_TXT, b, 2, :], mixed[:, :]).then_inc(text_moved, 16)
                sp.wait_ge(text_moved, 16 * B)

            @block.gpsimd
            def _(pool):
                pool.memset(half[:, :], -0.5)
                pool.drain()
                pool.wait_ge(idx_done, 1)
                for b in range(B):
                    if b:
                        pool.wait_ge(text_done, b)
                    for j in range(2):
                        pool.indirect_dma_start(emb[:, j, :], None, a["embeds"],
                                                bass.IndirectOffsetOnAxis(ap=idx[:, b, j:j + 1], axis=0)).then_inc(gathered, 16)
                    for k, n in enumerate((96, 96, 128, 128, 32)):
                        pool.wait_ge(mom_done, 5 * b + k + 1)
                        pool.tensor_scalar(rstd[0:n, :], mom[0:n, 1:2], EPS, None, ALU.add)
                        pool.drain()
                        pool.tensor_tensor(rstd[0:n, :], rstd[0:n, :], half[0:n, :], ALU.pow).then_inc(rstd_done, 1)

            @block.tensor
            def _(pe):
                pe.wait_ge(loaded, 16 * NLOAD)
                pe.wait_ge(ready, 1)
                with pe.Fori(0, B) as b:
                    pe.wait_ge(x_in, 16 * b + 16)
                    for s in range(2):
                        for h in range(HD):
                            last = pe.matmul(p_kv[:, s, h, :, :], xv[:, h, s * 128:s * 128 + 128], w_kv[:, :], start=(h == 0), stop=True,
                                             skip_group_check=True)
                    last.then_inc(kv_full, 1)
                    for h in range(HD):
                        last = pe.matmul(p_q[64 * (h % 2):64 * (h % 2) + 64, h // 2, :], w_q[:, :], xv[:, h, :],
                                         start=(h // 2 == 0), stop=True, skip_group_check=True)
                    last.then_inc(q_full, 1)
                    pe.wait_ge(ekv_done, b + 1)
                    for out, j in ((p_num, 0), (p_den, 1)):
                        for m in range(2):
                            for s in range(2):
                                last = pe.matmul(out[:, m, :], ekv[:, s, j, m * 128:m * 128 + 128], ew[:, s, :],
                                                 start=(m == 0 and s == 0), stop=(s == 1), skip_group_check=True)
                    last.then_inc(nd_full, 1)
                    pe.wait_ge(y_done, b + 1)
                    for g, (t0, n) in enumerate(((0, 96), (96, 128), (224, 32))):
                        for m in range(2):
                            pe.matmul(p_h[0:n, g, 0:D], y_t[:, m, t0:t0 + n], w_out[:, m, :], start=(m == 0), stop=False,
                                      skip_group_check=True)
                        for h in range(HD):
                            last = pe.matmul(p_h[0:n, g, 64 * h:64 * h + 64], xv[:, h, t0:t0 + n], id_b[:, h, :],
                                             start=False, stop=True, skip_group_check=True)
                        last.then_inc(h_full, 1)

            @block.scalar
            def _(act):
                act.wait_ge(chain, 3)
                act.activation(ew[:, :, :], ew[:, :, :], ACT.Exp).then_inc(ready, 1)
                with act.Fori(0, B) as b:
                    act.wait_ge(kv_full, b + 1)
                    act.activation(ekv[:, :, 1, :].rearrange("p s (h d) -> p s h d", h=HD), p_kv[:, :, :, 0, :], ACT.Exp).then_inc(ek_done, 1)
                    act.wait_ge(q_full, b + 1)
                    act.activation(e_q[:, :, :], p_q[:, :, :], ACT.Exp, scale=-1.0).then_inc(eq_done, 1)

            @block.vector
            def _(dve):
                dve.wait_ge(loaded, 16 * NLOAD)
                dve.tensor_copy(maskf[:, :, :], mask8[:, :, :].bitcast(U8))
                dve.tensor_copy(idf[:, :, :], ids[:, :, :]).then_inc(chain, 2)
                dve.drain()
                dve.tensor_tensor(ew[:, :, :], ew[:, :, :], maskf[:, :, :], ALU.mult).then_inc(chain, 1)
                dve.tensor_scalar(pad[:, :, :], idf[:, :, :], -1.0, 4097.0, ALU.is_equal, ALU.mult)
                dve.drain()
                dve.tensor_tensor(idx[:, :, :], idf[:, :, :], pad[:, :, :], ALU.add).then_inc(idx_done, 1)
                for k, (u, v) in enumerate(((1, 3), (1, 2), (0, 3), (0, 2))):
                    dve.tensor_tensor(w4[:, k, :], fr[:, u, :], fr[:, v, :], ALU.mult)
                dve.wait_ge(ready, 1)
                dve.drain().then_inc(b_done, 1)
                with dve.Fori(0, B) as b:
                    dve.wait_ge(ek_done, b + 1)
                    for s in range(2):
                        last = dve.tensor_tensor(ekv[:, s, 0, :].rearrange("p (h d) -> p h d", h=HD), p_kv[:, s, :, 1, :],
                                                 ekv[:, s, 1, :].rearrange("p (h d) -> p h d", h=HD), ALU.mult)
                    last.then_inc(ekv_done, 1)
                    dve.wait_ge(nd_full, b + 1)
                    dve.wait_ge(eq_done, b + 1)
                    dve.scalar_tensor_tensor(dq[:, :, :], e_q[:, :, :], 1.0, p_den[:, :, :], ALU.add, ALU.mult)
                    dve.drain()
                    dve.reciprocal(rq[:, :, :], dq[:, :, :])
                    dve.drain()
                    dve.tensor_tensor(y_t[:, :, :], p_num[:, :, :], rq[:, :, :], ALU.mult).then_inc(y_done, 1)
                    dve.wait_ge(gathered, 32 * b + 32)
                    dve.tensor_scalar(mixed[:, :], emb[:, 0, :], w4[:, 0, bass.ds(b, 1)], None, ALU.mult)
                    for k in range(1, 4):
                        dve.drain()
                        last = dve.scalar_tensor_tensor(mixed[:, :], emb[:, 1, :], w4[:, k, bass.ds(b, 1)], mixed[:, :], ALU.mult, ALU.add)
                    last.then_inc(text_done, 1)
                    k = 0
                    for g, n in enumerate((96, 128, 32)):
                        dve.drain()
                        dve.wait_ge(h_full, 3 * b + g + 1)
                        layer_norm_stats(dve, stats[0:n, :], mom[0:n, :], p_h[0:n, g, 0:D]).then_inc(mom_done, 1)
                        k += 1
                        dve.wait_ge(rstd_done, 5 * b + k)
                        dve.tensor_scalar(xn[0:n, :], p_h[0:n, g, 0:D], mom[0:n, 0:1], rstd[0:n, :], ALU.subtract, ALU.mult)
                        dve.drain()
                        dve.tensor_tensor(xg[0:n, :], xn[0:n, :], gain[0:n, :], ALU.mult)
                        dve.drain()
                        if g == 2:
                            dve.tensor_tensor(state_h[0:n, b, g, :], xg[0:n, :], shift[0:n, :], ALU.add)
                            dve.drain()
                            dve.wait_ge(text_moved, 16 * b + 16)
                            break
                        dve.tensor_tensor(state_h[0:n, b, g, :], xg[0:n, :], shift[0:n, :], ALU.add)
                        dve.drain()
                        layer_norm_stats(dve, stats[0:n, :], mom[0:n, :], state_h[0:n, b, g, :]).then_inc(mom_done, 1)
                        k += 1
                        dve.wait_ge(rstd_done, 5 * b + k)
                        dve.tensor_scalar(state_x[0:n, b, g, :], state_h[0:n, b, g, :], mom[0:n, 0:1], rstd[0:n, :],
                                          ALU.subtract, ALU.mult)
                        dve.drain()
                    n = TILE_N[2]
                    dve.tensor_scalar(xn[0:n, :], state_h[0:n, b, 2, :], 1.0, None, ALU.mult)
                    dve.drain()
                    layer_norm_stats(dve, stats[0:n, :], mom[0:n, :], xn[0:n, :])
                    dve.drain()
                    dve.tensor_copy(c["mom_last"][0:n, b, :], mom[0:n, :])
                    dve.drain().then_inc(b_done, 1)
        last_done = sem("t_last_done")
        with nc.Block() as block:
            rs = sb("rs_last", [128, B])
            mh = sb("mh_last", [128, B])
            n = TILE_N[2]

            @block.gpsimd
            def _(pool):
                pool.memset(mh[:, :], -0.5)
                pool.tensor_scalar(rs[0:n, :], c["mom_last"][0:n, :, 1], EPS, None, ALU.add)
                pool.drain()
                pool.tensor_tensor(rs[0:n, :], rs[0:n, :], mh[0:n, :], ALU.pow).then_inc(last_done, 1)

            @block.vector
            def _(dve):
                dve.wait_ge(last_done, 1)
                for b in range(B):
                    dve.tensor_scalar(state_x[0:n, b, 2, :], state_h[0:n, b, 2, :], c["mom_last"][0:n, b, 0:1], rs[0:n, b:b + 1],
                                      ALU.subtract, ALU.mult)


PAIRS = BLOCKS // 2
RING = 3
AHEAD = 3
PARTS = {"T": 2, "K": 8, "V": 2, "Q": 8, "PV": 8, "WO": 1, "T2": 2, "F1": 8, "F2": 1}
THIS, NEXT, LAST = range(3)


def body_plan():
    after = [[] for _ in range(PAIRS)]

    def pieces(kind, g, who=THIS):
        return [(kind, g, p, who) for p in range(PARTS[kind])]

    def stats(g, who, second):
        return [("LN", g, second, who), ("N", g, second, who)]

    def add(g, who, second):
        return pieces("F2" if second else "WO", g, who) + [("X", g, second, who)]

    after[2] += pieces("Q", 1) + pieces("PV", 2, LAST)[:2]
    after[3] += pieces("PV", 2, LAST)[2:]
    after[4] += add(2, LAST, 0) + stats(2, LAST, 1)
    after[5] += pieces("V", 0) + pieces("T2", 2, LAST)
    after[6] += pieces("F1", 2, LAST)
    after[7] += add(2, LAST, 1) + pieces("PV", 0)
    after[8] += pieces("V", 2)
    after[9] += pieces("V", 1) + add(0, THIS, 0)
    after[10] += pieces("Q", 2) + stats(0, THIS, 1)
    after[11] += pieces("T2", 0) + pieces("F1", 0)
    after[12] += add(0, THIS, 1)
    after[13] += stats(0, NEXT, 0)
    after[14] += pieces("T", 0, NEXT) + pieces("PV", 1)
    after[15] += add(1, THIS, 0)
    after[16] += stats(1, THIS, 1)
    after[17] += pieces("T2", 1) + [("MK", 0, 0, NEXT)] + pieces("K", 0, NEXT) + pieces("Q", 0, NEXT)
    after[18] += [("PM", 0, 0, NEXT)] + pieces("F1", 1) + stats(1, NEXT, 0)
    after[19] += pieces("T", 1, NEXT) + add(1, THIS, 1) + stats(2, NEXT, 0)
    after[20] += pieces("T", 2, NEXT) + pieces("K", 1, NEXT) + pieces("K", 2, NEXT)
    return after


def attention_stage(nc, a, c, state_x):
    after = body_plan()
    opening = [x for x in sum(after, []) if x[3] == NEXT]
    ending = [x for x in sum(after, []) if x[3] == LAST]
    body = sum(after, [])

    def numbered(items, kinds):
        return {x: i for i, x in enumerate(x for x in items if x[0] in kinds)}

    place, place0, place9 = [numbered(x, PARTS) for x in (body, opening, ending)]
    ln_no, ln_no0, ln_no9 = [numbered(x, ("LN",)) for x in (body, opening, ending)]
    x_no, x_no9 = numbered(body, ("X",)), numbered(ending, ("X",))
    N_PIECES, N_LN, N_X = len(place), len(ln_no), len(x_no)
    PIECES0, LN0 = len(place0), len(ln_no0)
    assert N_PIECES % 2 == 0 and PIECES0 % 2 == 0 and PAIRS % RING == 0
    tails = [p for p in range(PAIRS) if block_width(2 * p) < 128 * (tile_of(2 * p) + 1)]
    with ExitStack() as ctx:
        sb = lambda n, s, d=F32: ctx.enter_context(nc.sbuf_tensor(n, s, d))
        ps = lambda n, s, d=F32: ctx.enter_context(nc.psum_tensor(n, s, d))
        sem = lambda n: ctx.enter_context(nc.semaphore(n))
        ident = c["ident"]
        wqkv = sb("wqkv", [128, 2, 3, 1024])
        wo = sb("wo", [128, 8, D])
        w1 = sb("w1", [128, 2, 1024])
        w2 = sb("w2", [128, 8, D])
        mem_v = sb("mem_v", [MEM, 1024])
        mem_k = sb("mem_k", [128, 2, 8, MEM])
        rows1 = sb("rows1", [1, 2, D])
        ones1 = sb("ones1", [1, 128])
        gb1 = sb("gb1", [128, 2, 2])
        gb2 = sb("gb2", [128, 2, 2])
        b1 = sb("b1", [128, 8])
        mixb = sb("mixb", [128, 2, 2, H])
        eye8 = sb("eye8", [128, ROWS])
        diag = sb("diag", [128, ROWS])
        mixes = sb("mixes", [128, 2, 2, H, ROWS])
        pre_mix = sb("pre_mix", [128, 128])
        post_mix = sb("post_mix", [128, 128])
        k_t = sb("k_t", [128, 8, KEYS])
        v = sb("v", [128, 3, 1024])
        q_bd = sb("q_bd", [128, 16, 8, 32])
        xn = sb("xn_a", [128, D])
        xn_t = sb("xn_t", [128, 2, MEM + 336])
        xn2_t = sb("xn2_t", [128, 2, 128])
        dots = sb("dots", [128, 2, KEYS])
        mixed = sb("mixed_a", [128, 2 * RING, KEYS])
        work = sb("work", [128, 2, KEYS])
        vals = sb("vals", [128, 2, 8, 8])
        nmax = sb("nmax", [128, 2])
        rsum = sb("rsum", [128, 2])
        rinv = sb("rinv", [128, 2 * RING])
        expd = sb("expd", [128, 2, KEYS])
        prob = sb("prob", [128, 2 * RING, 384])
        post = sb("post", [128, 2 * RING, 128])
        attn_t = sb("attn_t", [128, 4, H, 128])
        wide_t = sb("wide_t", [128, 8, 128])
        delta = sb("delta", [128, D])
        junk = sb("junk_a", [128, D])
        s1 = sb("s1", [128, 1])
        s2 = sb("s2", [128, 1])
        nmean = sb("nmean", [128, 1])
        var = sb("var", [128, 1])
        rstd = sb("rstd_a", [128, 1])
        nmr = sb("nmr", [128, 1])
        half, eps, minus, per, nper, carry_p, carry_a, carry_b = [sb(k, [128, 1]) for k in (
            "half_a", "eps_a", "minus_a", "per_a", "nper_a", "carry_p", "carry_a", "carry_b")]
        zeros = sb("zeros_a", [128, 384])
        p_dots = ps("p_dots", [128, 2, 512])
        p_mix = ps("p_mix", [128, 2, 512])
        p_post = ps("p_post", [128, 2, 512])
        p_any = ps("p_any", [128, 2, 512])
        w_a, w_b, s_c, s_set, s_mixes = sem("a_weights_a"), sem("a_weights_b"), sem("a_consts"), sem("a_set"), sem("a_mixes")
        dots_full, dots_out, mix_full, mix_out, max_ready, nmax_ready, exp_ready, prob_ready, post_scaled, post_full, attn_out = [
            sem("a_" + k) for k in ("dots_full", "dots_out", "mix_full", "mix_out", "max_ready", "nmax_ready", "exp_ready",
                                    "prob_ready", "post_scaled", "post_full", "attn_out")]
        tail_zero, premix_ready = sem("a_tail_zero"), sem("a_premix_ready")
        piece_full, piece_out, x_added = sem("a_piece_full"), sem("a_piece_out"), sem("a_x_added")
        s1_ready, mean_ready, s2_ready, rstd_ready, xn_ready = [sem("a_" + k) for k in ("s1", "mean", "s2", "rstd", "xn")]
        NA, NB = 5, 6

        def counts(it):
            return (it * PAIRS + AHEAD, it * N_PIECES + PIECES0, it * N_LN + LN0, it * N_X + 1)

        def out_count(mode, it, x):
            if mode == "opening":
                return place0[x] + 1
            return counts(it)[1] + (place if mode == "body" else place9)[x] + 1

        def pipeline(mode, engine, start, middle, item):
            if mode == "opening":
                for x in opening:
                    item(x)
                for s in range(-3, 0):
                    start(s)
            elif mode == "ending":
                for x in ending:
                    item(x)
            else:
                for s in range(PAIRS):
                    start(s)
                    if s:
                        middle(s - 1)
                    for x in after[s]:
                        item(x)
                middle(PAIRS - 1)

        def run(engine, program):
            program("opening", 0)
            with engine.Fori(0, 2 * B) as it:
                program("body", it)
            program("ending", 2 * B)

        def slots(engine, mode, it):
            if mode == "opening":
                return (1, 1, 1)
            if mode == "ending":
                return (1, 1, B)
            begun = (it + 15) // 16
            return (engine.snap(it % B + 1), engine.snap((it + 1) % B + 1), engine.snap(((it + 7) % B + 1) * begun))

        with nc.Block() as block:
            @block.sync
            def _(sp):
                for dst, src in ((eye8[:, :], a["eye8"]), (diag[:, :], a["diag"]), (ones1[:, :], a["ones"][:, 0:128]),
                                 (mem_k[:, :, :, :], a["mem_k"])):
                    sp.dma_start(dst, src).then_inc(s_c, 16)
                for l in range(2):
                    for j, name in enumerate(("pre", "post")):
                        m = a[name][l]
                        src = bass.AP(m.tensor, m.offset, [[H, H], [0, ROWS], [1, H]])
                        sp.dma_start(mixb[:, l, j, :], src).then_inc(s_c, 16)

                def load_a(l):
                    for dst, src in ((wqkv[:, :, 1, :], a["wk"][l].rearrange("(c p) n -> p c n", p=128)),
                                     (wqkv[:, :, 0, :], a["wq"][l].rearrange("(c p) n -> p c n", p=128)),
                                     (wqkv[:, :, 2, :], a["wv"][l].rearrange("(c p) n -> p c n", p=128)),
                                     (mem_v[:, :], a["mem_v"][l]), (gb1[:, :, :], a["gb"][l][:, :, 0:2])):
                        sp.dma_start(dst, src).then_inc(w_a, 16)

                def load_b(l):
                    for dst, src in ((wo[:, :, :], a["wo"][l].rearrange("(c p) n -> p c n", p=128)),
                                     (w1[:, :, :], a["w1"][l].rearrange("(c p) n -> p c n", p=128)),
                                     (w2[:, :, :], a["w2"][l].rearrange("(c p) n -> p c n", p=128)),
                                     (rows1[:, :, :], a["bo_b2"][l]), (gb2[:, :, :], a["gb"][l][:, :, 2:4]), (b1[:, :], a["b1"][l])):
                        sp.dma_start(dst, src).then_inc(w_b, 16)

                load_a(0)
                load_b(0)
                sp.wait_ge(piece_out, counts(B - 1)[1] + place[("Q", 2, 7, THIS)] + 1)
                load_a(1)
                sp.wait_ge(piece_out, counts(B)[1] + place[("F2", 2, 0, LAST)] + 1)
                load_b(1)

            @block.gpsimd
            def _(pool):
                for t, value in ((q_bd[:, :, :, :], 0.0), (xn_t[:, :, :], 0.0), (prob[:, :, :], 0.0), (half[:, :], -0.5),
                                 (eps[:, :], EPS), (minus[:, :], -1.0), (per[:, :], 1.0 / D), (nper[:, :], -1.0 / D),
                                 (zeros[:, :], 0.0), (attn_t[:, :, :, :], 0.0), (v[:, :, :], 0.0), (state_x[:, 0, :, :], 0.0)):
                    pool.memset(t, value)
                pool.sem_inc(nmax_ready, AHEAD)
                pool.sem_inc(x_added, 1)
                pool.drain().then_inc(s_set, 1)

                def program(mode, it):
                    pairs, _, lns, xs = [pool.snap(q) if mode == "body" else q for q in counts(it)]
                    nt = pool.snap(it * len(tails)) if mode == "body" else 0
                    slot = slots(pool, mode, it)
                    lno, xno = (ln_no0, {}) if mode == "opening" else (ln_no9, x_no9) if mode == "ending" else (ln_no, x_no)
                    if mode == "opening":
                        lns = 0

                    def start(p):
                        if p < 0:
                            return
                        pool.wait_ge(max_ready, pairs + p + 1)
                        pool.tensor_tensor(nmax[:, :], vals[:, :, 0, 0], minus[:, 0:1].broadcast_to([128, 2]), ALU.mult).then_inc(nmax_ready, 1)
                        if p in tails:
                            pool.wait_ge(post_full, pairs + p - RING + 1)
                            for n in (2 * p, 2 * p + 1):
                                w, end = block_width(n), 128 * (tile_of(n) + 1)
                                if w < end:
                                    pool.tensor_tensor(prob[:, n % (2 * RING), w:end], zeros[:, w:end], zeros[:, w:end], ALU.mult)
                            pool.drain().then_inc(tail_zero, 1)

                    def item(x):
                        kind, g, p, who = x
                        n = TILE_N[g]
                        if kind == "X":
                            pool.wait_ge(piece_out, out_count(mode, it, ("F2" if p else "WO", g, 0, who)))
                            pool.tensor_tensor(carry_p[:, :], minus[:, :], minus[:, :], ALU.mult)
                            h = state_x[0:n, slot[who], g, :]
                            pool.tensor_tensor(h, h, delta[0:n, :], ALU.add)
                            pool.drain().then_inc(x_added, 1)
                        elif kind == "LN":
                            k = lno[x] + 1
                            pool.wait_ge(s1_ready, lns + k)
                            pool.tensor_tensor(nmean[0:n, :], s1[0:n, :], nper[0:n, :], ALU.mult).then_inc(mean_ready, 1)
                            pool.wait_ge(s2_ready, lns + k)
                            pool.tensor_tensor(var[0:n, :], s2[0:n, :], per[0:n, :], ALU.mult)
                            pool.drain()
                            pool.tensor_tensor(rstd[0:n, :], var[0:n, :], eps[0:n, :], ALU.add)
                            pool.drain()
                            pool.tensor_tensor(var[0:n, :], rstd[0:n, :], half[0:n, :], ALU.pow)
                            pool.drain()
                            pool.tensor_copy(rstd[0:n, :], var[0:n, :])
                            pool.tensor_tensor(nmr[0:n, :], var[0:n, :], nmean[0:n, :], ALU.mult)
                            pool.drain().then_inc(rstd_ready, 1)

                    pipeline(mode, pool, start, lambda p: None, item)

                run(pool, program)

            @block.tensor
            def _(pe):
                pe.sem_inc(dots_full, AHEAD)
                pe.sem_inc(mix_full, AHEAD)
                pe.sem_inc(post_full, AHEAD)
                pe.wait_ge(s_c, 16 * 8)
                pe.wait_ge(s_set, 1)

                def program(mode, it):
                    pairs, first, lns, _ = [pe.snap(q) if mode == "body" else q for q in counts(it)]
                    where, lno = (place0, ln_no0) if mode == "opening" else (place9, ln_no9) if mode == "ending" else (place, ln_no)
                    if mode == "opening":
                        first, lns = 0, 0
                        pe.wait_ge(w_a, 16 * NA)
                    if mode == "body":
                        layer_next = pe.snap((it + 9) // 16)

                    def out(x):
                        pe.wait_ge(piece_out, first + where[x] + 1)

                    def start(s):
                        p = s + 2
                        if p >= 0:
                            pe.wait_ge(dots_out, pairs + p + 1)
                            pe.wait_ge(mix_out, pairs + p)
                            if p % PAIRS == 0:
                                pe.wait_ge(premix_ready, it + 1 if mode == "opening" else it + 2)
                            for n in (2 * p, 2 * p + 1):
                                w = block_width(n % BLOCKS)
                                last = pe.matmul(p_mix[:, n % 2, 0:w], pre_mix[:, :], dots[:, n % 2, 0:w], start=True, stop=True)
                            last.then_inc(mix_full, 1)
                        p = s + 3
                        pe.wait_ge(dots_out, pairs + p)
                        if mode == "opening" and p == 0:
                            out(("Q", 0, 7, NEXT))
                        if mode == "body" and p == PAIRS:
                            out(("Q", 0, 7, NEXT))
                        if mode == "body" and 2 * p in GROUP0[1:3]:
                            out(("Q", tile_of(2 * p), 7, THIS))
                        for n in (2 * p, 2 * p + 1):
                            nn = n % BLOCKS
                            g, w = tile_of(nn), block_width(nn)
                            for j in range(2):
                                for q in range(4):
                                    last = pe.matmul(p_dots[32 * q:32 * q + 32, n % 2, 0:w], q_bd[:, nn - GROUP0[g], 2 * q + j, :],
                                                     k_t[:, 2 * q + j, 0:w], start=(j == 0), stop=(j == 1))
                        last.then_inc(dots_full, 1)

                    def middle(p):
                        pe.wait_ge(post_scaled, pairs + p + 1)
                        pe.wait_ge(attn_out, pairs + p)
                        for n in (2 * p, 2 * p + 1):
                            for j in range(tile_of(n) + 1):
                                last = pe.matmul(p_post[:, n % 2, 128 * j:128 * j + 128], prob[:, n % (2 * RING), 128 * j:128 * j + 128],
                                                 post[:, n % (2 * RING), :], start=(j == 0), stop=True, skip_group_check=True)
                        last.then_inc(post_full, 1)

                    def item(x):
                        kind, g, p, who = x
                        if kind not in PARTS:
                            return
                        k = where[x]
                        n, t0 = TILE_N[g], TILE0[g]
                        bank = p_any[:, k % 2, :]
                        if mode != "opening" or k >= 2:
                            pe.wait_ge(piece_out, first + k - 1)
                        if kind in ("T", "T2"):
                            if p == 0:
                                if who == NEXT and mode == "body":
                                    pe.wait_ge(w_a, layer_next * (16 * NA) + 16 * NA)
                                pe.wait_ge(xn_ready, lns + lno[("LN", g, 0 if kind == "T" else 1, who)] + 1)
                            last = pe.transpose(bank[:, 0:n], xn[0:n, 128 * p:128 * p + 128], ident[0:n, 0:n])
                        elif kind == "K":
                            if p == 0:
                                out(("T", g, 1, who))
                            for j in range(2):
                                last = pe.matmul(bank[:, 0:n], wqkv[:, j, 1, 128 * p:128 * p + 128], xn_t[:, j, MEM + t0:MEM + t0 + n],
                                                 start=(j == 0), stop=(j == 1))
                        elif kind == "V":
                            m = 128 if g < 2 else n
                            for j in range(2):
                                last = pe.matmul(bank[0:m, :], xn_t[:, j, 128 * g:128 * g + m], wqkv[:, j, 2, 512 * p:512 * p + 512],
                                                 start=(j == 0), stop=(j == 1 and g > 0))
                            if g == 0:
                                last = pe.matmul(bank[0:m, :], ident[0:MEM, 0:128], mem_v[:, 512 * p:512 * p + 512], start=False, stop=True)
                        elif kind == "Q":
                            m = 8 * (-(-n // 8))
                            for j in range(2):
                                last = pe.matmul(bank[:, 0:m], wqkv[:, j, 0, 128 * p:128 * p + 128], xn_t[:, j, MEM + t0:MEM + t0 + m],
                                                 start=(j == 0), stop=(j == 1))
                        elif kind == "PV":
                            if p == 0 and who == LAST:
                                pe.wait_ge(attn_out, pairs)
                            elif p == 0:
                                pe.wait_ge(attn_out, pairs + GROUP0[g + 1] // 2)
                                out(("V", g, 1, who))
                            for j in range(g + 1):
                                r = 128 if j < 2 else TILE_N[2]
                                for hh in range(2):
                                    h = 2 * p + hh
                                    last = pe.matmul(bank[64 * hh:64 * hh + 64, 0:n], v[0:r, j, 64 * h:64 * h + 64], attn_t[0:r, j if g else 3, h, 0:n],
                                                     start=(j == 0), stop=(j == g))
                        elif kind in ("WO", "F2"):
                            if kind == "WO":
                                src, w, r = wide_t, wo, 0
                                out(("PV", g, 7, who))
                                if mode == "body" and who == THIS and g == 0:
                                    pe.wait_ge(w_b, (it // B) * (16 * NB) + 16 * NB)
                                if who == LAST:
                                    pe.wait_ge(w_b, 16 * NB)
                            else:
                                src, w, r = wide_t, w2, 1
                                out(("F1", g, 7, who))
                            for j in range(8):
                                pe.matmul(bank[0:n, 0:D], src[:, j, 0:n], w[:, j, :], start=(j == 0), stop=False)
                            last = pe.matmul(bank[0:n, 0:D], ones1[0:1, 0:n], rows1[0:1, r, :], start=False, stop=True)
                        elif kind == "F1":
                            if p == 0:
                                out(("T2", g, 1, who))
                            for j in range(2):
                                last = pe.matmul(bank[:, 0:n], w1[:, j, 128 * p:128 * p + 128], xn2_t[:, j, 0:n], start=(j == 0), stop=(j == 1))
                        last.then_inc(piece_full, 1)

                    pipeline(mode, pe, start, middle, item)

                run(pe, program)

            @block.scalar
            def _(act):
                for q in (dots_out, mix_out, exp_ready, post_scaled, attn_out):
                    act.sem_inc(q, AHEAD)
                act.wait_ge(s_set, 1)
                act.wait_ge(s_mixes, 1)

                def program(mode, it):
                    pairs, first, lns, xs = [act.snap(q) if mode == "body" else q for q in counts(it)]
                    where, lno = (place0, ln_no0) if mode == "opening" else (place9, ln_no9) if mode == "ending" else (place, ln_no)
                    slot = slots(act, mode, it)
                    added = [0]
                    if mode == "opening":
                        first, lns, xs = 0, 0, 0
                    next_layer = act.snap(((it + 1) // B) % 2) if mode == "body" else 0
                    if mode == "body":
                        act.activation(post_mix[:, :], mixes[:, act.snap(it // B), 1, :, :].rearrange("p k i -> p (k i)"), ACT.Copy)

                    def start(s):
                        p = s
                        if p >= 0:
                            act.wait_ge(nmax_ready, pairs + p + 1)
                            for n in (2 * p, 2 * p + 1):
                                w = block_width(n)
                                last = act.activation(expd[:, n % 2, 0:w], mixed[:, n % (2 * RING), 0:w], ACT.Exp, bias=nmax[:, n % 2:n % 2 + 1])
                            last.then_inc(exp_ready, 1)
                        p = s + 2
                        if p >= 0:
                            act.wait_ge(mix_full, pairs + p + 1)
                            act.wait_ge(prob_ready, pairs + p - RING + 1)
                            for n in (2 * p, 2 * p + 1):
                                w = block_width(n % BLOCKS)
                                last = act.activation(mixed[:, n % (2 * RING), 0:w], p_mix[:, n % 2, 0:w], ACT.Copy)
                            last.then_inc(mix_out, 1)
                        p = s + 3
                        act.wait_ge(dots_full, pairs + p + 1)
                        for n in (2 * p, 2 * p + 1):
                            w = block_width(n % BLOCKS)
                            last = act.activation(dots[:, n % 2, 0:w], p_dots[:, n % 2, 0:w], ACT.Copy, scale=DH ** -0.5)
                        last.then_inc(dots_out, 1)

                    def middle(p):
                        g = tile_of(2 * p)
                        act.wait_ge(prob_ready, pairs + p + 1)
                        for n in (2 * p, 2 * p + 1):
                            last = act.activation(post[:, n % (2 * RING), :], post_mix[:, :], ACT.Copy, scale=rinv[:, n % (2 * RING):n % (2 * RING) + 1])
                        last.then_inc(post_scaled, 1)
                        act.wait_ge(post_full, pairs + p + 1)
                        for n in (2 * p, 2 * p + 1):
                            i0 = ROWS * (n - GROUP0[g])
                            last = act.activation(attn_t[:, 0:g + 1, :, i0:i0 + ROWS] if g else attn_t[:, 3:4, :, i0:i0 + ROWS],
                                                  p_post[:, n % 2, 0:128 * (g + 1)].rearrange("p (j k i) -> p j k i", j=g + 1, k=H), ACT.Copy)
                        last.then_inc(attn_out, 1)

                    def item(x):
                        kind, g, p, who = x
                        n, t0 = TILE_N[g], TILE0[g]
                        rows = state_x[0:n, slot[who], g, :]
                        if kind == "MK":
                            if mode == "body":
                                act.wait_ge(dots_full, pairs + PAIRS)
                            act.activation(carry_a[:, :], minus[:, :], ACT.Copy)
                            act.activation(k_t[:, :, 0:MEM], mem_k[:, next_layer, :, :], ACT.Copy)
                            return
                        if kind == "PM":
                            if mode == "body":
                                act.wait_ge(mix_full, pairs + PAIRS)
                            act.activation(carry_b[:, :], minus[:, :], ACT.Copy)
                            act.activation(pre_mix[:, :], mixes[:, next_layer, 0, :, :].rearrange("p k i -> p (k i)"), ACT.Copy).then_inc(premix_ready, 1)
                            return
                        if kind == "X":
                            added[0] += 1
                            return
                        if kind == "LN":
                            if mode != "opening":
                                act.wait_ge(x_added, xs + added[0])
                            act.activation(carry_a[:, :], minus[:, :], ACT.Copy)
                            act.activation(junk[0:n, :], rows, ACT.Copy, accum_out=s1[0:n, :])
                            act.drain().then_inc(s1_ready, 1)
                            act.wait_ge(mean_ready, lns + lno[x] + 1)
                            act.activation(carry_a[:, :], minus[:, :], ACT.Copy)
                            act.activation(junk[0:n, :], rows, ACT.Square, bias=nmean[0:n, :], accum_out=s2[0:n, :])
                            act.drain().then_inc(s2_ready, 1)
                            return
                        if kind == "N":
                            act.wait_ge(rstd_ready, lns + lno[("LN",) + x[1:]] + 1)
                            act.activation(carry_a[:, :], minus[:, :], ACT.Copy)
                            act.activation(xn[0:n, :], rows, ACT.Identity, scale=rstd[0:n, :], bias=nmr[0:n, :]).then_inc(xn_ready, 1)
                            return
                        bank = p_any[:, where[x] % 2, :]
                        act.wait_ge(piece_full, first + where[x] + 1)
                        if kind == "T":
                            last = act.activation(xn_t[:, p, MEM + t0:MEM + t0 + n], bank[:, 0:n], ACT.Identity,
                                                  scale=gb1[:, p, 0:1], bias=gb1[:, p, 1:2])
                        elif kind == "T2":
                            last = act.activation(xn2_t[:, p, 0:n], bank[:, 0:n], ACT.Identity, scale=gb2[:, p, 0:1], bias=gb2[:, p, 1:2])
                        elif kind == "K":
                            last = act.activation(k_t[:, p, MEM + t0:MEM + t0 + n], bank[:, 0:n], ACT.Copy)
                        elif kind == "V":
                            m = 128 if g < 2 else n
                            last = act.activation(v[0:m, g, 512 * p:512 * p + 512], bank[0:m, :], ACT.Copy)
                        elif kind == "Q":
                            nbk = -(-n // 8)
                            for hh in range(2):
                                h4 = 2 * (p % 2) + hh
                                last = act.activation(q_bd[64 * hh:64 * hh + 64, 0:nbk, p, 8 * h4:8 * h4 + 8],
                                                      bank[64 * hh:64 * hh + 64, 0:8 * nbk].rearrange("p (b i) -> p b i", i=8), ACT.Copy)
                        elif kind == "PV":
                            last = act.activation(wide_t[:, p, 0:n], bank[:, 0:n], ACT.Copy)
                        elif kind == "F1":
                            last = act.activation(wide_t[:, p, 0:n], bank[:, 0:n], ACT.Gelu, bias=b1[:, p:p + 1])
                        else:
                            act.wait_ge(x_added, xs + added[0])
                            last = act.activation(delta[0:n, :], bank[0:n, 0:D], ACT.Copy)
                        last.then_inc(piece_out, 1)

                    pipeline(mode, act, start, middle, item)

                run(act, program)

            @block.vector
            def _(dve):
                for q in (max_ready, prob_ready):
                    dve.sem_inc(q, AHEAD)
                dve.wait_ge(s_c, 16 * 8)
                for l in range(2):
                    for j in range(2):
                        dve.tensor_tensor(mixes[:, l, j, :, :], mixb[:, l, j, :].unsqueeze(2).broadcast_to([128, H, ROWS]),
                                          eye8[:, :].unsqueeze(1).broadcast_to([128, H, ROWS]), ALU.mult)
                dve.drain().then_inc(s_mixes, 1)

                def program(mode, it):
                    if mode != "body":
                        return
                    pairs = dve.snap(counts(it)[0])
                    nt = dve.snap(it * len(tails))

                    def start(p):
                        both = [(n, n % 2, block_width(n), mixed[:, n % (2 * RING), :]) for n in (2 * p, 2 * p + 1)]
                        dve.wait_ge(mix_out, pairs + p + 1)
                        for n, u, w, m in both:
                            d0 = MEM + ROWS * n
                            dve.tensor_tensor(m[:, d0:w], m[:, d0:w], diag[:, 0:w - d0], ALU.min)
                        dve.drain()
                        for n, u, w, m in both:
                            dve.max(vals[:, u, 0, :], m[:, 0:w])
                        dve.drain().then_inc(max_ready, 1)
                        select = 2 * p >= FULL_ROWS
                        if select:
                            for r in range(1, 8):
                                for n, u, w, m in both:
                                    dve.match_replace(work[:, u, 0:w], vals[:, u, r - 1, :], m[:, 0:w] if r == 1 else work[:, u, 0:w], -BIG)
                                dve.drain()
                                for n, u, w, m in both:
                                    dve.max(vals[:, u, r, :], work[:, u, 0:w])
                                dve.drain()
                        dve.wait_ge(exp_ready, pairs + p + 1)
                        if p in tails:
                            dve.wait_ge(tail_zero, nt + tails.index(p) + 1)
                        for n, u, w, m in both:
                            dve.scalar_tensor_tensor(prob[:, n % (2 * RING), 0:w], m[:, 0:w], vals[:, u, 7, 7:8] if select else -BIG,
                                                     expd[:, u, 0:w], ALU.is_ge, ALU.mult, accum_out=rsum[:, u:u + 1])
                        dve.drain()
                        r0 = (2 * p) % (2 * RING)
                        dve.reciprocal(rinv[:, r0:r0 + 2], rsum[:, :]).then_inc(prob_ready, 1)

                    pipeline(mode, dve, start, lambda p: None, lambda x: None)

                run(dve, program)


def router_stage(nc, a, c, state_h, state_x, m):
    with ExitStack() as ctx:
        sb = lambda n, s, d=F32: ctx.enter_context(nc.sbuf_tensor(n, s, d))
        ps = lambda n, s, d=F32: ctx.enter_context(nc.psum_tensor(n, s, d))
        sem = lambda n: ctx.enter_context(nc.semaphore(n))
        ident = c["ident"]
        gate = sb("gate", [128, 2, EXPERTS])
        sg = sb("sg", [128, 2, HID])
        su = sb("su", [128, 2, HID])
        sd = sb("sd", [128, 4, D])
        tri = sb("tri", [128, 128])
        ones_c = sb("ones_c", [128, 1])
        ones_r = sb("ones_r", [1, 128])
        iota_e = sb("iota_e", [128, EXPERTS])
        iota_p = sb("iota_p", [128, 1])
        zero = sb("zero", [128, D])
        run = sb("run", [1, EXPERTS])
        xn = sb("xn_m", [128, D])
        x_t = sb("x_t", [128, 2, 128])
        sl = sb("sl", [128, 4, 128])
        hid = sb("hid", [128, 4, 128])
        top = sb("top", [128, 8])
        top_i = sb("top_i", [128, 8], U32)
        top_f = sb("top_f", [128, 1])
        e_s = sb("e_s", [128, 1])
        d_s = sb("d_s", [128, 1])
        score = sb("score", [128, 1])
        junk = sb("junk", [128, EXPERTS])
        stats = sb("stats_m", [128, 6])
        mom = sb("mom_m", [128, 2])
        rstd = sb("rstd_m", [128, 1])
        half = sb("half_m", [128, 1])
        eps = sb("eps_m", [128, 1])
        onehot = sb("onehot", [128, B * 3, EXPERTS])
        spread = sb("spread", [128, B * 3, EXPERTS])
        rank = sb("rank", [128, B * 3])
        slot_f = sb("slot_f", [128, B * 3])
        tiles_i = sb("tiles_i", [1, EXPERTS], I32)
        tiles_s = sb("tiles_s", [1, EXPERTS], I32)
        tiles_f = sb("tiles_f", [1, EXPERTS])
        ones_e = sb("ones_e", [1, EXPERTS])
        bounds = sb("bounds", [1, 2, EXPERTS])
        before = sb("before", [128, EXPERTS])
        e_col = sb("e_col", [128, 1])
        p_t = ps("pm_t", [128, 4, 128])[:, 0:2, :]
        p_g = ps("pm_g", [128, 4, 128])
        p_u = ps("pm_u", [128, 4, 128])
        p_y = ps("pm_y", [128, 512])[:, 0:D]
        p_l = ps("pm_l", [128, 512])[:, 0:EXPERTS]
        p_r = ps("pm_r", [128, 512])[:, 0:EXPERTS]
        p_l2 = p_t[:, 0, :]
        hot_now = sb("hot_now", [128, EXPERTS])
        logits = sb("logits", [128, EXPERTS])
        p_c = ps("pm_c", [128, 512])[:, 0:EXPERTS]
        p_b = ps("pm_b", [128, 8, 64])[:, 0, :].rearrange("p (j e) -> p j e", j=2)
        loaded, zeroed, ready = sem("m_loaded"), sem("m_zeroed"), sem("m_ready")
        mom_ready, rstd_ready, xn_ready = sem("m_mom"), sem("m_rstd"), sem("m_xn")
        t_full, t_out, l_full, g_full, s_out = sem("m_t_full"), sem("m_t_out"), sem("m_l_full"), sem("m_g_full"), sem("m_silu")
        hid_ready, y_full, top_ready, exp_ready = sem("m_hid"), sem("m_y_full"), sem("m_top"), sem("m_exp")
        hot_ready, r_full, tile_done = sem("m_hot"), sem("m_r_full"), sem("m_tile_done")
        bound_ready, bound_full, col_ready, row_full, slots_ready = (sem("m_bound"), sem("m_bound_full"), sem("m_col"),
                                                                     sem("m_row_full"), sem("m_slots"))
        scattered = sem("m_scattered")
        NL = 9
        ZC = 4
        with nc.Block() as block:
            @block.sync
            def _(sp):
                for dst, src in ((gate[:, :, :], a["gate_w"].rearrange("(c p) n -> p c n", p=128)),
                                 (sg[:, :, :], a["sg"].rearrange("(c p) n -> p c n", p=128)),
                                 (su[:, :, :], a["su"].rearrange("(c p) n -> p c n", p=128)),
                                 (sd[:, :, :], a["sd"].rearrange("(c p) n -> p c n", p=128)),
                                 (tri[:, :], a["tri"]), (iota_e[:, :], a["iota_e"]), (iota_p[:, :], a["iota_p"]),
                                 (ones_r[:, :], a["ones"][:, 0:128]), (ones_c[:, :], a["ones_c"])):
                    sp.dma_start(dst, src).then_inc(loaded, 16)
                sp.wait_ge(ready, 1)
                for k in range(ZC):
                    n = SLOT_TILES // ZC
                    sp.dma_start(m["xs"][128 * n * k:128 * n * (k + 1), :].rearrange("(t p) n -> p t n", p=128),
                                 zero[:, :].unsqueeze(1).broadcast_to([128, n, D])).then_inc(zeroed, 16)
                sp.wait_ge(zeroed, 16 * ZC)

            @block.gpsimd
            def _(pool):
                pool.memset(half[:, :], -0.5)
                pool.memset(eps[:, :], EPS)
                pool.memset(zero[:, :], 0.0)
                pool.memset(run[:, :], 0.0)
                pool.memset(ones_e[:, :], 1.0)
                pool.memset(onehot[:, :, :], 0.0)
                pool.memset(rank[:, :], 0.0)
                pool.drain().then_inc(ready, 1)
                with pool.Fori(0, B) as b:
                    t0 = pool.snap(b * 3)
                    for g in range(3):
                        n = TILE_N[g]
                        pool.wait_ge(mom_ready, t0 + g + 1)
                        pool.tensor_tensor(rstd[0:n, :], mom[0:n, 1:2], eps[0:n, :], ALU.add)
                        pool.drain()
                        pool.tensor_tensor(rstd[0:n, :], rstd[0:n, :], half[0:n, :], ALU.pow).then_inc(rstd_ready, 1)
                pool.wait_ge(slots_ready, 1)
                pool.wait_ge(zeroed, 16 * ZC)
                for b in range(B):
                    for g in range(3):
                        n, t = TILE_N[g], 3 * b + g
                        pool.indirect_dma_start(m["xs"], bass.IndirectOffsetOnAxis(ap=m["slot"][0:n, t:t + 1], axis=0),
                                                state_x[0:n, b, g, :], None).then_inc(scattered, 16)
                pool.wait_ge(scattered, 16 * 3 * B)

            @block.tensor
            def _(pe):
                pe.wait_ge(loaded, 16 * NL)
                pe.wait_ge(ready, 1)
                with pe.Fori(0, B) as b:
                    t0 = pe.snap(b * 3)
                    for g in range(3):
                        n, t = TILE_N[g], t0 + g
                        pe.wait_ge(xn_ready, t + 1)
                        for j in range(2):
                            last = pe.transpose(p_t[:, j, 0:n], xn[0:n, 128 * j:128 * j + 128], ident[0:n, 0:n])
                        last.then_inc(t_full, 1)
                        pe.wait_ge(t_out, t + 1)
                        for j in range(2):
                            last = pe.matmul(p_l[0:n, :], x_t[:, j, 0:n], gate[:, j, :], start=(j == 0), stop=(j == 1))
                        last.then_inc(l_full, 1)
                        for p, w in ((p_g, sg), (p_u, su)):
                            for q in range(4):
                                for j in range(2):
                                    last = pe.matmul(p[:, q, 0:n], w[:, j, 128 * q:128 * q + 128], x_t[:, j, 0:n],
                                                     start=(j == 0 and q == 0), stop=(j == 1), skip_group_check=True)
                        last.then_inc(g_full, 1)
                        pe.wait_ge(hot_ready, t + 1)
                        hot = hot_now[0:n, :]
                        pe.matmul(p_r[0:n, :], tri[0:n, 0:n], hot, start=True, stop=False)
                        pe.matmul(p_r[0:n, :], ones_r[0:1, 0:n], run[0:1, :], start=False, stop=True)
                        pe.matmul(p_c[0:1, :], ones_c[0:n, 0:1], hot, start=True, stop=True).then_inc(r_full, 1)
                        pe.wait_ge(hid_ready, t + 1)
                        for q in range(4):
                            last = pe.matmul(p_y[0:n, :], hid[:, q, 0:n], sd[:, q, :], start=(q == 0), stop=(q == 3))
                        last.then_inc(y_full, 1)
                pe.wait_ge(bound_ready, 1)
                pe.matmul(p_b[:, :, :], ones_r[0:1, :], bounds[0:1, :, :], start=True, stop=True).then_inc(bound_full, 1)
                pe.wait_ge(col_ready, 1)
                pe.matmul(p_l2[0:1, 0:SLOT_TILES], e_col[0:SLOT_TILES, :],
                          ident[0:SLOT_TILES, 0:SLOT_TILES], start=True, stop=True).then_inc(row_full, 1)

            @block.scalar
            def _(act):
                with act.Fori(0, B) as b:
                    t0 = act.snap(b * 3)
                    for g in range(3):
                        n, t = TILE_N[g], t0 + g
                        act.wait_ge(t_full, t + 1)
                        act.activation(x_t[:, :, 0:n], p_t[:, :, 0:n], ACT.Copy).then_inc(t_out, 1)
                        act.wait_ge(top_ready, t + 1)
                        act.activation(e_s[0:n, :], top[0:n, 0:1], ACT.Exp, scale=-1.0).then_inc(exp_ready, 1)
                        act.wait_ge(g_full, t + 1)
                        act.activation(sl[:, :, 0:n], p_g[:, :, 0:n], ACT.Silu).then_inc(s_out, 1)

            @block.vector
            def _(dve):
                dve.wait_ge(loaded, 16 * NL)
                dve.wait_ge(ready, 1)
                with dve.Fori(0, B) as b:
                    t0 = dve.snap(b * 3)
                    for g in range(3):
                        n, t = TILE_N[g], t0 + g
                        h, x = state_h[0:n, b, g, :], state_x[0:n, b, g, :]
                        dve.tensor_tensor(h, h, x, ALU.add)
                        dve.drain()
                        layer_norm_stats(dve, stats[0:n, :], mom[0:n, :], h).then_inc(mom_ready, 1)
                        dve.wait_ge(rstd_ready, t + 1)
                        dve.tensor_scalar(xn[0:n, :], h, mom[0:n, 0:1], rstd[0:n, :], ALU.subtract, ALU.mult).then_inc(xn_ready, 1)
                        dve.wait_ge(l_full, t + 1)
                        dve.tensor_copy(logits[0:n, :], p_l[0:n, :])
                        dve.drain()
                        dve.max(top[0:n, :], logits[0:n, :])
                        dve.drain()
                        dve.max_index(top_i[0:n, :], top[0:n, :], logits[0:n, :]).then_inc(top_ready, 1)
                        dve.drain()
                        dve.tensor_copy(top_f[0:n, :], top_i[0:n, 0:1])
                        dve.drain()
                        dve.tensor_scalar(hot_now[0:n, :], iota_e[0:n, :], top_f[0:n, :], None, ALU.is_equal).then_inc(hot_ready, 1)
                        dve.drain()
                        dve.tensor_copy(onehot[0:n, t, :], hot_now[0:n, :])
                        dve.wait_ge(exp_ready, t + 1)
                        dve.tensor_scalar(d_s[0:n, :], e_s[0:n, :], 1.0, None, ALU.add)
                        dve.drain()
                        dve.reciprocal(score[0:n, :], d_s[0:n, :])
                        dve.drain()
                        dve.tensor_scalar(x, xn[0:n, :], score[0:n, :], None, ALU.mult)
                        dve.wait_ge(s_out, t + 1)
                        dve.tensor_tensor(hid[:, :, 0:n], sl[:, :, 0:n], p_u[:, :, 0:n], ALU.mult).then_inc(hid_ready, 1)
                        dve.wait_ge(r_full, t + 1)
                        dve.tensor_tensor(junk[0:n, :], hot_now[0:n, :], p_r[0:n, :], ALU.mult)
                        dve.tensor_tensor(run[:, :], run[:, :], p_c[0:1, :], ALU.add)
                        dve.drain()
                        dve.tensor_reduce(rank[0:n, bass.ds(t, 1)], junk[0:n, :], AX.X, ALU.add)
                        dve.wait_ge(y_full, t + 1)
                        dve.tensor_tensor(h, h, p_y[0:n, :], ALU.add)
                        dve.drain()
                dve.tensor_scalar(tiles_i[:, :], run[:, :], 127.0, None, ALU.add)
                dve.drain()
                dve.tensor_scalar(tiles_s[:, :], tiles_i[:, :], 7, None, ALU.arith_shift_right)
                dve.drain()
                dve.tensor_copy(tiles_f[:, :], tiles_s[:, :])
                dve.drain()
                dve.tensor_tensor_scan(bounds[:, 0, :], ones_e[:, :], tiles_f[:, :], 0.0, ALU.mult, ALU.add)
                dve.drain()
                dve.tensor_tensor(junk[0:1, :], bounds[:, 0, :], tiles_f[:, :], ALU.subtract)
                dve.drain()
                dve.tensor_scalar(bounds[:, 1, :], junk[0:1, :], 128.0, None, ALU.mult).then_inc(bound_ready, 1)
                dve.wait_ge(bound_full, 1)
                dve.tensor_tensor(spread[:, :, :], onehot[:, :, :], p_b[:, 1, :].unsqueeze(1).broadcast_to([128, 3 * B, EXPERTS]), ALU.mult)
                dve.tensor_scalar(before[:, :], p_b[:, 0, :], iota_p[:, 0:1], None, ALU.is_le)
                dve.drain()
                dve.tensor_reduce(slot_f[:, :], spread[:, :, :], AX.X, ALU.add)
                dve.tensor_reduce(e_col[:, :], before[:, :], AX.X, ALU.add)
                dve.drain()
                dve.tensor_scalar(e_col[:, :], e_col[:, :], EXPERTS - 1.0, None, ALU.min).then_inc(col_ready, 1)
                dve.tensor_tensor(m["slot"][:, :], slot_f[:, :], rank[:, :], ALU.add).then_inc(slots_ready, 1)
                dve.wait_ge(row_full, 1)
                dve.tensor_copy(m["experts"][:, :], p_l2[0:1, 0:SLOT_TILES])


def experts_stage(nc, a, c, m):
    with ExitStack() as ctx:
        sb = lambda n, s, d=F32: ctx.enter_context(nc.sbuf_tensor(n, s, d))
        ps = lambda n, s, d=F32: ctx.enter_context(nc.psum_tensor(n, s, d))
        sem = lambda n: ctx.enter_context(nc.semaphore(n))
        ident = c["ident"]
        wg = sb("wg", [128, 2, 2, HID])
        wu = sb("wu", [128, 2, 2, HID])
        wd = sb("wd", [128, 2, 4, D])
        xs = sb("xs_sb", [128, 2, D])
        x_t = sb("xs_t", [128, 2, 2, 128])
        sl = sb("sl_e", [128, 2, 4, 128])
        hid = sb("hid_e", [128, 2, 4, 128])
        y = sb("y_e", [128, 2, D])
        p_t = ps("pe_t", [128, 1, 4, 128])
        p_g = ps("pe_g", [128, 2, 4, 128])
        p_u = ps("pe_u", [128, 2, 4, 128])
        p_y = ps("pe_y", [128, 2, 512])
        in_x, in_w = [sem("e_in_x0"), sem("e_in_x1")], [sem("e_in_w0"), sem("e_in_w1")]
        t_full, t_out, g_full, s_out, hid_ready, y_full, y_out = [sem("e_" + k) for k in (
            "t_full", "t_out", "g_full", "silu", "hid", "y_full", "y_out")]
        stored = [sem("e_stored0"), sem("e_stored1")]
        with nc.Block() as block:
            @block.sync
            def _(sp):
                with sp.Fori(0, SLOT_TILES // 2) as i:
                    for u in range(2):
                        t = i * 2 + u
                        e = sp.value_load(m["experts"][0:1, bass.ds(t, 1)], min_val=0, max_val=EXPERTS - 1)
                        sp.wait_ge(y_full, t + 1)
                        sp.dma_start(xs[:, u, :], m["xs"].rearrange("(t p) n -> t p n", p=128)[t]).then_inc(in_x[u], 16)
                        sp.dma_start(wg[:, u, :, :], a["rg"][e].rearrange("(c p) n -> p c n", p=128)).then_inc(in_w[u], 16)
                        sp.dma_start(wu[:, u, :, :], a["ru"][e].rearrange("(c p) n -> p c n", p=128)).then_inc(in_w[u], 16)
                        sp.dma_start(wd[:, u, :, :], a["rd"][e].rearrange("(c p) n -> p c n", p=128)).then_inc(in_w[u], 16)

            @block.tensor
            def _(pe):
                pe.sem_inc(y_full, 2)
                with pe.Fori(0, SLOT_TILES // 2) as i:
                    for u in range(2):
                        t = i * 2 + u
                        pe.wait_ge(in_x[u], i * 16 + 16)
                        for j in range(2):
                            last = pe.transpose(p_t[:, 0, j, :], xs[:, u, 128 * j:128 * j + 128], ident[:, :])
                        last.then_inc(t_full, 1)
                        pe.wait_ge(in_w[u], i * 48 + 48)
                        pe.wait_ge(t_out, t + 1)
                        for p, w in ((p_g, wg), (p_u, wu)):
                            for q in range(4):
                                for j in range(2):
                                    last = pe.matmul(p[:, u, q, :], w[:, u, j, 128 * q:128 * q + 128], x_t[:, u, j, :],
                                                     start=(j == 0 and q == 0), stop=(j == 1), skip_group_check=True)
                        last.then_inc(g_full, 1)
                        pe.wait_ge(hid_ready, t + 1)
                        pe.wait_ge(y_out, t + 1)
                        for q in range(4):
                            last = pe.matmul(p_y[:, u, 0:D], hid[:, u, q, :], wd[:, u, q, :], start=(q == 0), stop=(q == 3))
                        last.then_inc(y_full, 1)

            @block.scalar
            def _(act):
                with act.Fori(0, SLOT_TILES // 2) as i:
                    for u in range(2):
                        t = i * 2 + u
                        act.wait_ge(t_full, t + 1)
                        act.activation(x_t[:, u, :, :], p_t[:, 0, 0:2, :], ACT.Copy).then_inc(t_out, 1)
                        act.wait_ge(g_full, t + 1)
                        act.activation(sl[:, u, :, :], p_g[:, u, :, :], ACT.Silu).then_inc(s_out, 1)
                        act.wait_ge(y_out, t + 2)
                        act.dma_start(m["ys"].rearrange("(t p) n -> t p n", p=128)[t], y[:, u, :]).then_inc(stored[u], 16)
                for u in range(2):
                    act.wait_ge(stored[u], 16 * (SLOT_TILES // 2) + 16)

            @block.vector
            def _(dve):
                dve.sem_inc(y_out, 1)
                for u in range(2):
                    dve.sem_inc(stored[u], 16)
                with dve.Fori(0, SLOT_TILES // 2) as i:
                    for u in range(2):
                        t = i * 2 + u
                        dve.wait_ge(s_out, t + 1)
                        dve.tensor_tensor(hid[:, u, :, :], sl[:, u, :, :], p_u[:, u, :, :], ALU.mult).then_inc(hid_ready, 1)
                        dve.wait_ge(y_full, t + 3)
                        dve.wait_ge(stored[u], i * 16 + 16)
                        dve.tensor_copy(y[:, u, :], p_y[:, u, 0:D]).then_inc(y_out, 1)


def combine_stage(nc, out, state_h, m):
    RING = 6
    with ExitStack() as ctx:
        sem = lambda n: ctx.enter_context(nc.semaphore(n))
        got = ctx.enter_context(nc.sbuf_tensor("got", [128, RING, D], F32))
        fetched, added, stored = [sem(f"c_fetched{i}") for i in range(RING)], sem("c_added"), sem("c_stored")
        tiles = [(b, g) for b in range(B) for g in range(3)]
        with nc.Block() as block:
            @block.gpsimd
            def _(pool):
                for t, (b, g) in enumerate(tiles):
                    n = TILE_N[g]
                    if t >= RING:
                        pool.wait_ge(added, t - RING + 1)
                    pool.indirect_dma_start(got[0:n, t % RING, :], None, m["ys"],
                                            bass.IndirectOffsetOnAxis(ap=m["slot"][0:n, t:t + 1], axis=0)).then_inc(fetched[t % RING], 16)

            @block.vector
            def _(dve):
                for t, (b, g) in enumerate(tiles):
                    n = TILE_N[g]
                    dve.wait_ge(fetched[t % RING], 16 * (t // RING + 1))
                    dve.tensor_tensor(state_h[0:n, b, g, :], state_h[0:n, b, g, :], got[0:n, t % RING, :], ALU.add).then_inc(added, 1)

            @block.sync
            def _(sp):
                for t, (b, g) in enumerate(tiles):
                    sp.wait_ge(added, t + 1)
                    sp.dma_start(out[b, TILE0[g]:TILE0[g] + TILE_N[g], :], state_h[0:TILE_N[g], b, g, :]).then_inc(stored, 16)
                sp.wait_ge(stored, 16 * len(tiles))


def move_rows(nc, state_h, h_rows, back):
    with nc.semaphore("moved_in" if back else "moved_out") as moved, nc.Block() as block:
        @block.sync
        def _(sp):
            for g, n in enumerate(TILE_N):
                pair = (state_h[0:n, :, g, :], h_rows[g, 0:n])
                sp.dma_start(*(pair if back else pair[::-1])).then_inc(moved, 16)
            sp.wait_ge(moved, 48)


def build(nc, a, out):
    with ExitStack() as ctx:
        sb = lambda n, s, d=F32: ctx.enter_context(nc.sbuf_tensor(n, s, d))
        state_x = sb("state_x", [128, B + 1, 3, D])
        c = {"ident": sb("ident", [128, 128]), "mom_last": sb("mom_last", [128, B, 2])}
        m = {"slot": sb("slot", [128, 3 * B], U32), "experts": sb("experts", [1, SLOT_TILES], I32),
             "xs": nc.dram_tensor("xs_slots", (SLOT_TILES * 128, D), F32, kind="Internal").ap(),
             "ys": nc.dram_tensor("ys_slots", (SLOT_TILES * 128, D), F32, kind="Internal").ap()}
        h_rows = nc.dram_tensor("h_rows", (3, 128, B, D), F32, kind="Internal").ap()
        with nc.sbuf_tensor("state_h1", [128, B, 3, D], F32) as state_h:
            tokens_stage(nc, a, c, state_h, state_x[:, 1:B + 1, :, :])
            move_rows(nc, state_h, h_rows, False)
        attention_stage(nc, a, c, state_x)
        state_h = sb("state_h2", [128, B, 3, D])
        move_rows(nc, state_h, h_rows, True)
        router_stage(nc, a, c, state_h, state_x[:, 1:B + 1, :, :], m)
        experts_stage(nc, a, c, m)
        combine_stage(nc, out, state_h, m)


def kernel(**x):
    import concourse.bacc as _bacc
    from concourse.bass_utils import run_bass_kernel_spmd as _run

    t = {k: np.asarray(v) for k, v in x.items()}
    cat = np.concatenate
    tok = lambda k: t["L0_tok_" + k]
    att = lambda k: t["L0_attn_" + k]
    eye = np.eye(128, dtype=np.float32)
    row = lambda v: v.reshape(1, -1)
    feat = np.stack([att("ln1_g"), att("ln1_b"), att("ln2_g"), att("ln2_b")], 1).reshape(2, 4, 2, 128)
    i8 = np.arange(128) % ROWS
    arrays = {
        "x": t["x"], "ids": np.stack([t["x_txt"], t["itok_BS_0_4096"]], 0).transpose(2, 1, 0),
        "fractions": np.stack([t["fside_BS_delta_" + k] for k in ("x1", "x2", "y1", "y2")], 0).transpose(2, 0, 1),
        "Wq": cat([tok("Wq_w").T, row(tok("Wq_b"))]),
        "Wkv": cat([cat([tok("Wk_w").T, row(tok("Wk_b"))]), cat([tok("Wv_w").T, row(tok("Wv_b"))])], 1),
        "id_b": cat([np.broadcast_to(eye[:64, None, :64], (64, HD, 64)), tok("out_b").reshape(1, HD, 64)]),
        "w_bias_t": tok("w_bias").T, "mask_t": np.ascontiguousarray(tok("local_mask").T).view(np.int32),
        "out_w": tok("out_w"), "ln_g": tok("ln_g"), "ln_b": tok("ln_b"), "embeds": t["L0_txt_loc_embeds"],
        "wq": att("wq"), "wk": att("wk"), "wv": att("wv"), "wo": att("wo"), "w1": att("w1"), "w2": att("w2"),
        "mem_k": att("mem_k").reshape(2, 8, 2, MEM, DH).transpose(2, 4, 0, 1, 3).reshape(128, 2, 8, MEM),
        "mem_v": att("mem_v").transpose(0, 2, 1, 3).reshape(2, MEM, H * DH),
        "pre": att("pre_proj"), "post": att("post_proj"),
        "bo_b2": np.stack([att("bo"), att("b2")], 1).reshape(2, 1, 2, D), "b1": att("b1").reshape(2, 8, 128).transpose(0, 2, 1),
        "gb": feat.transpose(0, 3, 2, 1),
        "gate_w": t["L0_ffn_gate_w"], "sg": t["L0_ffn_shared_gate_w"], "su": t["L0_ffn_shared_up_w"], "sd": t["L0_ffn_shared_down_w"],
        "rg": t["L0_ffn_routed_gate_w"], "ru": t["L0_ffn_routed_up_w"], "rd": t["L0_ffn_routed_down_w"],
        "ident": eye, "ones": np.ones((1, L * HD), np.float32), "ones_c": np.ones((128, 1), np.float32),
        "eye8": eye[:ROWS, :ROWS][i8],
        "diag": np.where(np.arange(ROWS)[None, :] <= i8[:, None], np.float32(BIG), np.float32(-BIG)),
        "tri": np.triu(np.ones((128, 128), np.float32), 1),
        "iota_e": np.broadcast_to(np.arange(EXPERTS, dtype=np.float32), (128, EXPERTS)),
        "iota_p": np.arange(128, dtype=np.float32).reshape(128, 1),
    }
    nc = _bacc.Bacc("TRN2", target_bir_lowering=False, num_devices=1)
    arrays = {k: np.ascontiguousarray(v) for k, v in arrays.items()}
    a = {k: nc.dram_tensor("in_" + k, v.shape, mybir.dt.from_np(v.dtype), kind="ExternalInput").ap() for k, v in arrays.items()}
    out = nc.dram_tensor("out_0", (B, SEQ, D), F32, kind="ExternalOutput").ap()
    build(nc, a, out)
    r = _run(nc, [{"in_" + k: v for k, v in arrays.items()}], core_ids=[0])
    return r.results[0]["out_0"]
```

```python
from contextlib import ExitStack

import numpy as np
import concourse.bass as bass
from concourse import mybir

F32 = mybir.dt.float32
I32 = mybir.dt.int32
U32 = mybir.dt.uint32
U8 = mybir.dt.uint8
ALU = mybir.AluOpType
ACT = mybir.ActivationFunctionType
AX = mybir.AxisListType

B, F, L, HD, D = 8, 64, 256, 4, 256
S_TXT = 77
SEQ = L + S_TXT
H, DH, MEM = 16, 64, 32
KEYS = SEQ + MEM
TILE0 = (0, 96, 224)
TILE_N = (96, 128, 109)
ROWS = 8
BLOCKS = -(-SEQ // ROWS)
GROUP0 = (0, 12, 28, BLOCKS)
FULL_ROWS = MEM // ROWS
EXPERTS, HID = 32, 512
SLOT_TILES = EXPERTS + (B * SEQ - EXPERTS) // 128
BIG = 3.4028234663852886e38
EPS = 1e-5


def all_rows(vector, rows):
    return bass.AP(vector.tensor, vector.offset, [[0, rows], [1, vector.shape[-1]]])


def block_width(n):
    return min(MEM + ROWS * (n + 1), KEYS)


def tile_of(n):
    return sum(n >= g for g in GROUP0[1:3])


def layer_norm_stats(dve, stats, moments, source):
    dve.bn_stats(stats, source)
    dve.drain()
    return dve.bn_aggr(moments, stats)


def tokens_stage(nc, a, c, state_h, state_x):
    with ExitStack() as ctx:
        sb = lambda n, s, d=F32: ctx.enter_context(nc.sbuf_tensor(n, s, d))
        ps = lambda n, s, d=F32: ctx.enter_context(nc.psum_tensor(n, s, d))
        sem = lambda n: ctx.enter_context(nc.semaphore(n))
        xa = sb("xa", [65, 2, L * HD])
        w_q = sb("w_q", [65, 64])
        w_kv = sb("w_kv", [65, 128])
        id_b = sb("id_b", [65, HD, 64])
        ew = sb("ew", [128, 2, L])
        mask8 = sb("mask8", [128, 2, L // 4], I32)
        maskf = sb("maskf", [128, 2, L])
        w_out = sb("w_out", [128, 2, D])
        gain = sb("gain", [128, D])
        shift = sb("shift", [128, D])
        ekv = sb("ekv", [128, 2, 2, D])
        e_q = sb("e_q", [128, 2, L])
        dq = sb("dq", [128, 2, L])
        rq = sb("rq", [128, 2, L])
        y_t = sb("y_t", [128, 2, L])
        stats = sb("stats", [128, 6])
        mom = sb("mom", [128, 2])
        rstd = sb("rstd", [128, 1])
        half = sb("half", [128, 1])
        xn = sb("xn", [128, D])
        xg = sb("xg", [128, D])
        ids = sb("ids", [S_TXT, B, 2], I32)
        idf = sb("idf", [S_TXT, B, 2])
        pad = sb("pad", [S_TXT, B, 2])
        idx = sb("idx", [S_TXT, B, 2], U32)
        fr = sb("fr", [S_TXT, 4, B])
        w4 = sb("w4", [S_TXT, 4, B])
        emb = sb("emb", [S_TXT, 2, D])
        mixed = sb("mixed", [S_TXT, D])
        p_kv = ps("p_kv", [128, 2, HD, 2, 64])
        p_q = ps("p_q", [128, 2, L])
        p_num = ps("p_num", [128, 2, L])
        p_den = ps("p_den", [128, 2, L])
        p_h = ps("p_h", [128, 3, 512])
        loaded = sem("t_loaded")
        x_in = [sem("t_x_in0"), sem("t_x_in1")]
        ready = sem("t_ready")
        kv_full = sem("t_kv_full")
        q_full = sem("t_q_full")
        ek_done = sem("t_ek_done")
        eq_done = sem("t_eq_done")
        ekv_done = sem("t_ekv_done")
        nd_full = sem("t_nd_full")
        y_done = sem("t_y_done")
        h_full = sem("t_h_full")
        mom_done = sem("t_mom_done")
        rstd_done = sem("t_rstd_done")
        gathered = sem("t_gathered")
        text_done = sem("t_text_done")
        text_moved = sem("t_text_moved")
        b_done = sem("t_b_done")
        idx_done = sem("t_idx_done")
        chain = sem("t_chain")
        NLOAD = 13
        xv = [xa[:, u, :].rearrange("c (l h) -> c h l", h=HD) for u in range(2)]
        with nc.Block() as block:
            @block.sync
            def _(sp):
                loads = [(w_q[:, :], a["Wq"]), (w_kv[:, :], a["Wkv"]), (id_b[:, :, :], a["id_b"]),
                         (ew[:, :, :], a["w_bias_t"].rearrange("(s p) t -> p s t", p=128)),
                         (mask8[:, :, :], a["mask_t"].rearrange("(s p) t -> p s t", p=128)),
                         (w_out[:, :, :], a["out_w"].rearrange("(c p) n -> p c n", p=128)),
                         (gain[:, :], all_rows(a["ln_g"], 128)),
                         (shift[:, :], all_rows(a["ln_b"], 128)),
                         (ids[:, :, :], a["ids"]), (fr[:, :, :], a["fractions"]),
                         (c["ident"][:, :], a["ident"]), (xa[64:65, 0, :], a["ones"]), (xa[64:65, 1, :], a["ones"])]
                assert len(loads) == NLOAD
                for dst, src in loads:
                    sp.dma_start(dst, src).then_inc(loaded, 16)

                def load_x(b, u):
                    sp.dma_start(xa[0:64, u, :], a["x"][b].rearrange("c l h -> c (l h)")).then_inc(x_in[u], 16)

                def move_text(b):
                    sp.wait_ge(text_done, b + 1)
                    sp.dma_start(state_h[32:32 + S_TXT, b, 2, :], mixed[:, :]).then_inc(text_moved, 16)

                for u in range(2):
                    load_x(u, u)
                with sp.Fori(0, B // 2 - 1) as i:
                    for u in range(2):
                        b = i * 2 + u
                        move_text(b)
                        sp.wait_ge(h_full, 3 * b + 3)
                        load_x(i * 2 + (u + 2), u)
                for b in (B - 2, B - 1):
                    move_text(b)
                sp.wait_ge(text_moved, 16 * B)

            @block.gpsimd
            def _(pool):
                pool.memset(half[:, :], -0.5)
                pool.drain()
                pool.wait_ge(idx_done, 1)
                for b in range(B):
                    if b:
                        pool.wait_ge(text_done, b)
                    for j in range(2):
                        pool.indirect_dma_start(emb[:, j, :], None, a["embeds"],
                                                bass.IndirectOffsetOnAxis(ap=idx[:, b, j:j + 1], axis=0)).then_inc(gathered, 16)
                    for k, n in enumerate((96, 96, 128, 128, 32)):
                        pool.wait_ge(mom_done, 5 * b + k + 1)
                        pool.tensor_scalar(rstd[0:n, :], mom[0:n, 1:2], EPS, None, ALU.add)
                        pool.drain()
                        pool.tensor_tensor(rstd[0:n, :], rstd[0:n, :], half[0:n, :], ALU.pow).then_inc(rstd_done, 1)

            @block.tensor
            def _(pe):
                pe.wait_ge(loaded, 16 * NLOAD)
                pe.wait_ge(ready, 1)

                def project(i, u):
                    x = xv[u % 2]
                    pe.wait_ge(x_in[u % 2], 16 * (i + u // 2) + 16)
                    for s in range(2):
                        for h in range(HD):
                            last = pe.matmul(p_kv[:, s, h, :, :], x[:, h, s * 128:s * 128 + 128], w_kv[:, :], start=(h == 0), stop=True,
                                             skip_group_check=True)
                    last.then_inc(kv_full, 1)
                    pe.wait_ge(eq_done, i * 2 + u + 1)
                    for h in range(HD):
                        last = pe.matmul(p_q[64 * (h % 2):64 * (h % 2) + 64, h // 2, :], w_q[:, :], x[:, h, :],
                                         start=(h // 2 == 0), stop=True, skip_group_check=True)
                    last.then_inc(q_full, 1)

                def mix(i, u):
                    b, x = i * 2 + u, xv[u]
                    pe.wait_ge(ekv_done, b + 1)
                    for out, j in ((p_num, 0), (p_den, 1)):
                        for m in range(2):
                            for s in range(2):
                                last = pe.matmul(out[:, m, :], ekv[:, s, j, m * 128:m * 128 + 128], ew[:, s, :],
                                                 start=(m == 0 and s == 0), stop=(s == 1), skip_group_check=True)
                    last.then_inc(nd_full, 1)
                    pe.wait_ge(y_done, b + 2)
                    pe.wait_ge(b_done, b + 1)
                    for g, (t0, n) in enumerate(((0, 96), (96, 128), (224, 32))):
                        for m in range(2):
                            pe.matmul(p_h[0:n, g, 0:D], y_t[:, m, t0:t0 + n], w_out[:, m, :], start=(m == 0), stop=False,
                                      skip_group_check=True)
                        for h in range(HD):
                            last = pe.matmul(p_h[0:n, g, 64 * h:64 * h + 64], x[:, h, t0:t0 + n], id_b[:, h, :],
                                             start=False, stop=True, skip_group_check=True)
                        last.then_inc(h_full, 1)

                project(0, 0)
                with pe.Fori(0, B // 2 - 1) as i:
                    for u in range(2):
                        mix(i, u)
                        project(i, u + 1)
                mix(B // 2 - 1, 0)
                project(B // 2 - 1, 1)
                mix(B // 2 - 1, 1)

            @block.scalar
            def _(act):
                act.wait_ge(chain, 3)
                act.activation(ew[:, :, :], ew[:, :, :], ACT.Exp).then_inc(ready, 1)
                act.sem_inc(eq_done, 1)
                with act.Fori(0, B) as b:
                    act.wait_ge(kv_full, b + 1)
                    act.activation(ekv[:, :, 1, :].rearrange("p s (h d) -> p s h d", h=HD), p_kv[:, :, :, 0, :], ACT.Exp).then_inc(ek_done, 1)
                    act.wait_ge(q_full, b + 1)
                    act.wait_ge(y_done, b + 1)
                    act.activation(e_q[:, :, :], p_q[:, :, :], ACT.Exp, scale=-1.0).then_inc(eq_done, 1)

            @block.vector
            def _(dve):
                dve.wait_ge(loaded, 16 * NLOAD)
                dve.tensor_copy(maskf[:, :, :], mask8[:, :, :].bitcast(U8))
                dve.tensor_copy(idf[:, :, :], ids[:, :, :]).then_inc(chain, 2)
                dve.drain()
                dve.tensor_tensor(ew[:, :, :], ew[:, :, :], maskf[:, :, :], ALU.mult).then_inc(chain, 1)
                dve.tensor_scalar(pad[:, :, :], idf[:, :, :], -1.0, 4097.0, ALU.is_equal, ALU.mult)
                dve.drain()
                dve.tensor_tensor(idx[:, :, :], idf[:, :, :], pad[:, :, :], ALU.add).then_inc(idx_done, 1)
                for k, (u, v) in enumerate(((1, 3), (1, 2), (0, 3), (0, 2))):
                    dve.tensor_tensor(w4[:, k, :], fr[:, u, :], fr[:, v, :], ALU.mult)
                dve.wait_ge(ready, 1)
                dve.sem_inc(y_done, 1)
                dve.drain().then_inc(b_done, 1)
                with dve.Fori(0, B) as b:
                    dve.wait_ge(ek_done, b + 1)
                    for s in range(2):
                        last = dve.tensor_tensor(ekv[:, s, 0, :].rearrange("p (h d) -> p h d", h=HD), p_kv[:, s, :, 1, :],
                                                 ekv[:, s, 1, :].rearrange("p (h d) -> p h d", h=HD), ALU.mult)
                    last.then_inc(ekv_done, 1)
                    dve.wait_ge(nd_full, b + 1)
                    dve.wait_ge(eq_done, b + 2)
                    dve.scalar_tensor_tensor(dq[:, :, :], e_q[:, :, :], 1.0, p_den[:, :, :], ALU.add, ALU.mult)
                    dve.drain()
                    dve.reciprocal(rq[:, :, :], dq[:, :, :])
                    dve.drain()
                    dve.tensor_tensor(y_t[:, :, :], p_num[:, :, :], rq[:, :, :], ALU.mult).then_inc(y_done, 1)
                    dve.wait_ge(gathered, 32 * b + 32)
                    dve.tensor_scalar(mixed[:, :], emb[:, 0, :], w4[:, 0, bass.ds(b, 1)], None, ALU.mult)
                    for k in range(1, 4):
                        dve.drain()
                        last = dve.scalar_tensor_tensor(mixed[:, :], emb[:, 1, :], w4[:, k, bass.ds(b, 1)], mixed[:, :], ALU.mult, ALU.add)
                    last.then_inc(text_done, 1)
                    k = 0
                    for g, n in enumerate((96, 128, 32)):
                        dve.drain()
                        dve.wait_ge(h_full, 3 * b + g + 1)
                        layer_norm_stats(dve, stats[0:n, :], mom[0:n, :], p_h[0:n, g, 0:D]).then_inc(mom_done, 1)
                        k += 1
                        dve.wait_ge(rstd_done, 5 * b + k)
                        dve.tensor_scalar(xn[0:n, :], p_h[0:n, g, 0:D], mom[0:n, 0:1], rstd[0:n, :], ALU.subtract, ALU.mult)
                        dve.drain()
                        dve.tensor_tensor(xg[0:n, :], xn[0:n, :], gain[0:n, :], ALU.mult)
                        dve.drain()
                        if g == 2:
                            dve.tensor_tensor(state_h[0:n, b, g, :], xg[0:n, :], shift[0:n, :], ALU.add)
                            dve.drain()
                            dve.wait_ge(text_moved, 16 * b + 16)
                            break
                        dve.tensor_tensor(state_h[0:n, b, g, :], xg[0:n, :], shift[0:n, :], ALU.add)
                        dve.drain()
                        layer_norm_stats(dve, stats[0:n, :], mom[0:n, :], state_h[0:n, b, g, :]).then_inc(mom_done, 1)
                        k += 1
                        dve.wait_ge(rstd_done, 5 * b + k)
                        dve.tensor_scalar(state_x[0:n, b, g, :], state_h[0:n, b, g, :], mom[0:n, 0:1], rstd[0:n, :],
                                          ALU.subtract, ALU.mult)
                        dve.drain()
                    n = TILE_N[2]
                    dve.tensor_scalar(xn[0:n, :], state_h[0:n, b, 2, :], 1.0, None, ALU.mult)
                    dve.drain()
                    layer_norm_stats(dve, stats[0:n, :], mom[0:n, :], xn[0:n, :])
                    dve.drain()
                    dve.tensor_copy(c["mom_last"][0:n, b, :], mom[0:n, :])
                    dve.drain().then_inc(b_done, 1)
        last_done = sem("t_last_done")
        with nc.Block() as block:
            rs = sb("rs_last", [128, B])
            mh = sb("mh_last", [128, B])
            n = TILE_N[2]

            @block.gpsimd
            def _(pool):
                pool.memset(mh[:, :], -0.5)
                pool.tensor_scalar(rs[0:n, :], c["mom_last"][0:n, :, 1], EPS, None, ALU.add)
                pool.drain()
                pool.tensor_tensor(rs[0:n, :], rs[0:n, :], mh[0:n, :], ALU.pow).then_inc(last_done, 1)

            @block.vector
            def _(dve):
                dve.wait_ge(last_done, 1)
                for b in range(B):
                    dve.tensor_scalar(state_x[0:n, b, 2, :], state_h[0:n, b, 2, :], c["mom_last"][0:n, b, 0:1], rs[0:n, b:b + 1],
                                      ALU.subtract, ALU.mult)


PAIRS = BLOCKS // 2
RING = 3
AHEAD = 3
PARTS = {"T": 2, "K": 8, "V": 2, "Q": 8, "PV": 8, "WO": 1, "T2": 2, "F1": 8, "F2": 1}
THIS, NEXT, LAST = range(3)


def body_plan():
    items = [[] for _ in range(PAIRS)]

    def pieces(kind, g, who=THIS):
        return [(kind, g, p, who) for p in range(PARTS[kind])]

    def stats(g, who, second):
        return [("LN", g, second, who), ("N", g, second, who)]

    def add(g, who, second):
        return pieces("F2" if second else "WO", g, who) + [("X", g, second, who)]

    items[1] += pieces("K", 1)
    items[2] += pieces("Q", 1)
    items[3] += pieces("PV", 2, LAST)
    items[4] += add(2, LAST, 0) + stats(2, LAST, 1)
    items[5] += pieces("V", 0) + pieces("T2", 2, LAST)
    items[6] += pieces("F1", 2, LAST)
    items[7] += add(2, LAST, 1) + pieces("PV", 0)
    items[8] += pieces("K", 2)
    items[9] += add(0, THIS, 0) + stats(0, THIS, 1)
    items[10] += pieces("Q", 2) + pieces("T2", 0)
    items[11] += pieces("F1", 0)
    items[12] += add(0, THIS, 1)
    items[13] += pieces("V", 2) + stats(0, NEXT, 0)
    items[14] += pieces("V", 1) + pieces("T", 0, NEXT)
    items[15] += pieces("PV", 1)
    items[16] += add(1, THIS, 0) + stats(1, THIS, 1)
    items[17] += [("MK", 0, 0, NEXT)] + pieces("K", 0, NEXT) + pieces("Q", 0, NEXT)
    items[18] += [("PM", 0, 0, NEXT)] + pieces("T2", 1) + stats(1, NEXT, 0)
    items[19] += pieces("T", 1, NEXT) + pieces("F1", 1) + stats(2, NEXT, 0)
    items[20] += add(1, THIS, 1) + pieces("T", 2, NEXT)
    return items


def attention_stage(nc, a, c, state_x):
    items = body_plan()
    opening = [x for x in sum(items, []) if x[3] == NEXT]
    ending = [x for x in sum(items, []) if x[3] == LAST]
    body = sum(items, [])

    def numbered(order, kinds):
        return {x: i for i, x in enumerate(x for x in order if x[0] in kinds)}

    place, place0, place9 = [numbered(x, PARTS) for x in (body, opening, ending)]
    ln_no, ln_no0, ln_no9 = [numbered(x, ("LN",)) for x in (body, opening, ending)]
    x_no, x_no9 = numbered(body, ("X",)), numbered(ending, ("X",))
    N_PIECES, N_LN, N_X = len(place), len(ln_no), len(x_no)
    PIECES0, LN0 = len(place0), len(ln_no0)
    assert N_PIECES % 2 == 0 and PIECES0 % 2 == 0 and PAIRS % RING == 0
    tails = [p for p in range(PAIRS) if block_width(2 * p) < 128 * (tile_of(2 * p) + 1)]
    with ExitStack() as ctx:
        sb = lambda n, s, d=F32: ctx.enter_context(nc.sbuf_tensor(n, s, d))
        ps = lambda n, s, d=F32: ctx.enter_context(nc.psum_tensor(n, s, d))
        sem = lambda n: ctx.enter_context(nc.semaphore(n))
        ident = c["ident"]
        wqkv = sb("wqkv", [128, 2, 3, 1024])
        wo = sb("wo", [128, 8, D])
        w1 = sb("w1", [128, 2, 1024])
        w2 = sb("w2", [128, 8, D])
        mem_v = sb("mem_v", [MEM, 1024])
        mem_k = sb("mem_k", [128, 2, 8, MEM])
        rows1 = sb("rows1", [1, 2, D])
        ones1 = sb("ones1", [1, 128])
        gb1 = sb("gb1", [128, 2, 2])
        gb2 = sb("gb2", [128, 2, 2])
        b1 = sb("b1", [128, 8])
        mixb = sb("mixb", [128, 2, 2, H])
        eye8 = sb("eye8", [128, ROWS])
        diag = sb("diag", [128, ROWS])
        mixes = sb("mixes", [128, 2, 2, H, ROWS])
        pre_mix = sb("pre_mix", [128, 128])
        post_mix = sb("post_mix", [128, 128])
        k_t = sb("k_t", [128, 8, KEYS])
        v = sb("v", [128, 3, 1024])
        q_bd = sb("q_bd", [128, 16, 8, 32])
        xn = sb("xn_a", [128, D])
        xn_t = sb("xn_t", [128, 2, MEM + 336])
        xn2_t = sb("xn2_t", [128, 2, 128])
        dots = sb("dots", [128, 2, KEYS])
        mixed = sb("mixed_a", [128, 2 * RING, KEYS])
        work = sb("work", [128, 2, KEYS])
        vals = sb("vals", [128, 2 * RING, 8, 8])
        nmax = sb("nmax", [128, 2 * RING])
        rsum = sb("rsum", [128, 2 * RING])
        rinv = sb("rinv", [128, 2 * RING])
        kept = sb("kept", [128, 2, KEYS])
        prob = sb("prob", [128, 2 * RING, 384])
        post = sb("post", [128, 2 * RING, 128])
        attn_t = sb("attn_t", [128, 4, H, 128])
        wide_t = sb("wide_t", [128, 8, 128])
        delta = sb("delta", [128, D])
        junk = sb("junk_a", [128, D])
        s1 = sb("s1", [128, 1])
        s2 = sb("s2", [128, 1])
        nmean = sb("nmean", [128, 1])
        var = sb("var", [128, 1])
        rstd = sb("rstd_a", [128, 1])
        nmr = sb("nmr", [128, 1])
        half, eps, minus, per, nper, carry_p, carry_a, carry_b, carry_v = [sb(k, [128, 1]) for k in (
            "half_a", "eps_a", "minus_a", "per_a", "nper_a", "carry_p", "carry_a", "carry_b", "carry_v")]
        zeros = sb("zeros_a", [128, 384])
        p_dots = ps("p_dots", [128, 2, 512])
        p_mix = ps("p_mix", [128, 2, 512])
        p_post = ps("p_post", [128, 2, 512])
        p_any = ps("p_any", [128, 2, 512])
        w_a, w_b, s_c, s_set, s_mixes = sem("a_weights_a"), sem("a_weights_b"), sem("a_consts"), sem("a_set"), sem("a_mixes")
        dots_full, dots_out, mix_full, mix_out, max_ready, nmax_ready, exp_ready, prob_ready, post_scaled, post_full, attn_out = [
            sem("a_" + k) for k in ("dots_full", "dots_out", "mix_full", "mix_out", "max_ready", "nmax_ready", "exp_ready",
                                    "prob_ready", "post_scaled", "post_full", "attn_out")]
        mask_ready, threshold_ready, selected, premix_ready = [
            sem("a_" + k) for k in ("mask_ready", "threshold_ready", "selected", "premix_ready")]
        piece_full, piece_out, x_added = sem("a_piece_full"), sem("a_piece_out"), sem("a_x_added")
        s1_ready, mean_ready, s2_ready, rstd_ready, xn_ready = [sem("a_" + k) for k in ("s1", "mean", "s2", "rstd", "xn")]
        NA, NB = 5, 6

        def counts(it):
            return (it * PAIRS + AHEAD, it * N_PIECES + PIECES0, it * N_LN + LN0, it * N_X + 1)

        def out_count(mode, it, x):
            if mode == "opening":
                return place0[x] + 1
            return counts(it)[1] + (place if mode == "body" else place9)[x] + 1

        def pipeline(mode, engine, start, middle, item):
            if mode == "opening":
                for x in opening:
                    item(x)
                for s in range(-3, 1):
                    start(s)
            elif mode == "ending":
                for x in ending:
                    item(x)
            else:
                for s in range(PAIRS):
                    if s:
                        start(s)
                    for x in items[s]:
                        item(x)
                    if s:
                        middle(s - 1)
                start(PAIRS)
                middle(PAIRS - 1)

        def run(engine, program):
            program("opening", 0)
            with engine.Fori(0, 2 * B) as it:
                program("body", it)
            program("ending", 2 * B)

        def slots(engine, mode, it):
            if mode == "opening":
                return (1, 1, 1)
            if mode == "ending":
                return (1, 1, B)
            begun = (it + 15) // 16
            return (engine.snap(it % B + 1), engine.snap((it + 1) % B + 1), engine.snap(((it + 7) % B + 1) * begun))

        with nc.Block() as block:
            @block.sync
            def _(sp):
                for dst, src in ((eye8[:, :], a["eye8"]), (diag[:, :], a["diag"]), (ones1[:, :], a["ones"][:, 0:128]),
                                 (mem_k[:, :, :, :], a["mem_k"])):
                    sp.dma_start(dst, src).then_inc(s_c, 16)
                for l in range(2):
                    for j, name in enumerate(("pre", "post")):
                        m = a[name][l]
                        src = bass.AP(m.tensor, m.offset, [[H, H], [0, ROWS], [1, H]])
                        sp.dma_start(mixb[:, l, j, :], src).then_inc(s_c, 16)

                def load_a(l):
                    for dst, src in ((wqkv[:, :, 1, :], a["wk"][l].rearrange("(c p) n -> p c n", p=128)),
                                     (wqkv[:, :, 0, :], a["wq"][l].rearrange("(c p) n -> p c n", p=128)),
                                     (wqkv[:, :, 2, :], a["wv"][l].rearrange("(c p) n -> p c n", p=128)),
                                     (mem_v[:, :], a["mem_v"][l]), (gb1[:, :, :], a["gb"][l][:, :, 0:2])):
                        sp.dma_start(dst, src).then_inc(w_a, 16)

                def load_b(l):
                    for dst, src in ((wo[:, :, :], a["wo"][l].rearrange("(c p) n -> p c n", p=128)),
                                     (w1[:, :, :], a["w1"][l].rearrange("(c p) n -> p c n", p=128)),
                                     (w2[:, :, :], a["w2"][l].rearrange("(c p) n -> p c n", p=128)),
                                     (rows1[:, :, :], a["bo_b2"][l]), (gb2[:, :, :], a["gb"][l][:, :, 2:4]), (b1[:, :], a["b1"][l])):
                        sp.dma_start(dst, src).then_inc(w_b, 16)

                load_a(0)
                load_b(0)
                sp.wait_ge(piece_out, counts(B - 1)[1] + place[("V", 1, 1, THIS)] + 1)
                load_a(1)
                sp.wait_ge(piece_out, counts(B)[1] + place[("F2", 2, 0, LAST)] + 1)
                load_b(1)

            @block.gpsimd
            def _(pool):
                for t, value in ((q_bd[:, :, :, :], 0.0), (xn_t[:, :, :], 0.0), (prob[:, :, :], 0.0), (half[:, :], -0.5),
                                 (eps[:, :], EPS), (minus[:, :], -1.0), (per[:, :], 1.0 / D), (nper[:, :], -1.0 / D),
                                 (zeros[:, :], 0.0), (attn_t[:, :, :, :], 0.0), (v[:, :, :], 0.0), (state_x[:, 0, :, :], 0.0)):
                    pool.memset(t, value)
                pool.wait_ge(s_c, 16 * 8)
                for q in (nmax_ready, mask_ready, prob_ready):
                    pool.sem_inc(q, AHEAD)
                pool.sem_inc(x_added, 1)
                pool.drain().then_inc(s_set, 1)

                def program(mode, it):
                    pairs, _, lns, xs = [pool.snap(q) if mode == "body" else q for q in counts(it)]
                    slot = slots(pool, mode, it)
                    lno, xno = (ln_no0, {}) if mode == "opening" else (ln_no9, x_no9) if mode == "ending" else (ln_no, x_no)
                    if mode == "opening":
                        lns = 0

                    def select(p):
                        if 2 * p < FULL_ROWS:
                            return
                        pool.wait_ge(threshold_ready, pairs + p + 1)
                        pool.tensor_tensor(carry_p[:, :], minus[:, :], minus[:, :], ALU.mult)
                        for n in (2 * p, 2 * p + 1):
                            r6, w = n % (2 * RING), block_width(n)
                            pool.tensor_scalar(kept[:, n % 2, 0:w], mixed[:, r6, 0:w], vals[:, r6, 7, 7:8], -BIG / 2, ALU.is_lt, ALU.mult)
                        pool.drain()
                        for n in (2 * p, 2 * p + 1):
                            r6, w = n % (2 * RING), block_width(n)
                            pool.tensor_tensor(kept[:, n % 2, 0:w], kept[:, n % 2, 0:w], mixed[:, r6, 0:w], ALU.add)
                        pool.drain().then_inc(selected, 1)

                    def invert(p):
                        r0 = (2 * p) % (2 * RING)
                        pool.wait_ge(exp_ready, pairs + p + 1)
                        pool.tensor_tensor(rinv[:, r0:r0 + 2], rsum[:, r0:r0 + 2], minus[:, 0:1].broadcast_to([128, 2]), ALU.pow)
                        pool.drain().then_inc(prob_ready, 1)

                    def start(s):
                        p = s
                        if p > 0:
                            select(p - 1)
                        if p >= 0:
                            u = (2 * p) % (2 * RING)
                            pool.wait_ge(max_ready, pairs + p + 1)
                            pool.tensor_tensor(nmax[:, u:u + 2], vals[:, u:u + 2, 0, 0], minus[:, 0:1].broadcast_to([128, 2]), ALU.mult).then_inc(nmax_ready, 1)
                        if p >= 0 and p % PAIRS in tails:
                            pool.wait_ge(post_full, pairs + p - RING + 1)
                            for n in (2 * p, 2 * p + 1):
                                w, end = block_width(n % BLOCKS), 128 * (tile_of(n % BLOCKS) + 1)
                                if w < end:
                                    pool.tensor_tensor(prob[:, n % (2 * RING), w:end], zeros[:, w:end], zeros[:, w:end], ALU.mult)
                        p = s + 2
                        if p >= 0:
                            pool.wait_ge(mix_out, pairs + p + 1)
                            for n in (2 * p, 2 * p + 1):
                                d0, w = MEM + ROWS * (n % BLOCKS), block_width(n % BLOCKS)
                                m = mixed[:, n % (2 * RING), d0:w]
                                pool.tensor_tensor(m, m, diag[:, 0:w - d0], ALU.add)
                            pool.drain().then_inc(mask_ready, 1)
                        if s > 0:
                            invert(s - 1)

                    def item(x):
                        kind, g, p, who = x
                        n = TILE_N[g]
                        if kind == "X":
                            pool.wait_ge(piece_out, out_count(mode, it, ("F2" if p else "WO", g, 0, who)))
                            pool.tensor_tensor(carry_p[:, :], minus[:, :], minus[:, :], ALU.mult)
                            h = state_x[0:n, slot[who], g, :]
                            pool.tensor_tensor(h, h, delta[0:n, :], ALU.add)
                            pool.drain().then_inc(x_added, 1)
                        elif kind == "LN":
                            k = lno[x] + 1
                            pool.wait_ge(s1_ready, lns + k)
                            pool.tensor_tensor(nmean[0:n, :], s1[0:n, :], nper[0:n, :], ALU.mult).then_inc(mean_ready, 1)
                            pool.wait_ge(s2_ready, lns + k)
                            pool.tensor_tensor(var[0:n, :], s2[0:n, :], per[0:n, :], ALU.mult)
                            pool.drain()
                            pool.tensor_tensor(rstd[0:n, :], var[0:n, :], eps[0:n, :], ALU.add)
                            pool.drain()
                            pool.tensor_tensor(var[0:n, :], rstd[0:n, :], half[0:n, :], ALU.pow)
                            pool.drain()
                            pool.tensor_copy(rstd[0:n, :], var[0:n, :])
                            pool.tensor_tensor(nmr[0:n, :], var[0:n, :], nmean[0:n, :], ALU.mult)
                            pool.drain().then_inc(rstd_ready, 1)

                    pipeline(mode, pool, start, lambda p: None, item)

                run(pool, program)

            @block.tensor
            def _(pe):
                pe.sem_inc(dots_full, AHEAD)
                pe.sem_inc(mix_full, AHEAD)
                pe.sem_inc(post_full, AHEAD)
                pe.wait_ge(s_c, 16 * 8)
                pe.wait_ge(s_set, 1)

                def program(mode, it):
                    pairs, first, lns, _ = [pe.snap(q) if mode == "body" else q for q in counts(it)]
                    where, lno = (place0, ln_no0) if mode == "opening" else (place9, ln_no9) if mode == "ending" else (place, ln_no)
                    if mode == "opening":
                        first, lns = 0, 0
                        pe.wait_ge(w_a, 16 * NA)
                    if mode == "body":
                        layer_next = pe.snap((it + 9) // 16)

                    def out(x):
                        pe.wait_ge(piece_out, first + where[x] + 1)

                    def start(s):
                        p = s + 2
                        if p >= 0:
                            pe.wait_ge(dots_out, pairs + p + 1)
                            pe.wait_ge(mix_out, pairs + p)
                            if p % PAIRS == 0:
                                pe.wait_ge(premix_ready, it + 1 if mode == "opening" else it + 2)
                            for n in (2 * p, 2 * p + 1):
                                w = block_width(n % BLOCKS)
                                last = pe.matmul(p_mix[:, n % 2, 0:w], pre_mix[:, :], dots[:, n % 2, 0:w], start=True, stop=True)
                            last.then_inc(mix_full, 1)
                        p = s + 3
                        pe.wait_ge(dots_out, pairs + p)
                        if mode == "opening" and p == 0:
                            out(("Q", 0, 7, NEXT))
                        if mode == "body" and p == PAIRS:
                            out(("Q", 0, 7, NEXT))
                        if mode == "body" and 2 * p in GROUP0[1:3]:
                            out(("Q", tile_of(2 * p), 7, THIS))
                        for n in (2 * p, 2 * p + 1):
                            nn = n % BLOCKS
                            g, w = tile_of(nn), block_width(nn)
                            for j in range(2):
                                for q in range(4):
                                    last = pe.matmul(p_dots[32 * q:32 * q + 32, n % 2, 0:w], q_bd[:, nn - GROUP0[g], 2 * q + j, :],
                                                     k_t[:, 2 * q + j, 0:w], start=(j == 0), stop=(j == 1))
                        last.then_inc(dots_full, 1)

                    def middle(p):
                        pe.wait_ge(post_scaled, pairs + p + 1)
                        pe.wait_ge(attn_out, pairs + p)
                        for n in (2 * p, 2 * p + 1):
                            for j in range(tile_of(n) + 1):
                                last = pe.matmul(p_post[:, n % 2, 128 * j:128 * j + 128], prob[:, n % (2 * RING), 128 * j:128 * j + 128],
                                                 post[:, n % (2 * RING), :], start=(j == 0), stop=True, skip_group_check=True)
                        last.then_inc(post_full, 1)

                    def item(x):
                        kind, g, p, who = x
                        if kind not in PARTS:
                            return
                        k = where[x]
                        n, t0 = TILE_N[g], TILE0[g]
                        bank = p_any[:, k % 2, :]
                        if mode != "opening" or k >= 2:
                            pe.wait_ge(piece_out, first + k - 1)
                        if kind in ("T", "T2"):
                            if p == 0:
                                if who == NEXT and mode == "body":
                                    pe.wait_ge(w_a, layer_next * (16 * NA) + 16 * NA)
                                pe.wait_ge(xn_ready, lns + lno[("LN", g, 0 if kind == "T" else 1, who)] + 1)
                            last = pe.transpose(bank[:, 0:n], xn[0:n, 128 * p:128 * p + 128], ident[0:n, 0:n])
                        elif kind == "K":
                            if p == 0 and ("T", g, 1, who) in where:
                                out(("T", g, 1, who))
                            for j in range(2):
                                last = pe.matmul(bank[:, 0:n], wqkv[:, j, 1, 128 * p:128 * p + 128], xn_t[:, j, MEM + t0:MEM + t0 + n],
                                                 start=(j == 0), stop=(j == 1))
                        elif kind == "V":
                            m = 128 if g < 2 else n
                            for j in range(2):
                                last = pe.matmul(bank[0:m, :], xn_t[:, j, 128 * g:128 * g + m], wqkv[:, j, 2, 512 * p:512 * p + 512],
                                                 start=(j == 0), stop=(j == 1 and g > 0))
                            if g == 0:
                                last = pe.matmul(bank[0:m, :], ident[0:MEM, 0:128], mem_v[:, 512 * p:512 * p + 512], start=False, stop=True)
                        elif kind == "Q":
                            m = 8 * (-(-n // 8))
                            for j in range(2):
                                last = pe.matmul(bank[:, 0:m], wqkv[:, j, 0, 128 * p:128 * p + 128], xn_t[:, j, MEM + t0:MEM + t0 + m],
                                                 start=(j == 0), stop=(j == 1))
                        elif kind == "PV":
                            if p == 0 and who == LAST:
                                pe.wait_ge(attn_out, pairs)
                            elif p == 0:
                                pe.wait_ge(attn_out, pairs + GROUP0[g + 1] // 2)
                                out(("V", g, 1, who))
                            for j in range(g + 1):
                                r = 128 if j < 2 else TILE_N[2]
                                for hh in range(2):
                                    h = 2 * p + hh
                                    last = pe.matmul(bank[64 * hh:64 * hh + 64, 0:n], v[0:r, j, 64 * h:64 * h + 64], attn_t[0:r, j if g else 3, h, 0:n],
                                                     start=(j == 0), stop=(j == g))
                        elif kind in ("WO", "F2"):
                            if kind == "WO":
                                src, w, r = wide_t, wo, 0
                                out(("PV", g, 7, who))
                                if mode == "body" and who == THIS and g == 0:
                                    pe.wait_ge(w_b, (it // B) * (16 * NB) + 16 * NB)
                                if who == LAST:
                                    pe.wait_ge(w_b, 16 * NB)
                            else:
                                src, w, r = wide_t, w2, 1
                                out(("F1", g, 7, who))
                            for j in range(8):
                                pe.matmul(bank[0:n, 0:D], src[:, j, 0:n], w[:, j, :], start=(j == 0), stop=False)
                            last = pe.matmul(bank[0:n, 0:D], ones1[0:1, 0:n], rows1[0:1, r, :], start=False, stop=True)
                        elif kind == "F1":
                            if p == 0:
                                out(("T2", g, 1, who))
                            for j in range(2):
                                last = pe.matmul(bank[:, 0:n], w1[:, j, 128 * p:128 * p + 128], xn2_t[:, j, 0:n], start=(j == 0), stop=(j == 1))
                        last.then_inc(piece_full, 1)

                    pipeline(mode, pe, start, middle, item)

                run(pe, program)

            @block.scalar
            def _(act):
                for q in (dots_out, mix_out, exp_ready, post_scaled, attn_out):
                    act.sem_inc(q, AHEAD)
                act.wait_ge(s_set, 1)
                act.wait_ge(s_mixes, 1)

                def program(mode, it):
                    pairs, first, lns, xs = [act.snap(q) if mode == "body" else q for q in counts(it)]
                    where, lno = (place0, ln_no0) if mode == "opening" else (place9, ln_no9) if mode == "ending" else (place, ln_no)
                    slot = slots(act, mode, it)
                    added = [0]
                    if mode == "opening":
                        first, lns, xs = 0, 0, 0
                    chosen = act.snap(it * (PAIRS - FULL_ROWS // 2)) if mode == "body" else 0
                    next_layer = act.snap(((it + 1) // B) % 2) if mode == "body" else 0
                    if mode == "body":
                        act.activation(post_mix[:, :], mixes[:, act.snap(it // B), 1, :, :].rearrange("p k i -> p (k i)"), ACT.Copy)

                    def exponential(p):
                        act.wait_ge(nmax_ready, pairs + p + 1)
                        if 2 * p >= FULL_ROWS:
                            act.wait_ge(selected, chosen + p - FULL_ROWS // 2 + 1)
                        for n in (2 * p, 2 * p + 1):
                            r6, w = n % (2 * RING), block_width(n)
                            last = act.activation(prob[:, r6, 0:w], kept[:, n % 2, 0:w] if 2 * p >= FULL_ROWS else mixed[:, r6, 0:w], ACT.Exp,
                                                  bias=nmax[:, r6:r6 + 1], accum_out=rsum[:, r6:r6 + 1])
                        if 2 * p < FULL_ROWS:
                            last = act.drain()
                        last.then_inc(exp_ready, 1)

                    def start(s):
                        if s > 0:
                            exponential(s - 1)
                        p = s + 2
                        if p >= 0:
                            act.wait_ge(mix_full, pairs + p + 1)
                            for n in (2 * p, 2 * p + 1):
                                w = block_width(n % BLOCKS)
                                last = act.activation(mixed[:, n % (2 * RING), 0:w], p_mix[:, n % 2, 0:w], ACT.Copy)
                            last.then_inc(mix_out, 1)
                        p = s + 3
                        act.wait_ge(dots_full, pairs + p + 1)
                        for n in (2 * p, 2 * p + 1):
                            w = block_width(n % BLOCKS)
                            last = act.activation(dots[:, n % 2, 0:w], p_dots[:, n % 2, 0:w], ACT.Copy, scale=DH ** -0.5)
                        last.then_inc(dots_out, 1)
                        p = s - 1
                        if p >= 0:
                            act.wait_ge(prob_ready, pairs + p + 1)
                            for n in (2 * p, 2 * p + 1):
                                last = act.activation(post[:, n % (2 * RING), :], post_mix[:, :], ACT.Copy, scale=rinv[:, n % (2 * RING):n % (2 * RING) + 1])
                            last.then_inc(post_scaled, 1)

                    def middle(p):
                        g = tile_of(2 * p)
                        act.wait_ge(post_full, pairs + p + 1)
                        for n in (2 * p, 2 * p + 1):
                            i0 = ROWS * (n - GROUP0[g])
                            last = act.activation(attn_t[:, 0:g + 1, :, i0:i0 + ROWS] if g else attn_t[:, 3:4, :, i0:i0 + ROWS],
                                                  p_post[:, n % 2, 0:128 * (g + 1)].rearrange("p (j k i) -> p j k i", j=g + 1, k=H), ACT.Copy)
                        last.then_inc(attn_out, 1)

                    def item(x):
                        kind, g, p, who = x
                        n, t0 = TILE_N[g], TILE0[g]
                        rows = state_x[0:n, slot[who], g, :]
                        if kind == "MK":
                            if mode == "body":
                                act.wait_ge(dots_full, pairs + PAIRS)
                            act.activation(carry_a[:, :], minus[:, :], ACT.Copy)
                            act.activation(k_t[:, :, 0:MEM], mem_k[:, next_layer, :, :], ACT.Copy)
                            return
                        if kind == "PM":
                            if mode == "body":
                                act.wait_ge(mix_full, pairs + PAIRS)
                            act.activation(carry_b[:, :], minus[:, :], ACT.Copy)
                            act.activation(pre_mix[:, :], mixes[:, next_layer, 0, :, :].rearrange("p k i -> p (k i)"), ACT.Copy).then_inc(premix_ready, 1)
                            return
                        if kind == "X":
                            added[0] += 1
                            return
                        if kind == "LN":
                            if mode != "opening":
                                act.wait_ge(x_added, xs + added[0])
                            act.activation(carry_a[:, :], minus[:, :], ACT.Copy)
                            act.activation(junk[0:n, :], rows, ACT.Copy, accum_out=s1[0:n, :])
                            act.drain().then_inc(s1_ready, 1)
                            act.wait_ge(mean_ready, lns + lno[x] + 1)
                            act.activation(carry_a[:, :], minus[:, :], ACT.Copy)
                            act.activation(junk[0:n, :], rows, ACT.Square, bias=nmean[0:n, :], accum_out=s2[0:n, :])
                            act.drain().then_inc(s2_ready, 1)
                            return
                        if kind == "N":
                            act.wait_ge(rstd_ready, lns + lno[("LN",) + x[1:]] + 1)
                            act.activation(carry_a[:, :], minus[:, :], ACT.Copy)
                            act.activation(xn[0:n, :], rows, ACT.Identity, scale=rstd[0:n, :], bias=nmr[0:n, :]).then_inc(xn_ready, 1)
                            return
                        bank = p_any[:, where[x] % 2, :]
                        act.wait_ge(piece_full, first + where[x] + 1)
                        if kind == "T":
                            last = act.activation(xn_t[:, p, MEM + t0:MEM + t0 + n], bank[:, 0:n], ACT.Identity,
                                                  scale=gb1[:, p, 0:1], bias=gb1[:, p, 1:2])
                        elif kind == "T2":
                            last = act.activation(xn2_t[:, p, 0:n], bank[:, 0:n], ACT.Identity, scale=gb2[:, p, 0:1], bias=gb2[:, p, 1:2])
                        elif kind == "K":
                            last = act.activation(k_t[:, p, MEM + t0:MEM + t0 + n], bank[:, 0:n], ACT.Copy)
                        elif kind == "V":
                            m = 128 if g < 2 else n
                            last = act.activation(v[0:m, g, 512 * p:512 * p + 512], bank[0:m, :], ACT.Copy)
                        elif kind == "Q":
                            nbk = -(-n // 8)
                            for hh in range(2):
                                h4 = 2 * (p % 2) + hh
                                last = act.activation(q_bd[64 * hh:64 * hh + 64, 0:nbk, p, 8 * h4:8 * h4 + 8],
                                                      bank[64 * hh:64 * hh + 64, 0:8 * nbk].rearrange("p (b i) -> p b i", i=8), ACT.Copy)
                        elif kind == "PV":
                            last = act.activation(wide_t[:, p, 0:n], bank[:, 0:n], ACT.Copy)
                        elif kind == "F1":
                            last = act.activation(wide_t[:, p, 0:n], bank[:, 0:n], ACT.Gelu, bias=b1[:, p:p + 1])
                        else:
                            act.wait_ge(x_added, xs + added[0])
                            last = act.activation(delta[0:n, :], bank[0:n, 0:D], ACT.Copy)
                        last.then_inc(piece_out, 1)

                    pipeline(mode, act, start, middle, item)

                run(act, program)

            @block.vector
            def _(dve):
                for q in (max_ready, threshold_ready):
                    dve.sem_inc(q, AHEAD)
                dve.wait_ge(s_c, 16 * 8)
                for l in range(2):
                    for j in range(2):
                        dve.tensor_tensor(mixes[:, l, j, :, :], mixb[:, l, j, :].unsqueeze(2).broadcast_to([128, H, ROWS]),
                                          eye8[:, :].unsqueeze(1).broadcast_to([128, H, ROWS]), ALU.mult)
                dve.drain().then_inc(s_mixes, 1)

                def program(mode, it):
                    if mode == "opening":
                        return
                    steps = range(PAIRS if mode == "body" else 1)
                    pairs = dve.snap(counts(it)[0]) if mode == "body" else counts(it)[0]

                    def start(p):
                        both = [(n, n % 2, n % (2 * RING), block_width(n)) for n in (2 * p, 2 * p + 1)]
                        dve.wait_ge(mask_ready, pairs + p + 1)
                        dve.tensor_tensor(carry_v[:, :], eye8[:, 0:1], eye8[:, 0:1], ALU.mult)
                        for n, u, r6, w in both:
                            dve.max(vals[:, r6, 0, :], mixed[:, r6, 0:w])
                        dve.drain().then_inc(max_ready, 1)
                        if 2 * p >= FULL_ROWS:
                            for r in range(1, 8):
                                for n, u, r6, w in both:
                                    dve.match_replace(work[:, u, 0:w], vals[:, r6, r - 1, :], (mixed[:, r6, 0:w] if r == 1 else work[:, u, 0:w]), -BIG)
                                dve.drain()
                                for n, u, r6, w in both:
                                    dve.max(vals[:, r6, r, :], work[:, u, 0:w])
                                if r < 7:
                                    dve.drain()
                        dve.drain().then_inc(threshold_ready, 1)

                    for p in steps:
                        start(p)

                run(dve, program)


def router_stage(nc, a, c, state_h, state_x, m):
    with ExitStack() as ctx:
        sb = lambda n, s, d=F32: ctx.enter_context(nc.sbuf_tensor(n, s, d))
        ps = lambda n, s, d=F32: ctx.enter_context(nc.psum_tensor(n, s, d))
        sem = lambda n: ctx.enter_context(nc.semaphore(n))
        ident = c["ident"]
        gate = sb("gate", [128, 2, EXPERTS])
        sg = sb("sg", [128, 2, HID])
        su = sb("su", [128, 2, HID])
        sd = sb("sd", [128, 4, D])
        tri = sb("tri", [128, 128])
        ones_c = sb("ones_c", [128, 1])
        ones_r = sb("ones_r", [1, 128])
        iota_e = sb("iota_e", [128, EXPERTS])
        iota_p = sb("iota_p", [128, 1])
        zero = sb("zero", [128, D])
        run = sb("run", [1, EXPERTS])
        xn = sb("xn_m", [128, D])
        x_t = sb("x_t", [128, 2, 128])
        sl = sb("sl", [128, 4, 128])
        hid = sb("hid", [128, 4, 128])
        top = sb("top", [128, 8])
        top_i = sb("top_i", [128, 8], U32)
        top_f = sb("top_f", [128, 1])
        e_s = sb("e_s", [128, 1])
        d_s = sb("d_s", [128, 1])
        score = sb("score", [128, 1])
        junk = sb("junk", [128, EXPERTS])
        stats = sb("stats_m", [128, 6])
        mom = sb("mom_m", [128, 2])
        rstd = sb("rstd_m", [128, 1])
        half = sb("half_m", [128, 1])
        eps = sb("eps_m", [128, 1])
        onehot = sb("onehot", [128, B * 3, EXPERTS])
        spread = sb("spread", [128, B * 3, EXPERTS])
        rank = sb("rank", [128, B * 3])
        slot_f = sb("slot_f", [128, B * 3])
        tiles_i = sb("tiles_i", [1, EXPERTS], I32)
        tiles_s = sb("tiles_s", [1, EXPERTS], I32)
        tiles_f = sb("tiles_f", [1, EXPERTS])
        ones_e = sb("ones_e", [1, EXPERTS])
        bounds = sb("bounds", [1, 2, EXPERTS])
        before = sb("before", [128, EXPERTS])
        e_col = sb("e_col", [128, 1])
        p_t = ps("pm_t", [128, 4, 128])[:, 0:2, :]
        p_g = ps("pm_g", [128, 4, 128])
        p_u = ps("pm_u", [128, 4, 128])
        p_y = ps("pm_y", [128, 512])[:, 0:D]
        p_l = ps("pm_l", [128, 512])[:, 0:EXPERTS]
        p_r = ps("pm_r", [128, 512])[:, 0:EXPERTS]
        p_l2 = p_t[:, 0, :]
        hot_now = sb("hot_now", [128, EXPERTS])
        logits = sb("logits", [128, EXPERTS])
        p_c = ps("pm_c", [128, 512])[:, 0:EXPERTS]
        p_b = ps("pm_b", [128, 8, 64])[:, 0, :].rearrange("p (j e) -> p j e", j=2)
        loaded, zeroed, ready = sem("m_loaded"), sem("m_zeroed"), sem("m_ready")
        mom_ready, rstd_ready, xn_ready = sem("m_mom"), sem("m_rstd"), sem("m_xn")
        t_full, t_out, l_full, g_full, s_out = sem("m_t_full"), sem("m_t_out"), sem("m_l_full"), sem("m_g_full"), sem("m_silu")
        hid_ready, y_full, top_ready, exp_ready = sem("m_hid"), sem("m_y_full"), sem("m_top"), sem("m_exp")
        hot_ready, r_full, tile_done = sem("m_hot"), sem("m_r_full"), sem("m_tile_done")
        bound_ready, bound_full, col_ready, row_full, slots_ready = (sem("m_bound"), sem("m_bound_full"), sem("m_col"),
                                                                     sem("m_row_full"), sem("m_slots"))
        scattered = sem("m_scattered")
        NL = 9
        ZC = 4

        def over_tiles(engine, first, tile, following):
            def entry(b, last):
                for g in range(3):
                    after = (b, g + 1) if g < 2 else (b + 1, 0)
                    tile(b, g, (lambda: None) if last and g == 2 else (lambda: following(*after)))

            first(0, 0)
            with engine.Fori(0, B - 1) as b:
                entry(b, False)
            entry(B - 1, True)

        with nc.Block() as block:
            @block.sync
            def _(sp):
                for dst, src in ((gate[:, :, :], a["gate_w"].rearrange("(c p) n -> p c n", p=128)),
                                 (sg[:, :, :], a["sg"].rearrange("(c p) n -> p c n", p=128)),
                                 (su[:, :, :], a["su"].rearrange("(c p) n -> p c n", p=128)),
                                 (sd[:, :, :], a["sd"].rearrange("(c p) n -> p c n", p=128)),
                                 (tri[:, :], a["tri"]), (iota_e[:, :], a["iota_e"]), (iota_p[:, :], a["iota_p"]),
                                 (ones_r[:, :], a["ones"][:, 0:128]), (ones_c[:, :], a["ones_c"])):
                    sp.dma_start(dst, src).then_inc(loaded, 16)
                sp.wait_ge(ready, 1)
                for k in range(ZC):
                    n = SLOT_TILES // ZC
                    sp.dma_start(m["xs"][128 * n * k:128 * n * (k + 1), :].rearrange("(t p) n -> p t n", p=128),
                                 zero[:, :].unsqueeze(1).broadcast_to([128, n, D])).then_inc(zeroed, 16)
                sp.wait_ge(zeroed, 16 * ZC)

            @block.gpsimd
            def _(pool):
                pool.memset(half[:, :], -0.5)
                pool.memset(eps[:, :], EPS)
                pool.memset(zero[:, :], 0.0)
                pool.memset(run[:, :], 0.0)
                pool.memset(ones_e[:, :], 1.0)
                pool.memset(onehot[:, :, :], 0.0)
                pool.memset(rank[:, :], 0.0)
                pool.drain().then_inc(ready, 1)
                with pool.Fori(0, B) as b:
                    t0 = pool.snap(b * 3)
                    for g in range(3):
                        n = TILE_N[g]
                        pool.wait_ge(mom_ready, t0 + g + 1)
                        pool.tensor_tensor(rstd[0:n, :], mom[0:n, 1:2], eps[0:n, :], ALU.add)
                        pool.drain()
                        pool.tensor_tensor(rstd[0:n, :], rstd[0:n, :], half[0:n, :], ALU.pow).then_inc(rstd_ready, 1)
                pool.wait_ge(slots_ready, 1)
                pool.wait_ge(zeroed, 16 * ZC)
                for b in range(B):
                    for g in range(3):
                        n, t = TILE_N[g], 3 * b + g
                        pool.indirect_dma_start(m["xs"], bass.IndirectOffsetOnAxis(ap=m["slot"][0:n, t:t + 1], axis=0),
                                                state_x[0:n, b, g, :], None).then_inc(scattered, 16)
                pool.wait_ge(scattered, 16 * 3 * B)

            @block.tensor
            def _(pe):
                pe.wait_ge(loaded, 16 * NL)
                pe.wait_ge(ready, 1)

                def transpose(b, g):
                    n, t = TILE_N[g], b * 3 + g
                    pe.wait_ge(xn_ready, t + 1)
                    for j in range(2):
                        last = pe.transpose(p_t[:, j, 0:n], xn[0:n, 128 * j:128 * j + 128], ident[0:n, 0:n])
                    last.then_inc(t_full, 1)

                def tile(b, g, ahead):
                    n, t = TILE_N[g], b * 3 + g
                    pe.wait_ge(t_out, t + 1)
                    for j in range(2):
                        last = pe.matmul(p_l[0:n, :], x_t[:, j, 0:n], gate[:, j, :], start=(j == 0), stop=(j == 1))
                    last.then_inc(l_full, 1)
                    for p, w in ((p_g, sg), (p_u, su)):
                        for q in range(4):
                            for j in range(2):
                                last = pe.matmul(p[:, q, 0:n], w[:, j, 128 * q:128 * q + 128], x_t[:, j, 0:n],
                                                 start=(j == 0 and q == 0), stop=(j == 1), skip_group_check=True)
                    last.then_inc(g_full, 1)
                    pe.wait_ge(hot_ready, t + 1)
                    hot = hot_now[0:n, :]
                    pe.matmul(p_r[0:n, :], tri[0:n, 0:n], hot, start=True, stop=False)
                    pe.matmul(p_r[0:n, :], ones_r[0:1, 0:n], run[0:1, :], start=False, stop=True)
                    pe.matmul(p_c[0:1, :], ones_c[0:n, 0:1], hot, start=True, stop=True).then_inc(r_full, 1)
                    ahead()
                    pe.wait_ge(hid_ready, t + 1)
                    for q in range(4):
                        last = pe.matmul(p_y[0:n, :], hid[:, q, 0:n], sd[:, q, :], start=(q == 0), stop=(q == 3))
                    last.then_inc(y_full, 1)

                over_tiles(pe, transpose, tile, transpose)
                pe.wait_ge(bound_ready, 1)
                pe.matmul(p_b[:, :, :], ones_r[0:1, :], bounds[0:1, :, :], start=True, stop=True).then_inc(bound_full, 1)
                pe.wait_ge(col_ready, 1)
                pe.matmul(p_l2[0:1, 0:SLOT_TILES], e_col[0:SLOT_TILES, :],
                          ident[0:SLOT_TILES, 0:SLOT_TILES], start=True, stop=True).then_inc(row_full, 1)

            @block.scalar
            def _(act):
                def turned(b, g):
                    n, t = TILE_N[g], b * 3 + g
                    act.wait_ge(t_full, t + 1)
                    act.activation(x_t[:, :, 0:n], p_t[:, :, 0:n], ACT.Copy).then_inc(t_out, 1)

                def tile(b, g, ahead):
                    n, t = TILE_N[g], b * 3 + g
                    act.wait_ge(top_ready, t + 1)
                    act.activation(e_s[0:n, :], top[0:n, 0:1], ACT.Exp, scale=-1.0).then_inc(exp_ready, 1)
                    act.wait_ge(g_full, t + 1)
                    act.activation(sl[:, :, 0:n], p_g[:, :, 0:n], ACT.Silu).then_inc(s_out, 1)
                    ahead()

                over_tiles(act, turned, tile, turned)

            @block.vector
            def _(dve):
                dve.wait_ge(loaded, 16 * NL)
                dve.wait_ge(ready, 1)

                def normalise(b, g):
                    n, t = TILE_N[g], b * 3 + g
                    h, x = state_h[0:n, b, g, :], state_x[0:n, b, g, :]
                    dve.tensor_tensor(h, h, x, ALU.add)
                    dve.drain()
                    layer_norm_stats(dve, stats[0:n, :], mom[0:n, :], h).then_inc(mom_ready, 1)
                    dve.wait_ge(rstd_ready, t + 1)
                    dve.tensor_scalar(xn[0:n, :], h, mom[0:n, 0:1], rstd[0:n, :], ALU.subtract, ALU.mult).then_inc(xn_ready, 1)

                def tile(b, g, ahead):
                    n, t = TILE_N[g], b * 3 + g
                    h, x = state_h[0:n, b, g, :], state_x[0:n, b, g, :]
                    dve.wait_ge(l_full, t + 1)
                    dve.tensor_copy(logits[0:n, :], p_l[0:n, :])
                    dve.drain()
                    dve.max(top[0:n, :], logits[0:n, :])
                    dve.drain()
                    dve.max_index(top_i[0:n, :], top[0:n, :], logits[0:n, :]).then_inc(top_ready, 1)
                    dve.drain()
                    dve.tensor_copy(top_f[0:n, :], top_i[0:n, 0:1])
                    dve.drain()
                    dve.tensor_scalar(hot_now[0:n, :], iota_e[0:n, :], top_f[0:n, :], None, ALU.is_equal).then_inc(hot_ready, 1)
                    dve.drain()
                    dve.tensor_copy(onehot[0:n, bass.ds(t, 1), :], hot_now[0:n, :].unsqueeze(1))
                    dve.wait_ge(exp_ready, t + 1)
                    dve.tensor_scalar(d_s[0:n, :], e_s[0:n, :], 1.0, None, ALU.add)
                    dve.drain()
                    dve.reciprocal(score[0:n, :], d_s[0:n, :])
                    dve.drain()
                    dve.tensor_scalar(x, xn[0:n, :], score[0:n, :], None, ALU.mult)
                    ahead()
                    dve.wait_ge(s_out, t + 1)
                    dve.tensor_tensor(hid[:, :, 0:n], sl[:, :, 0:n], p_u[:, :, 0:n], ALU.mult).then_inc(hid_ready, 1)
                    dve.wait_ge(r_full, t + 1)
                    dve.tensor_tensor(junk[0:n, :], hot_now[0:n, :], p_r[0:n, :], ALU.mult)
                    dve.tensor_tensor(run[:, :], run[:, :], p_c[0:1, :], ALU.add)
                    dve.drain()
                    dve.tensor_reduce(rank[0:n, bass.ds(t, 1)], junk[0:n, :], AX.X, ALU.add)
                    dve.wait_ge(y_full, t + 1)
                    dve.tensor_tensor(h, h, p_y[0:n, :], ALU.add)
                    dve.drain()

                over_tiles(dve, normalise, tile, normalise)
                dve.tensor_scalar(tiles_i[:, :], run[:, :], 127.0, None, ALU.add)
                dve.drain()
                dve.tensor_scalar(tiles_s[:, :], tiles_i[:, :], 7, None, ALU.arith_shift_right)
                dve.drain()
                dve.tensor_copy(tiles_f[:, :], tiles_s[:, :])
                dve.drain()
                dve.tensor_tensor_scan(bounds[:, 0, :], ones_e[:, :], tiles_f[:, :], 0.0, ALU.mult, ALU.add)
                dve.drain()
                dve.tensor_tensor(junk[0:1, :], bounds[:, 0, :], tiles_f[:, :], ALU.subtract)
                dve.drain()
                dve.tensor_scalar(bounds[:, 1, :], junk[0:1, :], 128.0, None, ALU.mult).then_inc(bound_ready, 1)
                dve.wait_ge(bound_full, 1)
                dve.tensor_tensor(spread[:, :, :], onehot[:, :, :], p_b[:, 1, :].unsqueeze(1).broadcast_to([128, 3 * B, EXPERTS]), ALU.mult)
                dve.tensor_scalar(before[:, :], p_b[:, 0, :], iota_p[:, 0:1], None, ALU.is_le)
                dve.drain()
                dve.tensor_reduce(slot_f[:, :], spread[:, :, :], AX.X, ALU.add)
                dve.tensor_reduce(e_col[:, :], before[:, :], AX.X, ALU.add)
                dve.drain()
                dve.tensor_scalar(e_col[:, :], e_col[:, :], EXPERTS - 1.0, None, ALU.min).then_inc(col_ready, 1)
                dve.tensor_tensor(m["slot"][:, :], slot_f[:, :], rank[:, :], ALU.add).then_inc(slots_ready, 1)
                dve.wait_ge(row_full, 1)
                dve.tensor_copy(m["experts"][:, :], p_l2[0:1, 0:SLOT_TILES])


def experts_stage(nc, a, c, m):
    RING = 4
    LOOPS = SLOT_TILES // RING - 1
    assert SLOT_TILES % RING == 0
    with ExitStack() as ctx:
        sb = lambda n, s, d=F32: ctx.enter_context(nc.sbuf_tensor(n, s, d))
        ps = lambda n, s, d=F32: ctx.enter_context(nc.psum_tensor(n, s, d))
        sem = lambda n: ctx.enter_context(nc.semaphore(n))
        ident = c["ident"]
        wg = sb("wg", [128, RING, 2, HID])
        wu = sb("wu", [128, RING, 2, HID])
        wd = sb("wd", [128, RING, 4, D])
        xs = sb("xs_sb", [128, RING, D])
        x_t = sb("xs_t", [128, 2, 2, 128])
        sl = sb("sl_e", [128, 2, 4, 128])
        hid = sb("hid_e", [128, 2, 4, 128])
        y = sb("y_e", [128, 2, D])
        p_t = ps("pe_t", [128, 1, 4, 128])
        p_g = ps("pe_g", [128, 2, 4, 128])
        p_u = ps("pe_u", [128, 2, 4, 128])
        p_y = ps("pe_y", [128, 2, 512])
        in_x, in_w = [sem(f"e_in_x{u}") for u in range(RING)], [sem(f"e_in_w{u}") for u in range(RING)]
        t_full, t_out, g_full, s_out, hid_ready, y_full, y_out = [sem("e_" + k) for k in (
            "t_full", "t_out", "g_full", "silu", "hid", "y_full", "y_out")]
        stored = [sem("e_stored0"), sem("e_stored1")]

        def number(i, k):
            return i * RING + k

        def round_of(i, k):
            return i + k // RING

        with nc.Block() as block:
            @block.sync
            def _(sp):
                def load(i, k):
                    t, u = number(i, k), k % RING
                    e = sp.value_load(m["experts"][0:1, bass.ds(t, 1)], min_val=0, max_val=EXPERTS - 1)
                    sp.dma_start(xs[:, u, :], m["xs"].rearrange("(t p) n -> t p n", p=128)[t]).then_inc(in_x[u], 16)
                    sp.dma_start(wg[:, u, :, :], a["rg"][e].rearrange("(c p) n -> p c n", p=128)).then_inc(in_w[u], 16)
                    sp.dma_start(wu[:, u, :, :], a["ru"][e].rearrange("(c p) n -> p c n", p=128)).then_inc(in_w[u], 16)
                    sp.dma_start(wd[:, u, :, :], a["rd"][e].rearrange("(c p) n -> p c n", p=128)).then_inc(in_w[u], 16)

                def store(i, k):
                    sp.wait_ge(y_out, number(i, k) + 3)
                    sp.dma_start(m["ys"].rearrange("(t p) n -> t p n", p=128)[number(i, k)], y[:, k % 2, :]).then_inc(stored[k % 2], 16)

                for k in range(RING):
                    load(0, k)
                with sp.Fori(0, LOOPS) as i:
                    for k in range(RING):
                        sp.wait_ge(y_full, number(i, k) + 1)
                        load(i, k + RING)
                        store(i, k)
                for k in range(RING):
                    store(LOOPS, k)
                for u in range(2):
                    sp.wait_ge(stored[u], 16 * (SLOT_TILES // 2) + 16)

            @block.tensor
            def _(pe):
                def transpose(i, k):
                    u = k % RING
                    pe.wait_ge(in_x[u], round_of(i, k) * 16 + 16)
                    for j in range(2):
                        last = pe.transpose(p_t[:, 0, j, :], xs[:, u, 128 * j:128 * j + 128], ident[:, :])
                    last.then_inc(t_full, 1)

                def gate_up(i, k):
                    u = k % RING
                    pe.wait_ge(in_w[u], round_of(i, k) * 48 + 48)
                    pe.wait_ge(t_out, number(i, k) + 1)
                    for p, w in ((p_g, wg), (p_u, wu)):
                        for q in range(4):
                            for j in range(2):
                                last = pe.matmul(p[:, k % 2, q, :], w[:, u, j, 128 * q:128 * q + 128], x_t[:, k % 2, j, :],
                                                 start=(j == 0 and q == 0), stop=(j == 1), skip_group_check=True)
                    last.then_inc(g_full, 1)

                def down(i, k):
                    u = k % RING
                    pe.wait_ge(hid_ready, number(i, k) + 1)
                    pe.wait_ge(y_out, number(i, k) + 1)
                    for q in range(4):
                        last = pe.matmul(p_y[:, k % 2, 0:D], hid[:, k % 2, q, :], wd[:, u, q, :], start=(q == 0), stop=(q == 3))
                    last.then_inc(y_full, 1)

                def step(i, k):
                    gate_up(i, k)
                    transpose(i, k + 1)
                    down(i, k - 1)

                transpose(0, 0)
                gate_up(0, 0)
                transpose(0, 1)
                with pe.Fori(0, LOOPS) as i:
                    for k in range(1, RING + 1):
                        step(i, k)
                for k in range(1, RING - 1):
                    step(LOOPS, k)
                gate_up(LOOPS, RING - 1)
                down(LOOPS, RING - 2)
                down(LOOPS, RING - 1)

            @block.scalar
            def _(act):
                def turned(i, k):
                    act.wait_ge(t_full, number(i, k) + 1)
                    act.activation(x_t[:, k % 2, :, :], p_t[:, 0, 0:2, :], ACT.Copy).then_inc(t_out, 1)

                def silu(i, k):
                    act.wait_ge(g_full, number(i, k) + 1)
                    act.activation(sl[:, k % 2, :, :], p_g[:, k % 2, :, :], ACT.Silu).then_inc(s_out, 1)

                turned(0, 0)
                with act.Fori(0, LOOPS) as i:
                    for k in range(RING):
                        silu(i, k)
                        turned(i, k + 1)
                for k in range(RING - 1):
                    silu(LOOPS, k)
                    turned(LOOPS, k + 1)
                silu(LOOPS, RING - 1)

            @block.vector
            def _(dve):
                dve.sem_inc(y_out, 2)
                for u in range(2):
                    dve.sem_inc(stored[u], 16)

                def gated(i, k):
                    dve.wait_ge(s_out, number(i, k) + 1)
                    dve.tensor_tensor(hid[:, k % 2, :, :], sl[:, k % 2, :, :], p_u[:, k % 2, :, :], ALU.mult).then_inc(hid_ready, 1)

                def out_of_bank(i, k):
                    dve.wait_ge(y_full, number(i, k) + 1)
                    dve.wait_ge(stored[k % 2], i * (8 * RING) + 16 * (k // 2) + 16)
                    dve.tensor_copy(y[:, k % 2, :], p_y[:, k % 2, 0:D]).then_inc(y_out, 1)

                gated(0, 0)
                with dve.Fori(0, LOOPS) as i:
                    for k in range(1, RING + 1):
                        gated(i, k)
                        out_of_bank(i, k - 1)
                for k in range(1, RING):
                    gated(LOOPS, k)
                    out_of_bank(LOOPS, k - 1)
                out_of_bank(LOOPS, RING - 1)


def combine_stage(nc, out, state_h, m):
    RING = 6
    with ExitStack() as ctx:
        sem = lambda n: ctx.enter_context(nc.semaphore(n))
        got = ctx.enter_context(nc.sbuf_tensor("got", [128, RING, D], F32))
        fetched, added, stored = [sem(f"c_fetched{i}") for i in range(RING)], sem("c_added"), sem("c_stored")
        tiles = [(b, g) for b in range(B) for g in range(3)]
        with nc.Block() as block:
            @block.gpsimd
            def _(pool):
                for t, (b, g) in enumerate(tiles):
                    n = TILE_N[g]
                    if t >= RING:
                        pool.wait_ge(added, t - RING + 1)
                    pool.indirect_dma_start(got[0:n, t % RING, :], None, m["ys"],
                                            bass.IndirectOffsetOnAxis(ap=m["slot"][0:n, t:t + 1], axis=0)).then_inc(fetched[t % RING], 16)

            @block.vector
            def _(dve):
                for t, (b, g) in enumerate(tiles):
                    n = TILE_N[g]
                    dve.wait_ge(fetched[t % RING], 16 * (t // RING + 1))
                    dve.tensor_tensor(state_h[0:n, b, g, :], state_h[0:n, b, g, :], got[0:n, t % RING, :], ALU.add).then_inc(added, 1)

            @block.sync
            def _(sp):
                for t, (b, g) in enumerate(tiles):
                    sp.wait_ge(added, t + 1)
                    sp.dma_start(out[b, TILE0[g]:TILE0[g] + TILE_N[g], :], state_h[0:TILE_N[g], b, g, :]).then_inc(stored, 16)
                sp.wait_ge(stored, 16 * len(tiles))


def move_rows(nc, state_h, h_rows, back):
    with nc.semaphore("moved_in" if back else "moved_out") as moved, nc.Block() as block:
        @block.sync
        def _(sp):
            for g, n in enumerate(TILE_N):
                pair = (state_h[0:n, :, g, :], h_rows[g, 0:n])
                sp.dma_start(*(pair if back else pair[::-1])).then_inc(moved, 16)
            sp.wait_ge(moved, 48)


def build(nc, a, out):
    with ExitStack() as ctx:
        sb = lambda n, s, d=F32: ctx.enter_context(nc.sbuf_tensor(n, s, d))
        state_x = sb("state_x", [128, B + 1, 3, D])
        c = {"ident": sb("ident", [128, 128]), "mom_last": sb("mom_last", [128, B, 2])}
        m = {"slot": sb("slot", [128, 3 * B], U32), "experts": sb("experts", [1, SLOT_TILES], I32),
             "xs": nc.dram_tensor("xs_slots", (SLOT_TILES * 128, D), F32, kind="Internal").ap(),
             "ys": nc.dram_tensor("ys_slots", (SLOT_TILES * 128, D), F32, kind="Internal").ap()}
        h_rows = nc.dram_tensor("h_rows", (3, 128, B, D), F32, kind="Internal").ap()
        with nc.sbuf_tensor("state_h1", [128, B, 3, D], F32) as state_h:
            tokens_stage(nc, a, c, state_h, state_x[:, 1:B + 1, :, :])
            move_rows(nc, state_h, h_rows, False)
        attention_stage(nc, a, c, state_x)
        state_h = sb("state_h2", [128, B, 3, D])
        move_rows(nc, state_h, h_rows, True)
        router_stage(nc, a, c, state_h, state_x[:, 1:B + 1, :, :], m)
        experts_stage(nc, a, c, m)
        combine_stage(nc, out, state_h, m)


def kernel(**x):
    import concourse.bacc as _bacc
    from concourse.bass_utils import run_bass_kernel_spmd as _run

    t = {k: np.asarray(v) for k, v in x.items()}
    cat = np.concatenate
    tok = lambda k: t["L0_tok_" + k]
    att = lambda k: t["L0_attn_" + k]
    eye = np.eye(128, dtype=np.float32)
    row = lambda v: v.reshape(1, -1)
    feat = np.stack([att("ln1_g"), att("ln1_b"), att("ln2_g"), att("ln2_b")], 1).reshape(2, 4, 2, 128)
    i8 = np.arange(128) % ROWS
    arrays = {
        "x": t["x"], "ids": np.stack([t["x_txt"], t["itok_BS_0_4096"]], 0).transpose(2, 1, 0),
        "fractions": np.stack([t["fside_BS_delta_" + k] for k in ("x1", "x2", "y1", "y2")], 0).transpose(2, 0, 1),
        "Wq": cat([tok("Wq_w").T, row(tok("Wq_b"))]),
        "Wkv": cat([cat([tok("Wk_w").T, row(tok("Wk_b"))]), cat([tok("Wv_w").T, row(tok("Wv_b"))])], 1),
        "id_b": cat([np.broadcast_to(eye[:64, None, :64], (64, HD, 64)), tok("out_b").reshape(1, HD, 64)]),
        "w_bias_t": tok("w_bias").T, "mask_t": np.ascontiguousarray(tok("local_mask").T).view(np.int32),
        "out_w": tok("out_w"), "ln_g": tok("ln_g"), "ln_b": tok("ln_b"), "embeds": t["L0_txt_loc_embeds"],
        "wq": att("wq"), "wk": att("wk"), "wv": att("wv"), "wo": att("wo"), "w1": att("w1"), "w2": att("w2"),
        "mem_k": att("mem_k").reshape(2, 8, 2, MEM, DH).transpose(2, 4, 0, 1, 3).reshape(128, 2, 8, MEM),
        "mem_v": att("mem_v").transpose(0, 2, 1, 3).reshape(2, MEM, H * DH),
        "pre": att("pre_proj"), "post": att("post_proj"),
        "bo_b2": np.stack([att("bo"), att("b2")], 1).reshape(2, 1, 2, D), "b1": att("b1").reshape(2, 8, 128).transpose(0, 2, 1),
        "gb": feat.transpose(0, 3, 2, 1),
        "gate_w": t["L0_ffn_gate_w"], "sg": t["L0_ffn_shared_gate_w"], "su": t["L0_ffn_shared_up_w"], "sd": t["L0_ffn_shared_down_w"],
        "rg": t["L0_ffn_routed_gate_w"], "ru": t["L0_ffn_routed_up_w"], "rd": t["L0_ffn_routed_down_w"],
        "ident": eye, "ones": np.ones((1, L * HD), np.float32), "ones_c": np.ones((128, 1), np.float32),
        "eye8": eye[:ROWS, :ROWS][i8],
        "diag": np.where(np.arange(ROWS)[None, :] <= i8[:, None], np.float32(0), np.float32(-BIG / 2)),
        "tri": np.triu(np.ones((128, 128), np.float32), 1),
        "iota_e": np.broadcast_to(np.arange(EXPERTS, dtype=np.float32), (128, EXPERTS)),
        "iota_p": np.arange(128, dtype=np.float32).reshape(128, 1),
    }
    nc = _bacc.Bacc("TRN2", target_bir_lowering=False, num_devices=1)
    arrays = {k: np.ascontiguousarray(v) for k, v in arrays.items()}
    a = {k: nc.dram_tensor("in_" + k, v.shape, mybir.dt.from_np(v.dtype), kind="ExternalInput").ap() for k, v in arrays.items()}
    out = nc.dram_tensor("out_0", (B, SEQ, D), F32, kind="ExternalOutput").ap()
    build(nc, a, out)
    r = _run(nc, [{"in_" + k: v for k, v in arrays.items()}], core_ids=[0])
    return r.results[0]["out_0"]
```
